# Optimizing a Trainium2 kernel written in Bass

```python
import numpy as np
import jax
import jax.numpy as jnp

def _softmax(x, axis=-1):
    return jax.nn.softmax(x, axis=axis)

def _gelu(x):
    return jax.nn.gelu(x, approximate=True)

def _silu(x):
    return jax.nn.silu(x)

def _sigmoid(x):
    return jax.nn.sigmoid(x)

def _layernorm(x, axis=-1, eps=1e-05):
    m = jnp.mean(x, axis=axis, keepdims=True)
    v = jnp.var(x, axis=axis, keepdims=True)
    return (x - m) / jnp.sqrt(v + eps)

def _scatter_add(tgt, idx, src, axis=0):
    return tgt.at[idx].add(src)

def _segment_sum(src, seg, n):
    return jax.ops.segment_sum(src, seg, n)
kernel_name = 'mk_pixart_seq_d4_seqx_r4_c07a1e'

def setup_inputs(seed: int=0):
    np.random.seed(seed)
    _w = jnp.asarray

    def _rec_inputs():
        import jax
        import jax.numpy as jnp
        _rk = jax.random.key(seed)
        x = -0.0002928 + 1 * jax.random.normal(jax.random.fold_in(_rk, 1), (16, 256, 256), jnp.float32)
        _lenS = 256 - jax.random.randint(jax.random.fold_in(_rk, 7), (16,), 0, max(1, 256 // 4) + 1, jnp.int32)
        _lenS2 = 120 - jax.random.randint(jax.random.fold_in(_rk, 8), (16,), 0, max(1, 120 // 4) + 1, jnp.int32)
        cond_1024 = 0.0061147 + 1.02565 * jax.random.normal(jax.random.fold_in(_rk, 11), (16, 256), jnp.float32)
        _ctx_1024P = jax.random.normal(jax.random.fold_in(_rk, 12), (16, 16, 256), jnp.float32)
        _ctx_1024c = jax.random.dirichlet(jax.random.fold_in(_rk, 512), 0.3 * jnp.ones((16,), jnp.float32), (16, 120))
        _ctx_1024t = jnp.einsum('bsk,bkd->bsd', _ctx_1024c, _ctx_1024P)
        _ctx_1024t = _ctx_1024t * jax.lax.rsqrt(jnp.mean(jnp.square(_ctx_1024t)) + 1e-12) * 0.953939
        ctx_1024 = -0.00265004 + 0.998804 * (_ctx_1024t + 0.3 * jax.random.normal(jax.random.fold_in(_rk, 612), (16, 120, 256), jnp.float32))
        return (x, cond_1024, ctx_1024)
    x, cond_1024, ctx_1024 = _rec_inputs()

    def _L0_xcond_setup():
        import jax, jax.numpy as jnp
        import numpy as np
        D = 256
        H = 16
        HD = D // H
        MLP = 4 * D
        EPS = 1e-06
        SCALE = HD ** (-0.5)

        def _p(key, shape, s=0.02):
            return jax.random.normal(key, shape, dtype=jnp.float32) * s

        def _ln(x):
            mu = jnp.mean(x, axis=-1, keepdims=True)
            var = jnp.var(x, axis=-1, keepdims=True)
            return (x - mu) * jax.lax.rsqrt(var + EPS)

        def _heads(t):
            B, L, _ = t.shape
            return t.reshape(B, L, H, HD).transpose(0, 2, 1, 3)

        def _attend(q, k, v):
            attn = jnp.einsum('bhnd,bhsd->bhns', q, k) * SCALE
            attn = jax.nn.softmax(attn, axis=-1)
            o = jnp.einsum('bhns,bhsd->bhnd', attn, v)
            B, _, N, _ = q.shape
            return o.transpose(0, 2, 1, 3).reshape(B, N, D)
        key = jax.random.key(seed)
        ks = jax.random.split(key, 24)
        B, N, S = (4, 256, 77)
        return {'x': jax.random.normal(ks[0], (B, N, D), dtype=jnp.float32), 't_emb': jax.random.normal(ks[1], (B, D), dtype=jnp.float32), 'context': jax.random.normal(ks[2], (B, S, D), dtype=jnp.float32), 'adaln_w': _p(ks[3], (D, 6 * D)), 'adaln_b': _p(ks[4], (6 * D,)), 'qkv_w': _p(ks[5], (D, 3 * D)), 'qkv_b': _p(ks[6], (3 * D,)), 'sa_proj_w': _p(ks[7], (D, D)), 'sa_proj_b': _p(ks[8], (D,)), 'q_w': _p(ks[9], (D, D)), 'q_b': _p(ks[10], (D,)), 'kv_w': _p(ks[11], (D, 2 * D)), 'kv_b': _p(ks[12], (2 * D,)), 'ca_proj_w': _p(ks[13], (D, D)), 'ca_proj_b': _p(ks[14], (D,)), 'fc1_w': _p(ks[15], (D, MLP)), 'fc1_b': _p(ks[16], (MLP,)), 'fc2_w': _p(ks[17], (MLP, D)), 'fc2_b': _p(ks[18], (D,))}
    _L0_xcond_all = _L0_xcond_setup()
    _L0_xcond_in = {k: v for k, v in _L0_xcond_all.items() if k in ('adaln_w', 'adaln_b', 'qkv_w', 'qkv_b', 'sa_proj_w', 'sa_proj_b', 'q_w', 'q_b', 'kv_w', 'kv_b', 'ca_proj_w', 'ca_proj_b', 'fc1_w', 'fc1_b', 'fc2_w', 'fc2_b')}
    del _L0_xcond_all

    def _L1_xcond_setup():
        import jax, jax.numpy as jnp
        import numpy as np
        EPS = 1e-05

        def _ada_ln(x, c, W_ss, b_ss):
            mu = jnp.mean(x, axis=-1, keepdims=True)
            var = jnp.mean((x - mu) ** 2, axis=-1, keepdims=True)
            h = (x - mu) / jnp.sqrt(var + EPS)
            ss = jax.nn.silu(c) @ W_ss + b_ss
            scale, bias = jnp.split(ss, 2, axis=-1)
            return (1.0 + scale)[:, None, :] * h + bias[:, None, :]
        key = jax.random.key(seed)
        ks = jax.random.split(key, 12)
        B, Lq, Lkv, H = (8, 512, 128, 256)
        s = 0.02
        return {'x_q': jax.random.normal(ks[0], (B, Lq, H), jnp.float32), 'x_kv': jax.random.normal(ks[1], (B, Lkv, H), jnp.float32), 't_vec': jax.random.normal(ks[2], (B, H), jnp.float32), 'Wq': jax.random.normal(ks[3], (H, H), jnp.float32) * s, 'bq': jnp.zeros((H,), jnp.float32), 'Wkv': jax.random.normal(ks[4], (H, 2 * H), jnp.float32) * s, 'bkv': jnp.zeros((2 * H,), jnp.float32), 'Wp': jax.random.normal(ks[5], (H, H), jnp.float32) * s, 'bp': jnp.zeros((H,), jnp.float32), 'Wss_q': jax.random.normal(ks[6], (H, 2 * H), jnp.float32) * s, 'bss_q': jnp.zeros((2 * H,), jnp.float32), 'Wss_kv': jax.random.normal(ks[7], (H, 2 * H), jnp.float32) * s, 'bss_kv': jnp.zeros((2 * H,), jnp.float32)}
    _L1_xcond_all = _L1_xcond_setup()
    _L1_xcond_in = {k: v for k, v in _L1_xcond_all.items() if k in ('Wq', 'bq', 'Wkv', 'bkv', 'Wp', 'bp', 'Wss_q', 'bss_q', 'Wss_kv', 'bss_kv')}
    del _L1_xcond_all

    def _L2_xcond_setup():
        import jax, jax.numpy as jnp
        import numpy as np
        EPS = 1e-06
        H = 16

        def layer_norm(x, gamma=None, beta=None):
            x32 = x.astype(jnp.float32)
            mu = jnp.mean(x32, axis=-1, keepdims=True)
            var = jnp.var(x32, axis=-1, keepdims=True)
            y = (x32 - mu) * jax.lax.rsqrt(var + EPS)
            if gamma is not None:
                y = y * gamma + beta
            return y.astype(x.dtype)

        def mha(q, k, v):
            B, Nq, C = q.shape
            d = C // H
            qh = q.reshape(B, Nq, H, d)
            kh = k.reshape(B, k.shape[1], H, d)
            vh = v.reshape(B, v.shape[1], H, d)
            scores = jnp.einsum('bqhd,bkhd->bhqk', qh, kh) / jnp.sqrt(jnp.asarray(d, q.dtype))
            attn = jax.nn.softmax(scores, axis=-1)
            out = jnp.einsum('bhqk,bkhd->bqhd', attn, vh)
            return out.reshape(B, Nq, C)
        key = jax.random.key(seed)
        ks = jax.random.split(key, 24)
        B, N, C, M, Cc = (4, 512, 256, 256, 256)
        hid = 4 * C
        s = 0.02
        return {'x': jax.random.normal(ks[0], (B, N, C), jnp.float32), 'mod': jax.random.normal(ks[1], (B, C), jnp.float32), 'context': jax.random.normal(ks[2], (B, M, Cc), jnp.float32), 'ada_w': jax.random.normal(ks[3], (C, 6 * C), jnp.float32) * s, 'ada_b': jnp.zeros((6 * C,), jnp.float32), 'qkv_w': jax.random.normal(ks[4], (C, 3 * C), jnp.float32) * s, 'qkv_b': jnp.zeros((3 * C,), jnp.float32), 'self_o_w': jax.random.normal(ks[5], (C, C), jnp.float32) * s, 'self_o_b': jnp.zeros((C,), jnp.float32), 'norm2_g': jnp.ones((C,), jnp.float32), 'norm2_b': jnp.zeros((C,), jnp.float32), 'q_w': jax.random.normal(ks[6], (C, C), jnp.float32) * s, 'q_b': jnp.zeros((C,), jnp.float32), 'kv_w': jax.random.normal(ks[7], (Cc, 2 * C), jnp.float32) * s, 'kv_b': jnp.zeros((2 * C,), jnp.float32), 'cross_o_w': jax.random.normal(ks[8], (C, C), jnp.float32) * s, 'cross_o_b': jnp.zeros((C,), jnp.float32), 'mlp_w1': jax.random.normal(ks[9], (C, hid), jnp.float32) * s, 'mlp_b1': jnp.zeros((hid,), jnp.float32), 'mlp_w2': jax.random.normal(ks[10], (hid, C), jnp.float32) * s, 'mlp_b2': jnp.zeros((C,), jnp.float32)}
    _L2_xcond_all = _L2_xcond_setup()
    _L2_xcond_in = {k: v for k, v in _L2_xcond_all.items() if k in ('ada_w', 'ada_b', 'qkv_w', 'qkv_b', 'self_o_w', 'self_o_b', 'norm2_g', 'norm2_b', 'q_w', 'q_b', 'kv_w', 'kv_b', 'cross_o_w', 'cross_o_b', 'mlp_w1', 'mlp_b1', 'mlp_w2', 'mlp_b2')}
    del _L2_xcond_all

    def _L3_xcond_setup():
        import jax, jax.numpy as jnp
        import numpy as np
        LN_EPS = 1e-06

        def _ln(x):
            mu = jnp.mean(x, axis=-1, keepdims=True)
            var = jnp.var(x, axis=-1, keepdims=True)
            return (x - mu) * jax.lax.rsqrt(var + LN_EPS)
        key = jax.random.key(seed)
        H, NH = (256, 16)
        B, N, S = (4, 256, 77)
        MLP = int(H * 4.0)
        ks = jax.random.split(key, 20)
        s = 1.0 / np.sqrt(H)
        return {'x': jax.random.normal(ks[0], (B, N, H), jnp.float32), 'c': jax.random.normal(ks[1], (B, H), jnp.float32), 'context': jax.random.normal(ks[2], (B, S, H), jnp.float32), 'W_mod': jax.random.normal(ks[3], (H, 6 * H), jnp.float32) * s, 'b_mod': jnp.zeros((6 * H,), jnp.float32), 'W_qkv': jax.random.normal(ks[4], (H, 3 * H), jnp.float32) * s, 'b_qkv': jnp.zeros((3 * H,), jnp.float32), 'W_proj': jax.random.normal(ks[5], (H, H), jnp.float32) * s, 'b_proj': jnp.zeros((H,), jnp.float32), 'W_qc': jax.random.normal(ks[6], (H, H), jnp.float32) * s, 'b_qc': jnp.zeros((H,), jnp.float32), 'W_kvc': jax.random.normal(ks[7], (H, 2 * H), jnp.float32) * s, 'b_kvc': jnp.zeros((2 * H,), jnp.float32), 'W_cproj': jax.random.normal(ks[8], (H, H), jnp.float32) * s, 'b_cproj': jnp.zeros((H,), jnp.float32), 'W_mlp1': jax.random.normal(ks[9], (H, MLP), jnp.float32) * s, 'b_mlp1': jnp.zeros((MLP,), jnp.float32), 'W_mlp2': jax.random.normal(ks[10], (MLP, H), jnp.float32) * (1.0 / np.sqrt(MLP)), 'b_mlp2': jnp.zeros((H,), jnp.float32)}
    _L3_xcond_all = _L3_xcond_setup()
    _L3_xcond_in = {k: v for k, v in _L3_xcond_all.items() if k in ('W_mod', 'b_mod', 'W_qkv', 'b_qkv', 'W_proj', 'b_proj', 'W_qc', 'b_qc', 'W_kvc', 'b_kvc', 'W_cproj', 'b_cproj', 'W_mlp1', 'b_mlp1', 'W_mlp2', 'b_mlp2')}
    del _L3_xcond_all
    return {'x': x, 'cond_1024': cond_1024, 'ctx_1024': ctx_1024, 'L0_xcond_adaln_w': _L0_xcond_in['adaln_w'], 'L0_xcond_adaln_b': _L0_xcond_in['adaln_b'], 'L0_xcond_qkv_w': _L0_xcond_in['qkv_w'], 'L0_xcond_qkv_b': _L0_xcond_in['qkv_b'], 'L0_xcond_sa_proj_w': _L0_xcond_in['sa_proj_w'], 'L0_xcond_sa_proj_b': _L0_xcond_in['sa_proj_b'], 'L0_xcond_q_w': _L0_xcond_in['q_w'], 'L0_xcond_q_b': _L0_xcond_in['q_b'], 'L0_xcond_kv_w': _L0_xcond_in['kv_w'], 'L0_xcond_kv_b': _L0_xcond_in['kv_b'], 'L0_xcond_ca_proj_w': _L0_xcond_in['ca_proj_w'], 'L0_xcond_ca_proj_b': _L0_xcond_in['ca_proj_b'], 'L0_xcond_fc1_w': _L0_xcond_in['fc1_w'], 'L0_xcond_fc1_b': _L0_xcond_in['fc1_b'], 'L0_xcond_fc2_w': _L0_xcond_in['fc2_w'], 'L0_xcond_fc2_b': _L0_xcond_in['fc2_b'], 'L1_xcond_Wq': _L1_xcond_in['Wq'], 'L1_xcond_bq': _L1_xcond_in['bq'], 'L1_xcond_Wkv': _L1_xcond_in['Wkv'], 'L1_xcond_bkv': _L1_xcond_in['bkv'], 'L1_xcond_Wp': _L1_xcond_in['Wp'], 'L1_xcond_bp': _L1_xcond_in['bp'], 'L1_xcond_Wss_q': _L1_xcond_in['Wss_q'], 'L1_xcond_bss_q': _L1_xcond_in['bss_q'], 'L1_xcond_Wss_kv': _L1_xcond_in['Wss_kv'], 'L1_xcond_bss_kv': _L1_xcond_in['bss_kv'], 'L2_xcond_ada_w': _L2_xcond_in['ada_w'], 'L2_xcond_ada_b': _L2_xcond_in['ada_b'], 'L2_xcond_qkv_w': _L2_xcond_in['qkv_w'], 'L2_xcond_qkv_b': _L2_xcond_in['qkv_b'], 'L2_xcond_self_o_w': _L2_xcond_in['self_o_w'], 'L2_xcond_self_o_b': _L2_xcond_in['self_o_b'], 'L2_xcond_norm2_g': _L2_xcond_in['norm2_g'], 'L2_xcond_norm2_b': _L2_xcond_in['norm2_b'], 'L2_xcond_q_w': _L2_xcond_in['q_w'], 'L2_xcond_q_b': _L2_xcond_in['q_b'], 'L2_xcond_kv_w': _L2_xcond_in['kv_w'], 'L2_xcond_kv_b': _L2_xcond_in['kv_b'], 'L2_xcond_cross_o_w': _L2_xcond_in['cross_o_w'], 'L2_xcond_cross_o_b': _L2_xcond_in['cross_o_b'], 'L2_xcond_mlp_w1': _L2_xcond_in['mlp_w1'], 'L2_xcond_mlp_b1': _L2_xcond_in['mlp_b1'], 'L2_xcond_mlp_w2': _L2_xcond_in['mlp_w2'], 'L2_xcond_mlp_b2': _L2_xcond_in['mlp_b2'], 'L3_xcond_W_mod': _L3_xcond_in['W_mod'], 'L3_xcond_b_mod': _L3_xcond_in['b_mod'], 'L3_xcond_W_qkv': _L3_xcond_in['W_qkv'], 'L3_xcond_b_qkv': _L3_xcond_in['b_qkv'], 'L3_xcond_W_proj': _L3_xcond_in['W_proj'], 'L3_xcond_b_proj': _L3_xcond_in['b_proj'], 'L3_xcond_W_qc': _L3_xcond_in['W_qc'], 'L3_xcond_b_qc': _L3_xcond_in['b_qc'], 'L3_xcond_W_kvc': _L3_xcond_in['W_kvc'], 'L3_xcond_b_kvc': _L3_xcond_in['b_kvc'], 'L3_xcond_W_cproj': _L3_xcond_in['W_cproj'], 'L3_xcond_b_cproj': _L3_xcond_in['b_cproj'], 'L3_xcond_W_mlp1': _L3_xcond_in['W_mlp1'], 'L3_xcond_b_mlp1': _L3_xcond_in['b_mlp1'], 'L3_xcond_W_mlp2': _L3_xcond_in['W_mlp2'], 'L3_xcond_b_mlp2': _L3_xcond_in['b_mlp2']}

def reference(x, cond_1024, ctx_1024, L0_xcond_adaln_w, L0_xcond_adaln_b, L0_xcond_qkv_w, L0_xcond_qkv_b, L0_xcond_sa_proj_w, L0_xcond_sa_proj_b, L0_xcond_q_w, L0_xcond_q_b, L0_xcond_kv_w, L0_xcond_kv_b, L0_xcond_ca_proj_w, L0_xcond_ca_proj_b, L0_xcond_fc1_w, L0_xcond_fc1_b, L0_xcond_fc2_w, L0_xcond_fc2_b, L1_xcond_Wq, L1_xcond_bq, L1_xcond_Wkv, L1_xcond_bkv, L1_xcond_Wp, L1_xcond_bp, L1_xcond_Wss_q, L1_xcond_bss_q, L1_xcond_Wss_kv, L1_xcond_bss_kv, L2_xcond_ada_w, L2_xcond_ada_b, L2_xcond_qkv_w, L2_xcond_qkv_b, L2_xcond_self_o_w, L2_xcond_self_o_b, L2_xcond_norm2_g, L2_xcond_norm2_b, L2_xcond_q_w, L2_xcond_q_b, L2_xcond_kv_w, L2_xcond_kv_b, L2_xcond_cross_o_w, L2_xcond_cross_o_b, L2_xcond_mlp_w1, L2_xcond_mlp_b1, L2_xcond_mlp_w2, L2_xcond_mlp_b2, L3_xcond_W_mod, L3_xcond_b_mod, L3_xcond_W_qkv, L3_xcond_b_qkv, L3_xcond_W_proj, L3_xcond_b_proj, L3_xcond_W_qc, L3_xcond_b_qc, L3_xcond_W_kvc, L3_xcond_b_kvc, L3_xcond_W_cproj, L3_xcond_b_cproj, L3_xcond_W_mlp1, L3_xcond_b_mlp1, L3_xcond_W_mlp2, L3_xcond_b_mlp2):
    import jax
    import jax.numpy as jnp

    def _L0_xcond_ref(x, t_emb, context, adaln_w, adaln_b, qkv_w, qkv_b, sa_proj_w, sa_proj_b, q_w, q_b, kv_w, kv_b, ca_proj_w, ca_proj_b, fc1_w, fc1_b, fc2_w, fc2_b):
        import jax, jax.numpy as jnp
        import numpy as np
        D = 256
        H = 16
        HD = D // H
        MLP = 4 * D
        EPS = 1e-06
        SCALE = HD ** (-0.5)

        def _p(key, shape, s=0.02):
            return jax.random.normal(key, shape, dtype=jnp.float32) * s

        def _ln(x):
            mu = jnp.mean(x, axis=-1, keepdims=True)
            var = jnp.var(x, axis=-1, keepdims=True)
            return (x - mu) * jax.lax.rsqrt(var + EPS)

        def _heads(t):
            B, L, _ = t.shape
            return t.reshape(B, L, H, HD).transpose(0, 2, 1, 3)

        def _attend(q, k, v):
            attn = jnp.einsum('bhnd,bhsd->bhns', q, k) * SCALE
            attn = jax.nn.softmax(attn, axis=-1)
            o = jnp.einsum('bhns,bhsd->bhnd', attn, v)
            B, _, N, _ = q.shape
            return o.transpose(0, 2, 1, 3).reshape(B, N, D)
        B, N, _ = x.shape
        S = context.shape[1]
        mod = jax.nn.silu(t_emb) @ adaln_w + adaln_b
        sh_sa, sc_sa, g_sa, sh_ff, sc_ff, g_ff = jnp.split(mod[:, None, :], 6, axis=-1)
        xm = _ln(x) * (1.0 + sc_sa) + sh_sa
        qkv = (xm @ qkv_w + qkv_b).reshape(B, N, 3, H, HD)
        q = qkv[:, :, 0].transpose(0, 2, 1, 3)
        k = qkv[:, :, 1].transpose(0, 2, 1, 3)
        v = qkv[:, :, 2].transpose(0, 2, 1, 3)
        x_sa = _attend(q, k, v) @ sa_proj_w + sa_proj_b
        x = x + g_sa * x_sa
        xn = _ln(x)
        q = _heads(xn @ q_w + q_b)
        kv = (context @ kv_w + kv_b).reshape(B, S, 2, H, HD)
        k = kv[:, :, 0].transpose(0, 2, 1, 3)
        v = kv[:, :, 1].transpose(0, 2, 1, 3)
        x_ca = _attend(q, k, v) @ ca_proj_w + ca_proj_b
        x = x + x_ca
        xm = _ln(x) * (1.0 + sc_ff) + sh_ff
        h = jax.nn.gelu(xm @ fc1_w + fc1_b, approximate=True)
        x_ff = h @ fc2_w + fc2_b
        x = x + g_ff * x_ff
        return x

    def _L1_xcond_ref(x_q, x_kv, t_vec, Wq, bq, Wkv, bkv, Wp, bp, Wss_q, bss_q, Wss_kv, bss_kv):
        import jax, jax.numpy as jnp
        import numpy as np
        EPS = 1e-05

        def _ada_ln(x, c, W_ss, b_ss):
            mu = jnp.mean(x, axis=-1, keepdims=True)
            var = jnp.mean((x - mu) ** 2, axis=-1, keepdims=True)
            h = (x - mu) / jnp.sqrt(var + EPS)
            ss = jax.nn.silu(c) @ W_ss + b_ss
            scale, bias = jnp.split(ss, 2, axis=-1)
            return (1.0 + scale)[:, None, :] * h + bias[:, None, :]
        B, Lq, H = x_q.shape
        Lkv = x_kv.shape[1]
        nh = 16
        dh = H // nh
        xq = _ada_ln(x_q, t_vec, Wss_q, bss_q)
        xkv = _ada_ln(x_kv, t_vec, Wss_kv, bss_kv)
        q = (xq @ Wq + bq).reshape(B, Lq, nh, dh)
        kv = (xkv @ Wkv + bkv).reshape(B, Lkv, 2, nh, dh)
        k = kv[:, :, 0]
        v = kv[:, :, 1]
        scores = jnp.einsum('bqhd,bkhd->bhqk', q, k) / jnp.sqrt(jnp.float32(dh))
        attn = jax.nn.softmax(scores, axis=-1)
        out = jnp.einsum('bhqk,bkhd->bqhd', attn, v).reshape(B, Lq, H)
        return x_q + (out @ Wp + bp)

    def _L2_xcond_ref(x, mod, context, ada_w, ada_b, qkv_w, qkv_b, self_o_w, self_o_b, norm2_g, norm2_b, q_w, q_b, kv_w, kv_b, cross_o_w, cross_o_b, mlp_w1, mlp_b1, mlp_w2, mlp_b2):
        import jax, jax.numpy as jnp
        import numpy as np
        EPS = 1e-06
        H = 16

        def layer_norm(x, gamma=None, beta=None):
            x32 = x.astype(jnp.float32)
            mu = jnp.mean(x32, axis=-1, keepdims=True)
            var = jnp.var(x32, axis=-1, keepdims=True)
            y = (x32 - mu) * jax.lax.rsqrt(var + EPS)
            if gamma is not None:
                y = y * gamma + beta
            return y.astype(x.dtype)

        def mha(q, k, v):
            B, Nq, C = q.shape
            d = C // H
            qh = q.reshape(B, Nq, H, d)
            kh = k.reshape(B, k.shape[1], H, d)
            vh = v.reshape(B, v.shape[1], H, d)
            scores = jnp.einsum('bqhd,bkhd->bhqk', qh, kh) / jnp.sqrt(jnp.asarray(d, q.dtype))
            attn = jax.nn.softmax(scores, axis=-1)
            out = jnp.einsum('bhqk,bkhd->bqhd', attn, vh)
            return out.reshape(B, Nq, C)
        C = x.shape[-1]
        m = jax.nn.silu(mod) @ ada_w + ada_b
        shift_msa, scale_msa, gate_msa, shift_mlp, scale_mlp, gate_mlp = [c[:, None, :] for c in jnp.split(m, 6, axis=-1)]
        h = layer_norm(x)
        h = h * (1.0 + scale_msa) + shift_msa
        qkv = h @ qkv_w + qkv_b
        q, k, v = jnp.split(qkv, 3, axis=-1)
        h = mha(q, k, v) @ self_o_w + self_o_b
        x = x + h * gate_msa
        h = layer_norm(x, norm2_g, norm2_b)
        q = h @ q_w + q_b
        kv = context @ kv_w + kv_b
        k, v = jnp.split(kv, 2, axis=-1)
        h = mha(q, k, v) @ cross_o_w + cross_o_b
        x = x + h
        h = layer_norm(x)
        h = h * (1.0 + scale_mlp) + shift_mlp
        h = jax.nn.gelu(h @ mlp_w1 + mlp_b1) @ mlp_w2 + mlp_b2
        x = x + h * gate_mlp
        return x

    def _L3_xcond_ref(x, c, context, W_mod, b_mod, W_qkv, b_qkv, W_proj, b_proj, W_qc, b_qc, W_kvc, b_kvc, W_cproj, b_cproj, W_mlp1, b_mlp1, W_mlp2, b_mlp2):
        import jax, jax.numpy as jnp
        import numpy as np
        LN_EPS = 1e-06

        def _ln(x):
            mu = jnp.mean(x, axis=-1, keepdims=True)
            var = jnp.var(x, axis=-1, keepdims=True)
            return (x - mu) * jax.lax.rsqrt(var + LN_EPS)
        B, N, H = x.shape
        NH = 16
        hd = H // NH
        scale = hd ** (-0.5)
        c_proj = jax.nn.silu(c) @ W_mod + b_mod
        shift_a, scale_a, gate_a, shift_m, scale_m, gate_m = jnp.split(c_proj, 6, axis=-1)

        def modulate(t, shift, sc):
            return t * (1 + sc[:, None]) + shift[:, None]
        x_norm = modulate(_ln(x), shift_a, scale_a)
        qkv = x_norm @ W_qkv + b_qkv
        q, k, v = jnp.split(qkv, 3, axis=-1)
        q = q.reshape(B, N, NH, hd).transpose(0, 2, 1, 3)
        k = k.reshape(B, N, NH, hd).transpose(0, 2, 1, 3)
        v = v.reshape(B, N, NH, hd).transpose(0, 2, 1, 3)
        attn_w = jax.nn.softmax(jnp.einsum('bhqd,bhkd->bhqk', q, k) * scale, axis=-1)
        attn_out = jnp.einsum('bhqk,bhkd->bhqd', attn_w, v)
        attn_out = attn_out.transpose(0, 2, 1, 3).reshape(B, N, H)
        attn_out = attn_out @ W_proj + b_proj
        x = x + gate_a[:, None] * attn_out
        S = context.shape[1]
        q_c = _ln(x) @ W_qc + b_qc
        kv_c = _ln(context) @ W_kvc + b_kvc
        k_c, v_c = jnp.split(kv_c, 2, axis=-1)
        q_c = q_c.reshape(B, N, NH, hd).transpose(0, 2, 1, 3)
        k_c = k_c.reshape(B, S, NH, hd).transpose(0, 2, 1, 3)
        v_c = v_c.reshape(B, S, NH, hd).transpose(0, 2, 1, 3)
        c_attn_w = jax.nn.softmax(jnp.einsum('bhqd,bhsd->bhqs', q_c, k_c) * scale, axis=-1)
        c_attn_out = jnp.einsum('bhqs,bhsd->bhqd', c_attn_w, v_c)
        c_attn_out = c_attn_out.transpose(0, 2, 1, 3).reshape(B, N, H)
        c_attn_out = c_attn_out @ W_cproj + b_cproj
        x = x + c_attn_out
        x_norm2 = modulate(_ln(x), shift_m, scale_m)
        h = jax.nn.gelu(x_norm2 @ W_mlp1 + b_mlp1)
        h = h @ W_mlp2 + b_mlp2
        x = x + gate_m[:, None] * h
        return x
    x = _L0_xcond_ref(x, cond_1024, ctx_1024, L0_xcond_adaln_w, L0_xcond_adaln_b, L0_xcond_qkv_w, L0_xcond_qkv_b, L0_xcond_sa_proj_w, L0_xcond_sa_proj_b, L0_xcond_q_w, L0_xcond_q_b, L0_xcond_kv_w, L0_xcond_kv_b, L0_xcond_ca_proj_w, L0_xcond_ca_proj_b, L0_xcond_fc1_w, L0_xcond_fc1_b, L0_xcond_fc2_w, L0_xcond_fc2_b)
    x = _L1_xcond_ref(x, ctx_1024, cond_1024, L1_xcond_Wq, L1_xcond_bq, L1_xcond_Wkv, L1_xcond_bkv, L1_xcond_Wp, L1_xcond_bp, L1_xcond_Wss_q, L1_xcond_bss_q, L1_xcond_Wss_kv, L1_xcond_bss_kv)
    x = _L2_xcond_ref(x, cond_1024, ctx_1024, L2_xcond_ada_w, L2_xcond_ada_b, L2_xcond_qkv_w, L2_xcond_qkv_b, L2_xcond_self_o_w, L2_xcond_self_o_b, L2_xcond_norm2_g, L2_xcond_norm2_b, L2_xcond_q_w, L2_xcond_q_b, L2_xcond_kv_w, L2_xcond_kv_b, L2_xcond_cross_o_w, L2_xcond_cross_o_b, L2_xcond_mlp_w1, L2_xcond_mlp_b1, L2_xcond_mlp_w2, L2_xcond_mlp_b2)
    x = _L3_xcond_ref(x, cond_1024, ctx_1024, L3_xcond_W_mod, L3_xcond_b_mod, L3_xcond_W_qkv, L3_xcond_b_qkv, L3_xcond_W_proj, L3_xcond_b_proj, L3_xcond_W_qc, L3_xcond_b_qc, L3_xcond_W_kvc, L3_xcond_b_kvc, L3_xcond_W_cproj, L3_xcond_b_cproj, L3_xcond_W_mlp1, L3_xcond_b_mlp1, L3_xcond_W_mlp2, L3_xcond_b_mlp2)
    return x

_drawn_inputs = setup_inputs


def setup_inputs(seed=0):
    import zlib

    import numpy as np

    out = dict(_drawn_inputs(seed))
    spreads = {'L1_xcond_bq': (0.0, 2.0),
     'L1_xcond_bkv': (0.0, 0.8),
     'L1_xcond_bp': (0.0, 0.276),
     'L1_xcond_bss_q': (0.0, 2.0),
     'L1_xcond_bss_kv': (0.0, 2.0),
     'L2_xcond_ada_b': (0.0, 0.442),
     'L2_xcond_qkv_b': (0.0, 0.8),
     'L2_xcond_self_o_b': (0.0, 0.363),
     'L2_xcond_norm2_g': (1.0, 0.6),
     'L2_xcond_norm2_b': (0.0, 2.0),
     'L2_xcond_q_b': (0.0, 2.0),
     'L2_xcond_kv_b': (0.0, 0.8),
     'L2_xcond_cross_o_b': (0.0, 0.429),
     'L2_xcond_mlp_b1': (0.0, 2.0),
     'L2_xcond_mlp_b2': (0.0, 1.149),
     'L3_xcond_b_mod': (0.0, 0.274),
     'L3_xcond_b_qkv': (0.0, 0.72),
     'L3_xcond_b_proj': (0.0, 0.693),
     'L3_xcond_b_qc': (0.0, 2.0),
     'L3_xcond_b_kvc': (0.0, 0.467),
     'L3_xcond_b_cproj': (0.0, 0.459),
     'L3_xcond_b_mlp1': (0.0, 1.08),
     'L3_xcond_b_mlp2': (0.0, 0.7)}
    factors = {'L0_xcond_adaln_w': 2.875,
     'L0_xcond_adaln_b': 8.0,
     'L0_xcond_qkv_w': 8.0,
     'L0_xcond_qkv_b': 8.0,
     'L0_xcond_sa_proj_w': 8.0,
     'L0_xcond_sa_proj_b': 8.0,
     'L0_xcond_q_w': 64.0,
     'L0_xcond_q_b': 64.0,
     'L0_xcond_kv_b': 32.79,
     'L0_xcond_ca_proj_b': 10.353,
     'L0_xcond_fc1_w': 3.125,
     'L0_xcond_fc1_b': 8.0,
     'L0_xcond_fc2_w': 3.008,
     'L0_xcond_fc2_b': 8.0,
     'L1_xcond_Wq': 23.27,
     'L1_xcond_Wss_q': 26.351,
     'L2_xcond_qkv_w': 8.0,
     'L2_xcond_self_o_w': 6.555,
     'L2_xcond_q_w': 64.0,
     'L2_xcond_mlp_w1': 2.769,
     'L0_xcond_kv_w': 3.593,
     'L0_xcond_ca_proj_w': 2.767,
     'L1_xcond_Wss_kv': 7.282,
     'L2_xcond_kv_w': 4.988,
     'L2_xcond_cross_o_w': 4.633}
    for name, (base, spread) in spreads.items():
        noise = np.random.default_rng([zlib.crc32(name.encode()), seed]).standard_normal(out[name].shape)
        drawn = base * np.exp(spread * noise) if base else spread * noise
        out[name] = jnp.asarray(drawn.astype(out[name].dtype))
    for name, factor in factors.items():
        out[name] = (out[name] * factor).astype(out[name].dtype)
    return out
```

```python
from contextlib import ExitStack

import numpy as np

import concourse.bass as bass
from concourse import mybir

F32 = mybir.dt.float32
F32R = mybir.dt.float32r
ALU = mybir.AluOpType
ACT = mybir.ActivationFunctionType
AX = mybir.AxisListType

P = 128
D = 256
KC = D // P
H = 16
HD = D // H
NT = 256
TT = NT // P
S = 120
MLP = 4 * D
MC = MLP // P
QUAD = 4
SLOT = 1024
BANK = 512
SLOTS = 3
SCALE = HD ** -0.5
LO_ROW = 64
MAX_ROW = 96
STACK_ROWS = MAX_ROW + 2

FULL = (True, False, True, True)
EPS = (1e-6, 1e-5, 1e-6, 1e-6)
CTX_LN = (False, True, False, True)
LAYERS = 4


def head_of(j):
    return (j % 2) * (H // 2) + j // 2


SELF_ATT = ["S0", "S1", "S2", "S3", "S4", "M0", "S5", "S6", "S7", "T0", "M1", "T1", "PV0", "T2", "PV1", "T3",
            "PV2", "T4", "PV3", "T5", "PV4", "T6", "PV5", "T7", "PV6", "PV7", "O1", "O2", "PR"]
CROSS_ATT = ["S0", "S1", "S2", "M0", "S3", "T0", "M1", "T1", "PV0", "T2", "PV1", "T3", "PV2", "PV3", "O1", "O2",
             "PR"]
F_FULL = ["LN", "QK", "V"] + SELF_ATT
G_FULL = ["C", "KV", "LN", "Q"] + CROSS_ATT + ["LN3", "H0", "H1", "F2"]
L1_FIRST = ["C", "KV", "LN", "Q"]
L1_SECOND = CROSS_ATT


def role_steps(layer, role):
    if FULL[layer]:
        return F_FULL if role == "F" else G_FULL
    return L1_FIRST + L1_SECOND


COST = {"LN": 0.3, "QK": 3.5, "V": 1.8, "C": 0.2, "KV": 1.7, "Q": 1.8, "S": 0.45, "M": 0.1, "T": 0.45,
        "PV": 0.55, "O1": 0.5, "O2": 0.3, "PR": 1.8, "LN3": 0.3, "H": 3.5, "F2": 7.0, "ld": 0.0, "ST": 0.0}


def cost(step):
    return COST[step] if step in COST else COST[step.rstrip("01234567")]


def merge(a, b):
    total = [sum(cost(e[2]) for e in x) or 1 for x in (a, b)]
    at = [0.0, 0.0]
    out, i, j = [], 0, 0
    while i < len(a) or j < len(b):
        if j >= len(b) or (i < len(a) and at[0] / total[0] <= at[1] / total[1]):
            out.append(a[i])
            at[0] += cost(a[i][2])
            i += 1
        else:
            out.append(b[j])
            at[1] += cost(b[j][2])
            j += 1
    return out


def entries(role, layer, steps, n):
    return [(role, layer, s, n) for s in steps]


def segments(nb):
    pairs = nb // 2
    out = [("pre", 0), ("weights", 0)]
    out.append(("run", entries("F", 0, ["ld"] + F_FULL, 0)))
    body = merge(entries("F", 0, ["ld"] + F_FULL, 1), entries("G", 0, ["ld"] + G_FULL + ["ST"], 0))
    out.append(("run", body))
    if nb > 2:
        out.append(("loop", nb - 2, [(r, m, s, n + 1) for r, m, s, n in body]))
    out.append(("pre", 1))
    first, second = ["ld"] + L1_FIRST, L1_SECOND + ["ST"]
    out.append(("run", merge(entries("F", 1, first, 0), entries("G", 0, ["ld"] + G_FULL + ["ST"], nb - 1))))
    out.append(("weights", 2))
    if pairs > 1:
        body = merge(entries("F", 1, second, 0), entries("G", 1, first, 0)) + \
            merge(entries("F", 1, first, 1), entries("G", 1, second, 0))
        out.append(("run", body))
    if pairs > 2:
        out.append(("loop", pairs - 2, [(r, m, s, n + 1) for r, m, s, n in body]))
    out.append(("run", merge(entries("F", 1, second, pairs - 1), entries("G", 1, first, pairs - 1))))
    out.append(("pre", 2))
    out.append(("run", merge(entries("G", 1, second, pairs - 1), entries("F", 2, ["ld"] + F_FULL, 0))))
    for layer in (2, 3):
        body = merge(entries("F", layer, ["ld"] + F_FULL, 1), entries("G", layer, ["ld"] + G_FULL + ["ST"], 0))
        out.append(("loop", nb - 1, body))
        last = entries("G", layer, ["ld"] + G_FULL + ["ST"], nb - 1)
        if layer == 2:
            out.append(("pre", 3))
            out.append(("run", merge(entries("F", 3, ["ld"] + F_FULL, 0), last)))
            out.append(("weights", 3))
        else:
            out.append(("run", last))
    return out


class Signal:

    def __init__(self, sem, steps, batches, by=1):
        self.sem, self.by = sem, by
        self.steps = [list(steps(layer)) for layer in range(LAYERS)]
        self.base = [0]
        for layer in range(LAYERS):
            self.base.append(self.base[-1] + by * len(self.steps[layer]) * batches[layer])

    def after(self, layer, step, n, nth=-1):
        at = [i for i, s in enumerate(self.steps[layer]) if s == step][nth]
        return n * (self.by * len(self.steps[layer])) + (self.base[layer] + self.by * (at + 1))

    def before(self, layer, n):
        if not self.steps[layer]:
            return self.base[layer]
        return n * (self.by * len(self.steps[layer])) + self.base[layer]

    def wait_before(self, eng, layer, n):
        value = self.before(layer, n)
        if not isinstance(value, int) or value > 0:
            eng.wait_ge(self.sem, value)


def numbered(name, steps):
    return [s for s in steps if s.startswith(name) and s[len(name):].isdigit()]


def places(steps):
    users = [e[:3] for e in steps if e[2] not in ("ld", "ST") and not e[2].startswith("PV")]
    return {e: i % SLOTS for i, e in enumerate(users)}


def walk(eng, program, handler, at_pre=None, at_weights=None):
    for seg in program:
        if seg[0] == "pre":
            if at_pre:
                at_pre(seg[1])
        elif seg[0] == "weights":
            if at_weights:
                at_weights(seg[1])
        elif seg[0] == "run":
            place = places(seg[1])
            for role, layer, step, n in seg[1]:
                handler(role, layer, step, n, False, place.get((role, layer, step)))
        elif seg[1] > 0:
            place = places(seg[2])
            with eng.Fori(0, seg[1]) as it:
                for role, layer, step, dn in seg[2]:
                    handler(role, layer, step, it + dn, True, place.get((role, layer, step)))


def build_program(nc, a, out, nb=16):
    program = segments(nb)
    ctx = ExitStack()
    with ctx:
        def sb(name, shape, dt=F32):
            return ctx.enter_context(nc.sbuf_tensor(name, shape, dt))

        def scratch(name, shape):
            return nc.dram_tensor(name, shape, F32, kind="Internal").ap()

        x_in = [a["x"]] + [scratch(f"x_after_{m}", [nb, NT, D]) for m in range(LAYERS - 1)]
        x_out = x_in[1:] + [out]
        gate_rows = [scratch(f"gate_rows_{m}", [nb, 4, D]) if FULL[m] else None for m in range(LAYERS)]
        q_parts_dram = {r: scratch(f"q_parts_{r}", [P, 2, KC * NT]) for r in "FG"}
        k_parts_dram = {r: scratch(f"k_parts_{r}", [P, 2, KC * NT]) for r in "F"}
        kc_parts_dram = {r: scratch(f"kc_parts_{r}", [P, 2, KC * S]) for r in "FG"}

        ident = sb("ident", [P, P])
        w_qkv = sb("w_qkv", [P, KC, 3 * D])
        w_proj = [sb(f"w_proj{i}", [P, KC, D]) for i in range(2)]
        w_q2 = sb("w_q2", [P, KC, D])
        w_kv2 = sb("w_kv2", [P, KC, 2 * D])
        w_cp = sb("w_cp", [P, KC, D])
        w_fc1 = sb("w_fc1", [P, KC, MLP])
        w_fc2 = sb("w_fc2", [P, MC, D])
        w_ada = sb("w_ada", [P, KC, 6 * D])
        rows = sb("rows", [36, P])
        cols = [sb(f"cols{i}", [P, 36]) for i in range(2)]
        mods = [sb(f"mods{i}", [P, nb, 8]) for i in range(2)]
        v_bias = [sb(f"v_bias{i}", [P, D]) for i in range(2)]
        vc_bias = [sb(f"vc_bias{i}", [P, D]) for i in range(2)]
        cp_bias = [sb(f"cp_bias{i}", [P, D]) for i in range(2)]
        cond = sb("cond", [nb, D])
        cond_e = sb("cond_e", [nb, D])
        silu_t = sb("silu_t", [P, KC, nb])

        x = {r: sb(f"x_{r}", [P, TT, D]) for r in "FG"}
        x_new = {r: sb(f"x_new_{r}", [P, TT, D]) for r in "FG"}
        x_mid = x_new["F"]
        x_hat = {r: sb(f"x_hat_{r}", [P, TT, D]) for r in "FG"}
        x_t = {r: sb(f"x_t_{r}", [P, KC, NT]) for r in "FG"}
        stats = {r: sb(f"stats_{r}", [P, TT, 6]) for r in "FG"}
        mean_var = {r: sb(f"mean_var_{r}", [P, TT, 2]) for r in "FG"}
        var_eps = {r: sb(f"var_eps_{r}", [P, TT]) for r in "FG"}
        rstd = {r: sb(f"rstd_{r}", [P, TT]) for r in "FG"}
        c_stats = {r: sb(f"c_stats_{r}", [P, 6]) for r in "FG"}
        c_mean_var = {r: sb(f"c_mean_var_{r}", [P, 2]) for r in "FG"}
        c_var_eps = {r: sb(f"c_var_eps_{r}", [P, 1]) for r in "FG"}
        c_rstd = {r: sb(f"c_rstd_{r}", [P, 1]) for r in "FG"}
        wait_mark = sb("wait_mark", [1, 1])
        minus_half = sb("minus_half", [P, TT])
        mod_now = {r: sb(f"mod_now_{r}", [P, 8]) for r in "FG"}
        gate_now = {r: sb(f"gate_now_{r}", [P, 2, D]) for r in "FG"}
        gated = {r: sb(f"gated_{r}", [P, TT, D]) for r in "FG"}
        context = {r: sb(f"context_{r}", [P, D]) for r in "FG"}
        context_hat = {r: sb(f"context_hat_{r}", [P, D]) for r in "FG"}
        context_t = {r: sb(f"context_t_{r}", [P, KC, S]) for r in "FG"}
        q_parts = {r: sb(f"q_parts_sb_{r}", [P, 2, KC, NT]) for r in "FG"}
        k_parts = sb("k_parts_sb", [P, 2, KC, NT])
        kc_parts = {r: sb(f"kc_parts_sb_{r}", [P, 2, KC, S]) for r in "FG"}
        q_stack = {r: sb(f"q_stack_{r}", [P, H, NT]) for r in "FG"}
        k_stack = {"F": sb("k_stack_F", [P, H * NT]), "G": sb("k_stack_G", [P, H * S])}
        v_self = sb("v_self", [P, TT, H, 2 * HD])
        v_ctx = {r: sb(f"v_ctx_{r}", [P, H, 2 * HD]) for r in "FG"}
        row_max = {r: sb(f"row_max_{r}", [P, TT, H]) for r in "FG"}
        max_parts = {r: sb(f"max_parts_{r}", [P, TT, 2, 2, H // 2]) for r in "FG"}
        max_t = {r: [sb(f"max_t_{r}{h}", [H, NT]) for h in range(2)] for r in "FG"}
        probs = {r: [sb(f"probs_{r}{i}", [P, QUAD, NT]) for i in range(2)] for r in "FG"}
        o_raw = {r: sb(f"o_raw_{r}", [P, H // QUAD, NT]) for r in "FG"}
        r_den = {r: sb(f"r_den_{r}", [P, TT, H]) for r in "FG"}
        o_norm = x_hat
        o_t = x_t
        h_t = sb("h_t", [P, MC, NT])
        bias_rows = probs["F"][0]
        gate_sb = probs["F"][1]

        slot = [ctx.enter_context(nc.psum_tensor(f"slot{i}", [P, SLOT], F32)) for i in range(SLOTS)]
        o_acc = {r: ctx.enter_context(nc.psum_tensor(f"o_acc_{r}", [P, BANK], F32)) for r in "FG"}

        def batches(role):
            return [(nb if FULL[m] else nb // 2) for m in range(LAYERS)]

        def signal(name, steps, by=1):
            return {r: Signal(ctx.enter_context(nc.semaphore(f"{name}_{r}")), lambda m, r=r: steps(m, r),
                              batches(r), by) for r in "FG"}

        def only(*names):
            return lambda m, r: [s for s in role_steps(m, r) if s in names]

        def norms(m, r):
            return [s for s in role_steps(m, r) if s in ("LN", "LN3") or (s == "C" and CTX_LN[m])]

        def out_banks(m, r):
            return ["PV3", "PV7"] if FULL[m] and r == "F" else ["PV1", "PV3"]

        psum_ready = signal("psum_ready", lambda m, r: role_steps(m, r))
        x_t_ready = signal("x_t_ready", only("LN", "LN3"))
        context_t_ready = signal("context_t_ready", only("C"))
        hi_ready = signal("hi_ready", only("QK", "Q", "KV"))
        max_t_ready = signal("max_t_ready", lambda m, r: numbered("M", role_steps(m, r)))
        probs_ready = signal("probs_ready", lambda m, r: numbered("T", role_steps(m, r)))
        o_raw_ready = signal("o_raw_ready", out_banks)
        o_t_ready = signal("o_t_ready", only("O2"))
        h_ready = signal("h_ready", only("H0", "H1"))
        mod_ready = signal("mod_ready", lambda m, r: ["ld"])
        stats_ready = signal("stats_ready", norms)
        mean_ready = signal("mean_ready", norms)
        var_ready = signal("var_ready", norms)
        x_hat_ready = signal("x_hat_ready", norms)
        lo_ready = signal("lo_ready", only("QK", "Q", "KV"))
        v_ready = signal("v_ready", only("V", "KV"))
        row_max_ready = signal("row_max_ready", lambda m, r: numbered("S", role_steps(m, r)))
        max_hi_ready = signal("max_hi_ready", lambda m, r: numbered("M", role_steps(m, r)))
        max_parts_ready = signal("max_parts_ready", lambda m, r: numbered("M", role_steps(m, r)))
        r_den_ready = signal("r_den_ready", only("O1"))
        o_norm_ready = signal("o_norm_ready", only("O1"))
        gated_ready = signal("gated_ready", lambda m, r: [] if not FULL[m] else (["PR"] if r == "F" else ["F2"]))
        x_cross_ready = signal("x_cross_ready", lambda m, r: ["PR"] if FULL[m] and r == "G" else [])
        rstd_ready = signal("rstd_ready", norms)
        x_biased = signal("x_biased", lambda m, r: [s for s in role_steps(m, r) if s in ("LN", "LN3")])
        x_mid_ready = signal("x_mid_ready", lambda m, r: ["PR"] if FULL[m] and r == "F" else [])
        x_new_ready = signal("x_new_ready", lambda m, r: (["F2"] if r == "G" else []) if FULL[m] else ["PR"])
        x_loaded = signal("x_loaded", lambda m, r: ["ld"] if r == "F" or not FULL[m] else [], 16)
        gate_loaded = signal("gate_loaded", lambda m, r: ["ld"] if FULL[m] else [], 16)
        context_loaded = signal("context_loaded", lambda m, r: ["ld"] if r == "G" or not FULL[m] else [], 16)
        q_stored = signal("q_stored", only("QK", "Q"), 16)
        k_stored = signal("k_stored", only("QK", "KV"), 16)
        q_stack_loaded = signal("q_stack_loaded", only("QK", "Q"), 48)
        k_stack_loaded = signal("k_stack_loaded", only("QK", "KV"), 48)
        max_row_loaded = [signal(f"max_row_loaded{h}", only(f"M{h}"), 16) for h in range(2)]
        x_stored = signal("x_stored", lambda m, r: ["ST"] if r == "G" or not FULL[m] else [], 16)

        cond_loaded = ctx.enter_context(nc.semaphore("cond_loaded"))
        silu_step = ctx.enter_context(nc.semaphore("silu_step"))
        silu_exp = ctx.enter_context(nc.semaphore("silu_exp"))
        silu_psum = ctx.enter_context(nc.semaphore("silu_psum"))
        const_ready = ctx.enter_context(nc.semaphore("const_ready"))
        ident_zero = ctx.enter_context(nc.semaphore("ident_zero"))
        ident_ready = ctx.enter_context(nc.semaphore("ident_ready"))
        rows_loaded = ctx.enter_context(nc.semaphore("rows_loaded"))
        ada_loaded = ctx.enter_context(nc.semaphore("ada_loaded"))
        bias_spread = ctx.enter_context(nc.semaphore("bias_spread"))
        gate_bias_loaded = ctx.enter_context(nc.semaphore("gate_bias_loaded"))
        wf_loaded = ctx.enter_context(nc.semaphore("wf_loaded"))
        wg_loaded = ctx.enter_context(nc.semaphore("wg_loaded"))
        pre_psum = ctx.enter_context(nc.semaphore("pre_psum"))
        cols_ready = ctx.enter_context(nc.semaphore("cols_ready"))
        mods_ready = ctx.enter_context(nc.semaphore("mods_ready"))
        gate_ready = ctx.enter_context(nc.semaphore("gate_ready"))
        gate_times_bias = ctx.enter_context(nc.semaphore("gate_times_bias"))
        gate_stored = ctx.enter_context(nc.semaphore("gate_stored"))

        CONSTS = 1 + 3 + 2 * 5

        def name(m, full_names, l1):
            return a[{0: f"L0_xcond_{full_names[0]}", 2: f"L2_xcond_{full_names[1]}",
                      3: f"L3_xcond_{full_names[2]}"}[m] if m != 1 else f"L1_xcond_{l1}"]

        def w(m, key):
            table = {
                "ada_w": ("adaln_w", "ada_w", "W_mod"), "ada_b": ("adaln_b", "ada_b", "b_mod"),
                "qkv_w": ("qkv_w", "qkv_w", "W_qkv"), "qkv_b": ("qkv_b", "qkv_b", "b_qkv"),
                "proj_w": ("sa_proj_w", "self_o_w", "W_proj"), "proj_b": ("sa_proj_b", "self_o_b", "b_proj"),
                "q_w": ("q_w", "q_w", "W_qc"), "q_b": ("q_b", "q_b", "b_qc"),
                "kv_w": ("kv_w", "kv_w", "W_kvc"), "kv_b": ("kv_b", "kv_b", "b_kvc"),
                "cp_w": ("ca_proj_w", "cross_o_w", "W_cproj"), "cp_b": ("ca_proj_b", "cross_o_b", "b_cproj"),
                "fc1_w": ("fc1_w", "mlp_w1", "W_mlp1"), "fc1_b": ("fc1_b", "mlp_b1", "b_mlp1"),
                "fc2_w": ("fc2_w", "mlp_w2", "W_mlp2"), "fc2_b": ("fc2_b", "mlp_b2", "b_mlp2"),
            }
            return name(m, table[key], None)

        l1 = {k: a[f"L1_xcond_{k}"] for k in ("Wq", "bq", "Wkv", "bkv", "Wp", "bp", "Wss_q", "bss_q", "Wss_kv",
                                              "bss_kv")}
        COL = {"ada": 0, "qkv": 12, "q": 18, "kv": 20, "fc1": 24, "gamma": 32, "beta": 34} 
        COL1 = {"ada": 0, "q": 8, "kv": 10}

        def row_vectors(m):
            if not FULL[m]:
                return [(0, l1["bss_q"]), (4, l1["bss_kv"]), (COL1["q"], l1["bq"]), (COL1["kv"], l1["bkv"])]
            v = [(COL["ada"], w(m, "ada_b")), (COL["qkv"], w(m, "qkv_b")), (COL["q"], w(m, "q_b")),
                 (COL["kv"], w(m, "kv_b")), (COL["fc1"], w(m, "fc1_b"))]
            if m == 2:
                v += [(COL["gamma"], a["L2_xcond_norm2_g"]), (COL["beta"], a["L2_xcond_norm2_b"])]
            return v

        def n_rows(m):
            return max(at + v.shape[0] // P for at, v in row_vectors(m))

        def col(m, key, i):
            at = (COL if FULL[m] else COL1)[key] + i
            return cols[m % 2][:, at:at + 1]

        def mod_sources(m):
            starts = (256, 0, 1024, 768) if FULL[m] else (0, 256, 512, 768)
            return [s + P * c for s in starts for c in range(KC)]

        def rows_done(m):
            return 16 * sum(len(row_vectors(i)) for i in range(m + 1))

        ADA_DMAS = [1, 2, 1, 1]

        def ada_done(m):
            return 16 * sum(ADA_DMAS[:m + 1])

        SPREAD = [3, 2, 3, 3]

        def spread_done(m):
            return 16 * sum(SPREAD[:m + 1])

        WF_DMAS = [2, 3, 2, 2]

        def wf_done(m):
            return 16 * sum(WF_DMAS[:m + 1])

        PRE_PSUM = [3, 2, 3, 3]

        def pre_done(m, k):
            return sum(PRE_PSUM[:m]) + k

        FULL_BEFORE = [sum(FULL[:m]) for m in range(LAYERS + 1)]

        def stack_source(dram, part, width):
            return dram.rearrange("(h d) e w -> e d h w", d=HD)[part]

        def is_self(m, r):
            return FULL[m] and r == "F"

        def parts_of(r, m, step, here):
            for c in range(KC):
                if step == "QK":
                    yield slot[here][:, c * NT:(c + 1) * NT], col(m, "qkv", c), q_parts[r], c
                    yield slot[here][:, BANK + c * NT:BANK + (c + 1) * NT], col(m, "qkv", KC + c), k_parts, c
                elif step == "Q":
                    yield slot[here][:, c * NT:(c + 1) * NT], col(m, "q", c), q_parts[r], c
                else:
                    yield slot[here][:, c * S:(c + 1) * S], col(m, "kv", c), kc_parts[r], c

        block = ctx.enter_context(nc.Block())

        @block.sync
        def _(sp):
            def weight(dst, src, sem, chunks=KC):
                sp.dma_start(dst, src.rearrange("(k p) n -> p k n", k=chunks)).then_inc(sem, 16)

            def load_ada(m):
                if FULL[m]:
                    weight(w_ada[:, :, :], w(m, "ada_w"), ada_loaded)
                else:
                    weight(w_ada[:, :, 0:2 * D], l1["Wss_q"], ada_loaded)
                    weight(w_ada[:, :, 2 * D:4 * D], l1["Wss_kv"], ada_loaded)

            def pre(m):
                if m == 0:
                    sp.dma_start(cond[:, :], a["cond_1024"][0:nb, :]).then_inc(cond_loaded, 16)
                    load_ada(0)
                else:
                    sp.wait_ge(pre_psum, pre_done(m - 1, 1))
                for at, v in row_vectors(m):
                    sp.dma_start(rows[at:at + v.shape[0] // P, :], v.rearrange("(n p) -> n p", p=P))\
                        .then_inc(rows_loaded, 16)
                if FULL[m]:
                    if m > 0:
                        prev = "PV3" if not FULL[m - 1] else "PV7"
                        last = nb - 1 if FULL[m - 1] else nb // 2 - 1
                        sp.wait_ge(psum_ready["F"].sem, psum_ready["F"].after(m - 1, prev, last))
                    ab = w(m, "ada_b").rearrange("(g d) -> g d", d=D)
                    for i, v in enumerate((ab[2], w(m, "proj_b"), ab[5], w(m, "fc2_b"))):
                        sp.dma_start(bias_rows[0:nb, i, :], v.unsqueeze(0).to_broadcast([nb, D]))\
                            .then_inc(gate_bias_loaded, 16)
                if m > 0:
                    if FULL[m - 1]:
                        sp.wait_ge(psum_ready["F"].sem, psum_ready["F"].after(m - 1, "V", nb - 1))
                    else:
                        for r in "FG":
                            sp.wait_ge(psum_ready[r].sem, psum_ready[r].after(m - 1, "Q", nb // 2 - 1))
                if FULL[m]:
                    weight(w_qkv[:, :, :], w(m, "qkv_w"), wf_loaded)
                    weight(w_proj[m % 2][:, :, :], w(m, "proj_w"), wf_loaded)
                    spread = ((v_bias, w(m, "qkv_b")[2 * D:3 * D]), (vc_bias, w(m, "kv_b")[D:2 * D]),
                              (cp_bias, w(m, "cp_b")))
                else:
                    weight(w_qkv[:, :, 0:D], l1["Wq"], wf_loaded)
                    weight(w_qkv[:, :, D:3 * D], l1["Wkv"], wf_loaded)
                    weight(w_proj[m % 2][:, :, :], l1["Wp"], wf_loaded)
                    spread = ((vc_bias, l1["bkv"][D:2 * D]), (cp_bias, l1["bp"]))
                for tile, v in spread:
                    sp.dma_start(tile[m % 2][:, :], v.unsqueeze(0).to_broadcast([P, D])).then_inc(bias_spread, 16)
                if FULL[m]:
                    sp.wait_ge(gate_times_bias, FULL_BEFORE[m] + 1)
                    sp.dma_start(gate_rows[m], gate_sb[0:nb, :, :]).then_inc(gate_stored, 16)
                if m + 1 < LAYERS:
                    sp.wait_ge(pre_psum, pre_done(m, PRE_PSUM[m]))
                    load_ada(m + 1)

            def weights_g(m):
                if m > 0:
                    prev = 0 if m == 2 else m - 1
                    sp.wait_ge(psum_ready["G"].sem, psum_ready["G"].after(prev, "F2", nb - 1))
                weight(w_kv2[:, :, :], w(m, "kv_w"), wg_loaded)
                weight(w_q2[:, :, :], w(m, "q_w"), wg_loaded)
                weight(w_cp[:, :, :], w(m, "cp_w"), wg_loaded)
                weight(w_fc1[:, :, :], w(m, "fc1_w"), wg_loaded)
                weight(w_fc2[:, :, :], w(m, "fc2_w"), wg_loaded, MC)

            def batch(r, m, n):
                return n if FULL[m] else 2 * n + (r == "G")

            def handler(r, m, step, n, looping, here):
                if step == "ld":
                    b = batch(r, m, n)
                    x_src = x_in[m][bass.ds(b, 1)].rearrange("o (t p) d -> p (o t) d", p=P)
                    context_src = a["ctx_1024"][bass.ds(b, 1)].rearrange("o s d -> (o s) d")
                    g = 0 if r == "F" else 2
                    gate_src = None
                    if FULL[m]:
                        gate_src = gate_rows[m][bass.ds(b, 1), g:g + 2, :].to_broadcast([P, 2, D])
                    if r == "F" or not FULL[m]:
                        x_mid_ready[r].wait_before(sp, m, n)
                        x_new_ready[r].wait_before(sp, m, n)
                        if m > 0:
                            if looping:
                                for q in "FG":
                                    x_stored[q].wait_before(sp, m, 0)
                            else:
                                q = "G" if FULL[m - 1] else "FG"[b % 2]
                                sp.wait_ge(x_stored[q].sem,
                                           x_stored[q].after(m - 1, "ST", b if FULL[m - 1] else b // 2))
                        sp.dma_start(x[r][:, :, :], x_src).then_inc(x_loaded[r].sem, 16)
                    if r == "G" or not FULL[m]:
                        psum_ready[r].wait_before(sp, m, n)
                        sp.dma_start(context[r][0:S, :], context_src)\
                            .then_inc(context_loaded[r].sem, 16)
                    if FULL[m]:
                        if r == "G":
                            x_new_ready[r].wait_before(sp, m, n)
                        sp.wait_ge(gate_stored, 16 * (FULL_BEFORE[m] + 1))
                        sp.dma_start(gate_now[r][:, :, :], gate_src).then_inc(gate_loaded[r].sem, 16)
                elif step in ("QK", "Q", "KV"):
                    sp.wait_ge(lo_ready[r].sem, lo_ready[r].after(m, step, n))
                    if step in ("QK", "Q"):
                        sp.dma_start(q_parts_dram[r].rearrange("p e w -> p (e w)"),
                                     q_parts[r][:, :, :, :].rearrange("p e m w -> p (e m w)"))\
                            .then_inc(q_stored[r].sem, 16)
                    if step == "QK":
                        sp.dma_start(k_parts_dram["F"].rearrange("p e w -> p (e w)"),
                                     k_parts[:, :, :, :].rearrange("p e m w -> p (e m w)"))\
                            .then_inc(k_stored[r].sem, 16)
                    if step == "KV":
                        sp.dma_start(kc_parts_dram[r].rearrange("p e w -> p (e w)"),
                                     kc_parts[r][:, :, :, :].rearrange("p e m w -> p (e m w)"))\
                            .then_inc(k_stored[r].sem, 16)
                    if step in ("QK", "Q"):
                        sp.wait_ge(q_stored[r].sem, q_stored[r].after(m, step, n))
                        if not looping:
                            sp.wait_ge(const_ready, CONSTS)
                        for row, part in ((0, 0), (HD, 0), (LO_ROW, 1)):
                            sp.dma_start(q_stack[r][row:row + HD, :, :].rearrange("p (h m) w -> p h (m w)", m=KC),
                                         stack_source(q_parts_dram[r], part, NT)).then_inc(q_stack_loaded[r].sem, 16)
                    if step in ("QK", "KV"):
                        sp.wait_ge(k_stored[r].sem, k_stored[r].after(m, step, n))
                        if not looping:
                            sp.wait_ge(const_ready, CONSTS)
                        width, dram = (NT, k_parts_dram["F"]) if step == "QK" else (S, kc_parts_dram[r])
                        for row, part in ((0, 0), (HD, 1), (LO_ROW, 0)):
                            sp.dma_start(k_stack[r][row:row + HD, 0:H * width].rearrange("p (h w) -> p h w", h=H // 2),
                                         stack_source(dram, part, width)).then_inc(k_stack_loaded[r].sem, 16)
                elif step in ("M0", "M1"):
                    h = int(step[1])
                    sp.wait_ge(max_t_ready[r].sem, max_t_ready[r].after(m, step, n))
                    sp.dma_start(q_stack[r][MAX_ROW:MAX_ROW + 2, h * 8:h * 8 + 8, :], max_t[r][h][:, :])\
                        .then_inc(max_row_loaded[h][r].sem, 16)
                elif step == "ST":
                    b = batch(r, m, n)
                    after = "F2" if FULL[m] else "PR"
                    dst = x_out[m][bass.ds(b, 1)].rearrange("o (t p) d -> p (o t) d", p=P)
                    sp.wait_ge(x_new_ready[r].sem, x_new_ready[r].after(m, after, n))
                    sp.dma_start(dst, x_new[r][:, :, :]).then_inc(x_stored[r].sem, 16)

            walk(sp, program, handler, pre, weights_g)
            for r in "FG":
                sp.wait_ge(x_stored[r].sem, x_stored[r].base[LAYERS])

        @block.gpsimd
        def _(pool):
            nc.gpsimd.memset(ident[:, :], 0.0).then_inc(ident_zero, 1)
            pool.wait_ge(ident_zero, 1)
            nc.gpsimd.affine_select(out=ident[:, :], in_=ident[:, :], compare_op=ALU.not_equal, fill=1.0, base=0,
                                    pattern=[[-1, P]], channel_multiplier=1).then_inc(ident_ready, 1)
            nc.gpsimd.memset(minus_half[:, :], -0.5).then_inc(const_ready, 1)
            for t in (v_self, v_ctx["F"], v_ctx["G"]):
                flat = t[:, :, :, :].rearrange("p c h k -> p (c h) k") if len(t.shape) == 4 else t[:, :, :]
                nc.gpsimd.memset(flat[:, :, HD:2 * HD], 1.0).then_inc(const_ready, 1)
            done = 4
            for r in "FG":
                for t, lo, hi, value in ((q_stack[r][:, :, :], 32, 64, 0.0), (q_stack[r][:, :, :], 64, 96, 0.0),
                                         (k_stack[r][:, :], 32, 64, 0.0), (k_stack[r][:, :], 64, 96, 0.0),
                                         (k_stack[r][:, :], MAX_ROW, MAX_ROW + 2, 1.0)):
                    pool.wait_ge(const_ready, done)
                    nc.gpsimd.memset(t[lo:hi], value).then_inc(const_ready, 1)
                    done += 1
            pool.wait_ge(const_ready, done)

            def rstd_of(r, m, step, n):
                pool.wait_ge(var_ready[r].sem, var_ready[r].after(m, step, n))
                if step == "C":
                    nc.gpsimd.tensor_tensor(c_rstd[r][0:S, :], c_var_eps[r][0:S, :], minus_half[0:S, 0:1], ALU.pow)\
                        .then_inc(rstd_ready[r].sem, 1)
                else:
                    nc.gpsimd.tensor_tensor(rstd[r][:, :], var_eps[r][:, :], minus_half[:, :], ALU.pow)\
                        .then_inc(rstd_ready[r].sem, 1)

            def pre_add(r, m, step, n):
                pool.wait_ge(x_hat_ready[r].sem, x_hat_ready[r].after(m, step, n))
                if FULL[m] and r == "G" and step == "LN":
                    x_new_ready[r].wait_before(pool, m, n)
                    src = x_mid
                else:
                    src = x[r]
                if FULL[m] and (r == "F" or step == "LN3"):
                    pool.wait_ge(gate_loaded[r].sem, gate_loaded[r].after(m, "ld", n))
                    bias = gate_now[r][:, 1:2, :].to_broadcast([P, TT, D])
                else:
                    pool.wait_ge(bias_spread, spread_done(m))
                    bias = cp_bias[m % 2][:, :].unsqueeze(1).to_broadcast([P, TT, D])
                nc.gpsimd.tensor_tensor(x[r][:, :, :], src[:, :, :], bias, ALU.add).then_inc(x_biased[r].sem, 1)

            def handler(r, m, step, n, looping, here):
                if step == "C" and CTX_LN[m]:
                    rstd_of(r, m, step, n)
                elif step in ("LN", "LN3"):
                    rstd_of(r, m, step, n)
                    pre_add(r, m, step, n)
                elif step == "PR" and FULL[m] and r == "F":
                    pool.wait_ge(gated_ready[r].sem, gated_ready[r].after(m, "PR", n))
                    pool.wait_ge(x_biased[r].sem, x_biased[r].after(m, "LN", n))
                    if looping:
                        pool.wait_ge(x_biased["G"].sem, x_biased["G"].after(m, "LN", n - 1))
                    else:
                        x_stored["F"].wait_before(pool, m, 0)
                    nc.gpsimd.tensor_tensor(x_mid[:, :, :], x["F"][:, :, :], gated["F"][:, :, :], ALU.add)\
                        .then_inc(x_mid_ready[r].sem, 1)
                elif step == "F2":
                    pool.wait_ge(gated_ready[r].sem, gated_ready[r].after(m, "F2", n))
                    pool.wait_ge(x_biased[r].sem, x_biased[r].after(m, "LN3", n))
                    x_stored[r].wait_before(pool, m, n)
                    nc.gpsimd.tensor_tensor(x_new["G"][:, :, :], x["G"][:, :, :], gated["G"][:, :, :], ALU.add)\
                        .then_inc(x_new_ready[r].sem, 1)

            walk(pool, program, handler)

        @block.vector
        def _(dve):
            def pre(m):
                if m == 0:
                    dve.wait_ge(silu_exp, 1)
                    nc.vector.tensor_scalar(cond_e[:, :], cond_e[:, :], 1.0, None, ALU.add).then_inc(silu_step, 1)
                    dve.wait_ge(silu_step, 1)
                    nc.vector.reciprocal(cond_e[:, :], cond_e[:, :]).then_inc(silu_step, 1)
                    dve.wait_ge(silu_step, 2)
                    nc.vector.tensor_tensor(cond[:, :], cond[:, :], cond_e[:, :], ALU.mult).then_inc(silu_step, 1)
                    dve.wait_ge(silu_psum, 1)
                    nc.vector.tensor_copy(silu_t[:, :, :].rearrange("p k b -> p (k b)"), o_acc["F"][:, 0:KC * nb])\
                        .then_inc(silu_step, 1)
                dve.wait_ge(pre_psum, pre_done(m, 1))
                nc.vector.tensor_copy(cols[m % 2][:, 0:n_rows(m)], o_acc["F"][:, 0:n_rows(m)])\
                    .then_inc(cols_ready, 1)
                dve.wait_ge(pre_psum, pre_done(m, 2))
                dve.wait_ge(cols_ready, m + 1)
                for j, src in enumerate(mod_sources(m)):
                    one = 1.0 if j % 4 < KC else 0.0
                    last = nc.vector.tensor_scalar(mods[m % 2][:, :, j], o_acc["F"][:, 64 + nb * j:64 + nb * (j + 1)],
                                                   col(m, "ada", src // P), one, ALU.add, ALU.add)
                last.then_inc(mods_ready, 1)
                if FULL[m]:
                    dve.wait_ge(pre_psum, pre_done(m, 3))
                    dve.wait_ge(gate_bias_loaded, 64 * (FULL_BEFORE[m] + 1))
                    for g in range(2):
                        last = nc.vector.tensor_tensor(gate_sb[0:nb, 2 * g, :], o_acc["F"][0:nb, g * D:(g + 1) * D],
                                                       bias_rows[0:nb, 2 * g, :], ALU.add)
                    last.then_inc(gate_ready, 1)
                    dve.wait_ge(gate_ready, FULL_BEFORE[m] + 1)
                    for g in range(2):
                        last = nc.vector.tensor_tensor(gate_sb[0:nb, 2 * g + 1, :], gate_sb[0:nb, 2 * g, :],
                                                       bias_rows[0:nb, 2 * g + 1, :], ALU.mult)
                    last.then_inc(gate_times_bias, 1)

            def norm(r, m, step, n):
                if step == "C":
                    dve.wait_ge(context_loaded[r].sem, context_loaded[r].after(m, "ld", n))
                    tiles = [(context[r][0:S, :], context_hat[r][0:S, :])]
                    st, mv, ve, rs = (c_stats[r][0:S, :].unsqueeze(1), c_mean_var[r][0:S, :].unsqueeze(1),
                                      c_var_eps[r][0:S, :], c_rstd[r][0:S, :])
                else:
                    x_src = x_mid if FULL[m] and r == "G" and step == "LN" else x[r]
                    tiles = [(x_src[:, t, :], x_hat[r][:, t, :]) for t in range(TT)]
                    st, mv, ve, rs = stats[r][:, :, :], mean_var[r][:, :, :], var_eps[r][:, :], rstd[r][:, :]
                    if step == "LN3":
                        dve.wait_ge(x_cross_ready[r].sem, x_cross_ready[r].after(m, "PR", n))
                    elif FULL[m] and r == "G":
                        dve.wait_ge(x_mid_ready["F"].sem, x_mid_ready["F"].after(m, "PR", n))
                    else:
                        dve.wait_ge(x_loaded[r].sem, x_loaded[r].after(m, "ld", n))
                for t, (src, _) in enumerate(tiles):
                    last = nc.vector.bn_stats(st[:, t, :], src)
                last.then_inc(stats_ready[r].sem, 1)
                dve.wait_ge(stats_ready[r].sem, stats_ready[r].after(m, step, n))
                nc.vector.memset(wait_mark[:, :], 0.0)
                for t in range(len(tiles)):
                    last = nc.vector.bn_aggr(mv[:, t, :], st[:, t, :])
                last.then_inc(mean_ready[r].sem, 1)
                dve.wait_ge(mean_ready[r].sem, mean_ready[r].after(m, step, n))
                nc.vector.tensor_scalar(ve, mv[:, :, 1], EPS[m], None, ALU.add).then_inc(var_ready[r].sem, 1)
                dve.wait_ge(rstd_ready[r].sem, rstd_ready[r].after(m, step, n))
                for t, (src, dst) in enumerate(tiles):
                    last = nc.vector.tensor_scalar(dst, src, mv[:, t, 0:1], rs[:, t:t + 1], ALU.subtract, ALU.mult)
                last.then_inc(x_hat_ready[r].sem, 1)

            def low_parts(r, m, step, n, here):
                dve.wait_ge(hi_ready[r].sem, hi_ready[r].after(m, step, n))
                for src, bias, tile, c in parts_of(r, m, step, here):
                    last = nc.vector.scalar_tensor_tensor(out=tile[:, 1, c, :].bitcast(F32R), in0=src, scalar=bias,
                                                          in1=tile[:, 0, c, :], op0=ALU.add, op1=ALU.subtract)
                last.then_inc(lo_ready[r].sem, 1)

            def handler(r, m, step, n, looping, here):
                if step == "ld":
                    if not looping:
                        dve.wait_ge(mods_ready, m + 1)
                    x_t_ready[r].wait_before(dve, m, n)
                    context_t_ready[r].wait_before(dve, m, n)
                    b = n if FULL[m] else 2 * n + (r == "G")
                    nc.vector.tensor_copy(mod_now[r][:, :], mods[m % 2][:, bass.ds(b, 1), :].rearrange("p o c -> p (o c)"))\
                        .then_inc(mod_ready[r].sem, 1)
                elif step in ("LN", "LN3") or (step == "C" and CTX_LN[m]):
                    norm(r, m, step, n)
                elif step in ("QK", "Q"):
                    low_parts(r, m, step, n, here)
                elif step == "KV":
                    low_parts(r, m, step, n, here)
                    if not looping:
                        dve.wait_ge(bias_spread, spread_done(m))
                    nc.vector.tensor_tensor(v_ctx[r][0:S, :, 0:HD],
                                            slot[here][0:S, BANK:BANK + D].rearrange("p (h d) -> p h d", d=HD),
                                            vc_bias[m % 2][0:S, :].rearrange("p (h d) -> p h d", d=HD), ALU.add)\
                        .then_inc(v_ready[r].sem, 1)
                elif step == "V":
                    dve.wait_ge(psum_ready[r].sem, psum_ready[r].after(m, step, n))
                    if not looping:
                        dve.wait_ge(bias_spread, spread_done(m))
                    for t in range(TT):
                        last = nc.vector.tensor_tensor(v_self[:, t, :, 0:HD],
                                                       slot[here][:, t * D:(t + 1) * D].rearrange("p (h d) -> p h d", d=HD),
                                                       v_bias[m % 2][:, :].rearrange("p (h d) -> p h d", d=HD), ALU.add)
                    last.then_inc(v_ready[r].sem, 1)
                elif step[0] == "S" and step[1:].isdigit():
                    u = int(step[1])
                    dve.wait_ge(psum_ready[r].sem, psum_ready[r].after(m, step, n))
                    if is_self(m, r):
                        heads, t = QUAD * (u // 2), u % 2
                        src = slot[here][:, :].rearrange("p (h k) -> p h k", h=QUAD)
                        dst = row_max[r][:, t, heads:heads + QUAD]
                    else:
                        heads, t = 2 * QUAD * (u // 2), u % 2
                        src = slot[here][:, :].rearrange("p (b w) -> p b w", b=2)[:, :, 0:QUAD * S]\
                            .rearrange("p b (h k) -> p b h k", h=QUAD)
                        dst = row_max[r][:, t, heads:heads + 2 * QUAD].rearrange("p (b h) -> p b h", b=2)
                    nc.vector.tensor_reduce(dst, src, AX.X, ALU.max).then_inc(row_max_ready[r].sem, 1)
                elif step in ("M0", "M1"):
                    h = int(step[1])
                    need = {True: ("S3", "S7"), False: ("S1", "S3")}[is_self(m, r)][h]
                    src = row_max[r][:, :, 8 * h:8 * h + 8]
                    hi, lo = max_parts[r][:, :, h, 0, :], max_parts[r][:, :, h, 1, :]
                    dve.wait_ge(row_max_ready[r].sem, row_max_ready[r].after(m, need, n))
                    nc.vector.tensor_scalar(hi.bitcast(F32R), src, -1.0, None, ALU.mult)\
                        .then_inc(max_hi_ready[r].sem, 1)
                    dve.wait_ge(max_hi_ready[r].sem, max_hi_ready[r].after(m, step, n))
                    nc.vector.scalar_tensor_tensor(out=lo.bitcast(F32R), in0=src, scalar=-1.0, in1=hi,
                                                   op0=ALU.mult, op1=ALU.subtract).then_inc(max_parts_ready[r].sem, 1)
                elif step == "O1":
                    dve.wait_ge(psum_ready[r].sem, psum_ready[r].after(m, step, n))
                    o = slot[here][:, :].rearrange("p (t j k) -> p t j k", t=TT, j=H)
                    nc.vector.reciprocal(r_den[r][:, :, :], o[:, :, :, HD]).then_inc(r_den_ready[r].sem, 1)
                    dve.wait_ge(r_den_ready[r].sem, r_den_ready[r].after(m, step, n))
                    for t in range(TT):
                        last = nc.vector.tensor_tensor(
                            o_norm[r][:, t, :].rearrange("p (e i d) -> p i e d", e=2, i=H // 2),
                            o[:, t, :, 0:HD].rearrange("p (i e) d -> p i e d", e=2),
                            r_den[r][:, t, :].rearrange("p (i e) -> p i e", e=2).unsqueeze(3)
                            .to_broadcast([P, H // 2, 2, HD]), ALU.mult)
                    last.then_inc(o_norm_ready[r].sem, 1)
                elif step == "PR":
                    dve.wait_ge(psum_ready[r].sem, psum_ready[r].after(m, step, n))
                    src = slot[here][:, 0:TT * D].rearrange("p (t d) -> p t d", t=TT)
                    if FULL[m] and r == "F":
                        dve.wait_ge(gate_loaded[r].sem, gate_loaded[r].after(m, "ld", n))
                        nc.vector.tensor_tensor(gated[r][:, :, :], src, gate_now[r][:, 0:1, :].to_broadcast([P, TT, D]),
                                                ALU.mult).then_inc(gated_ready[r].sem, 1)
                    else:
                        dve.wait_ge(x_biased[r].sem, x_biased[r].after(m, "LN", n))
                        if FULL[m]:
                            nc.vector.tensor_tensor(x[r][:, :, :], src, x[r][:, :, :], ALU.add)\
                                .then_inc(x_cross_ready[r].sem, 1)
                        else:
                            x_stored[r].wait_before(dve, m, n)
                            if r == "F":
                                x_biased["G"].wait_before(dve, m, 0)
                            nc.vector.tensor_tensor(x_new[r][:, :, :], src, x[r][:, :, :], ALU.add)\
                                .then_inc(x_new_ready[r].sem, 1)
                elif step == "F2":
                    dve.wait_ge(psum_ready[r].sem, psum_ready[r].after(m, step, n))
                    dve.wait_ge(gate_loaded[r].sem, gate_loaded[r].after(m, "ld", n))
                    x_new_ready[r].wait_before(dve, m, n)
                    nc.vector.tensor_tensor(gated[r][:, :, :],
                                            slot[here][:, 0:TT * D].rearrange("p (t d) -> p t d", t=TT),
                                            gate_now[r][:, 0:1, :].to_broadcast([P, TT, D]), ALU.mult)\
                        .then_inc(gated_ready[r].sem, 1)

            walk(dve, program, handler, pre)

        @block.scalar
        def _(act):
            def pre(m):
                if m == 0:
                    act.wait_ge(cond_loaded, 16)
                    nc.scalar.activation(cond_e[:, :], cond[:, :], ACT.Exp, scale=-1.0).then_inc(silu_exp, 1)

            def handler(r, m, step, n, looping, here):
                if step not in ("ld", "ST") and here is not None:
                    ps = slot[here]
                if step in ("LN", "LN3"):
                    act.wait_ge(psum_ready[r].sem, psum_ready[r].after(m, step, n))
                    plain = FULL[m] and r == "G" and step == "LN"
                    if not plain:
                        act.wait_ge(mod_ready[r].sem, mod_ready[r].after(m, "ld", n))
                    elif m == 2 and not looping:
                        act.wait_ge(cols_ready, m + 1)
                    at = 4 if step == "LN3" else 0
                    for c in range(KC):
                        if not plain:
                            bias, scale = mod_now[r][:, at + 2 + c:at + 3 + c], mod_now[r][:, at + c:at + c + 1]
                        elif m == 2:
                            bias, scale = col(m, "beta", c), col(m, "gamma", c)
                        else:
                            bias, scale = 0.0, 1.0
                        last = nc.scalar.activation(x_t[r][:, c, :], ps[:, c * NT:(c + 1) * NT], ACT.Identity,
                                                    bias=bias, scale=scale)
                    last.then_inc(x_t_ready[r].sem, 1)
                elif step == "C":
                    act.wait_ge(psum_ready[r].sem, psum_ready[r].after(m, step, n))
                    if FULL[m]:
                        nc.scalar.activation(context_t[r][:, :, :],
                                             ps[:, 0:KC * S].rearrange("p (c s) -> p c s", c=KC), ACT.Identity)\
                            .then_inc(context_t_ready[r].sem, 1)
                    else:
                        act.wait_ge(mod_ready[r].sem, mod_ready[r].after(m, "ld", n))
                        for c in range(KC):
                            last = nc.scalar.activation(context_t[r][:, c, :], ps[:, c * S:(c + 1) * S],
                                                        ACT.Identity, bias=mod_now[r][:, 6 + c:7 + c],
                                                        scale=mod_now[r][:, 4 + c:5 + c])
                        last.then_inc(context_t_ready[r].sem, 1)
                elif step in ("QK", "Q", "KV"):
                    act.wait_ge(psum_ready[r].sem, psum_ready[r].after(m, step, n))
                    if not looping:
                        act.wait_ge(cols_ready, m + 1)
                    if step in ("QK", "Q"):
                        q_stored[r].wait_before(act, m, n)
                    if step in ("QK", "KV"):
                        k_stored[r].wait_before(act, m, n)
                    for src, bias, tile, c in parts_of(r, m, step, here):
                        last = nc.scalar.activation(tile[:, 0, c, :].bitcast(F32R), src, ACT.Identity, bias=bias)
                    last.then_inc(hi_ready[r].sem, 1)
                elif step in ("M0", "M1"):
                    act.wait_ge(psum_ready[r].sem, psum_ready[r].after(m, step, n))
                    nc.scalar.activation(max_t[r][int(step[1])][:, :], ps[0:H, 0:NT], ACT.Identity)\
                        .then_inc(max_t_ready[r].sem, 1)
                elif step[0] == "T":
                    v = int(step[1:])
                    keys = P if is_self(m, r) else S
                    act.wait_ge(psum_ready[r].sem, psum_ready[r].after(m, step, n))
                    if not looping and is_self(m, r):
                        act.wait_ge(gate_stored, 16 * (FULL_BEFORE[m] + 1))
                    nc.scalar.activation(probs[r][v % 2][0:keys, :, :],
                                         ps[0:keys, :].rearrange("p (g q) -> p g q", g=QUAD), ACT.Exp, scale=SCALE)\
                        .then_inc(probs_ready[r].sem, 1)
                elif step in out_banks(m, r):
                    act.wait_ge(psum_ready[r].sem, psum_ready[r].after(m, step, n))
                    i = out_banks(m, r).index(step)
                    nc.scalar.activation(o_raw[r][:, 2 * i:2 * i + 2, :],
                                         o_acc[r][:, :].rearrange("p (i q) -> p i q", i=2), ACT.Identity)\
                        .then_inc(o_raw_ready[r].sem, 1)
                elif step == "O2":
                    act.wait_ge(psum_ready[r].sem, psum_ready[r].after(m, step, n))
                    nc.scalar.activation(o_t[r][:, :, :], ps[:, 0:KC * NT].rearrange("p (k q) -> p k q", k=KC),
                                         ACT.Identity).then_inc(o_t_ready[r].sem, 1)
                elif step in ("H0", "H1"):
                    act.wait_ge(psum_ready[r].sem, psum_ready[r].after(m, step, n))
                    for i in range(4):
                        c = 4 * int(step[1]) + i
                        last = nc.scalar.activation(h_t[:, c, :], ps[:, i * NT:(i + 1) * NT], ACT.Gelu_apprx_tanh,
                                                    bias=col(m, "fc1", c))
                    last.then_inc(h_ready[r].sem, 1)

            walk(act, program, handler, pre)

        @block.tensor
        def _(pe):
            mm = nc.tensor.matmul

            def transpose(dst, src, rows_in):
                return nc.tensor.transpose(dst, src, ident[0:rows_in, 0:rows_in])

            def release(r, m, step, n=None, before=False):
                if step in ("LN", "LN3"):
                    s = x_t_ready
                elif step == "C":
                    s = context_t_ready
                elif step in ("QK", "Q"):
                    s = lo_ready
                elif step in ("V", "KV"):
                    s = v_ready
                elif step[0] == "S":
                    s = row_max_ready
                elif step[0] == "M":
                    s = max_t_ready
                elif step[0] == "T":
                    s = probs_ready
                elif step == "O1":
                    s = o_norm_ready
                elif step == "O2":
                    s = o_t_ready
                elif step[0] == "H":
                    s = h_ready
                elif step == "F2" or (step == "PR" and is_self(m, r)):
                    s = gated_ready
                else:
                    s = x_cross_ready if FULL[m] else x_new_ready
                if before:
                    s[r].wait_before(pe, m, n)
                else:
                    pe.wait_ge(s[r].sem, s[r].after(m, step, n))

            last_user = {}

            def pre(m):
                pre_bank = o_acc["F"]
                if m == 0:
                    pe.wait_ge(ident_ready, 1)
                    pe.wait_ge(silu_step, 3)
                    for k in range(KC):
                        last = transpose(pre_bank[:, k * nb:(k + 1) * nb], cond[0:nb, k * P:(k + 1) * P], nb)
                    last.then_inc(silu_psum, 1)
                    pe.wait_ge(silu_step, 4)
                else:
                    end = out_banks(m - 1, "F")[-1]
                    pe.wait_ge(o_raw_ready["F"].sem,
                               o_raw_ready["F"].after(m - 1, end, (nb if FULL[m - 1] else nb // 2) - 1))
                pe.wait_ge(rows_loaded, rows_done(m))
                transpose(pre_bank[:, 0:n_rows(m)], rows[0:n_rows(m), :], n_rows(m)).then_inc(pre_psum, 1)
                pe.wait_ge(ada_loaded, ada_done(m))
                pe.wait_ge(cols_ready, m + 1)
                for j, src in enumerate(mod_sources(m)):
                    for k in range(KC):
                        last = mm(pre_bank[:, 64 + nb * j:64 + nb * (j + 1)], w_ada[:, k, src:src + P],
                                  silu_t[:, k, :], start=k == 0, stop=k == KC - 1)
                last.then_inc(pre_psum, 1)
                if FULL[m]:
                    pe.wait_ge(mods_ready, m + 1)
                    for g, at in enumerate((2 * D, 5 * D)):
                        for k in range(KC):
                            last = mm(pre_bank[0:nb, g * D:(g + 1) * D], silu_t[:, k, :],
                                      w_ada[:, k, at:at + D], start=k == 0, stop=k == KC - 1)
                    last.then_inc(pre_psum, 1)

            def weights_wait(r, m, looping):
                if looping:
                    return
                if r == "F" or not FULL[m]:
                    pe.wait_ge(wf_loaded, wf_done(m))
                else:
                    pe.wait_ge(wg_loaded, 80 * (FULL_BEFORE[m] + 1))

            def handler(r, m, step, n, looping, here):
                if step in ("ld", "ST"):
                    return
                if here is not None:
                    user = last_user.get(here)
                    if user == "last iteration":
                        ur, um, ustep, udn = loop_last[here]
                        release(ur, um, ustep, n - loop_dn[(r, m, step)] + udn, before=True)
                    elif user:
                        release(*user)
                    last_user[here] = (r, m, step, n)
                    ps = slot[here]
                if step in ("LN", "LN3"):
                    pe.wait_ge(x_hat_ready[r].sem, x_hat_ready[r].after(m, step, n))
                    for k in range(KC):
                        for t in range(TT):
                            last = transpose(ps[:, k * NT + t * P:k * NT + (t + 1) * P],
                                             x_hat[r][:, t, k * P:(k + 1) * P], P)
                elif step == "C":
                    if CTX_LN[m]:
                        pe.wait_ge(x_hat_ready[r].sem, x_hat_ready[r].after(m, step, n))
                    else:
                        pe.wait_ge(context_loaded[r].sem, context_loaded[r].after(m, "ld", n))
                    src = (context_hat if CTX_LN[m] else context)[r]
                    for k in range(KC):
                        last = transpose(ps[:, k * S:(k + 1) * S], src[0:S, k * P:(k + 1) * P], S)
                elif step in ("QK", "Q"):
                    weights_wait(r, m, looping)
                    pe.wait_ge(x_t_ready[r].sem, x_t_ready[r].after(m, "LN", n))
                    weight = w_q2 if FULL[m] and r == "G" else w_qkv
                    for c in range(4 if step == "QK" else 2):
                        for k in range(KC):
                            last = mm(ps[:, c * NT:(c + 1) * NT], weight[:, k, c * P:(c + 1) * P], x_t[r][:, k, :],
                                      start=k == 0, stop=k == KC - 1)
                elif step == "V":
                    for t in range(TT):
                        for k in range(KC):
                            last = mm(ps[:, t * D:(t + 1) * D], x_t[r][:, k, t * P:(t + 1) * P],
                                      w_qkv[:, k, 2 * D:3 * D], start=k == 0, stop=k == KC - 1)
                elif step == "KV":
                    weights_wait(r, m, looping)
                    pe.wait_ge(context_t_ready[r].sem, context_t_ready[r].after(m, "C", n))
                    weight, at = (w_kv2, 0) if FULL[m] else (w_qkv, D)
                    for c in range(KC):
                        for k in range(KC):
                            mm(ps[:, c * S:(c + 1) * S], weight[:, k, at + c * P:at + (c + 1) * P],
                               context_t[r][:, k, :], start=k == 0, stop=k == KC - 1)
                    for k in range(KC):
                        last = mm(ps[0:S, BANK:BANK + D], context_t[r][:, k, :], weight[:, k, at + D:at + 2 * D],
                                  start=k == 0, stop=k == KC - 1)
                elif step[0] == "S":
                    u = int(step[1:])
                    t = u % 2
                    if step == "S0":
                        qk = ("QK", "QK") if is_self(m, r) else ("Q", "KV")
                        pe.wait_ge(q_stack_loaded[r].sem, q_stack_loaded[r].after(m, qk[0], n))
                        pe.wait_ge(k_stack_loaded[r].sem, k_stack_loaded[r].after(m, qk[1], n))
                        if not looping:
                            pe.wait_ge(const_ready, CONSTS)
                    heads, width = (QUAD, NT) if is_self(m, r) else (2 * QUAD, S)
                    for i in range(heads):
                        j = heads * (u // 2) + i
                        at = i * width if is_self(m, r) else i // QUAD * BANK + i % QUAD * S
                        last = mm(ps[:, at:at + width], q_stack[r][0:MAX_ROW, j, t * P:(t + 1) * P].bitcast(F32R),
                                  k_stack[r][0:MAX_ROW, j * width:(j + 1) * width].bitcast(F32R),
                                  start=True, stop=True)
                elif step[0] == "M":
                    h = int(step[1:])
                    pe.wait_ge(max_parts_ready[r].sem, max_parts_ready[r].after(m, step, n))
                    for t in range(TT):
                        last = transpose(ps[0:H, t * P:(t + 1) * P],
                                         max_parts[r][:, t, h, :, :].rearrange("p e h -> p (e h)"), P)
                elif step[0] == "T":
                    v = int(step[1:])
                    quad, c, keys, width = (v // 2, v % 2, P, NT) if is_self(m, r) else (v, 0, S, S)
                    half = quad // 2
                    if quad % 2 == 0 and c == 0:
                        sem = max_row_loaded[half][r]
                        pe.wait_ge(sem.sem, sem.after(m, f"M{half}", n))
                    for g in range(QUAD):
                        j = QUAD * quad + g
                        last = mm(ps[0:keys, g * NT:(g + 1) * NT],
                                  k_stack[r][0:STACK_ROWS, j * width + c * P:j * width + c * P + keys].bitcast(F32R),
                                  q_stack[r][0:STACK_ROWS, j, :].bitcast(F32R), start=True, stop=True)
                elif step[:2] == "PV":
                    v = int(step[2:])
                    quad, c, keys = (v // 2, v % 2, P) if is_self(m, r) else (v, 0, S)
                    ends = out_banks(m, r)
                    if v == 0:
                        o_raw_ready[r].wait_before(pe, m, n)
                        kv = "V" if is_self(m, r) else "KV"
                        pe.wait_ge(v_ready[r].sem, v_ready[r].after(m, kv, n))
                    elif quad == 2 and c == 0:
                        pe.wait_ge(o_raw_ready[r].sem, o_raw_ready[r].after(m, ends[0], n))
                    pe.wait_ge(probs_ready[r].sem, probs_ready[r].after(m, f"T{v}", n))
                    for g in range(QUAD):
                        head = head_of(QUAD * quad + g)
                        v_head = v_self[:, c, head, :] if is_self(m, r) else v_ctx[r][0:S, head, :]
                        at = quad % 2 * NT
                        last = mm(o_acc[r][g * 2 * HD:(g + 1) * 2 * HD, at:at + NT], v_head,
                                  probs[r][v % 2][0:keys, g, :], start=c == 0, stop=c == 1 or not is_self(m, r))
                elif step == "O1":
                    pe.wait_ge(o_raw_ready[r].sem, o_raw_ready[r].after(m, out_banks(m, r)[1], n))
                    for t in range(TT):
                        for quad in range(H // QUAD):
                            last = transpose(ps[:, t * BANK + quad * P:t * BANK + (quad + 1) * P],
                                             o_raw[r][:, quad, t * P:(t + 1) * P], P)
                elif step == "O2":
                    pe.wait_ge(o_norm_ready[r].sem, o_norm_ready[r].after(m, "O1", n))
                    for k in range(KC):
                        for t in range(TT):
                            last = transpose(ps[:, k * NT + t * P:k * NT + (t + 1) * P],
                                             o_norm[r][:, t, k * P:(k + 1) * P], P)
                elif step == "PR":
                    pe.wait_ge(o_t_ready[r].sem, o_t_ready[r].after(m, "O2", n))
                    weight = w_cp if FULL[m] and r == "G" else w_proj[m % 2]
                    for t in range(TT):
                        for k in range(KC):
                            last = mm(ps[:, t * D:(t + 1) * D], o_t[r][:, k, t * P:(t + 1) * P], weight[:, k, :],
                                      start=k == 0, stop=k == KC - 1)
                elif step[0] == "H":
                    pe.wait_ge(x_t_ready[r].sem, x_t_ready[r].after(m, "LN3", n))
                    for i in range(4):
                        c = 4 * int(step[1:]) + i
                        for k in range(KC):
                            last = mm(ps[:, i * NT:(i + 1) * NT], w_fc1[:, k, c * P:(c + 1) * P], x_t[r][:, k, :],
                                      start=k == 0, stop=k == KC - 1)
                elif step == "F2":
                    pe.wait_ge(h_ready[r].sem, h_ready[r].after(m, "H1", n))
                    for t in range(TT):
                        for k in range(MC):
                            last = mm(ps[:, t * D:(t + 1) * D], h_t[:, k, t * P:(t + 1) * P], w_fc2[:, k, :],
                                      start=k == 0, stop=k == MC - 1)
                last.then_inc(psum_ready[r].sem, 1)

            loop_last, loop_dn = {}, {}
            for seg in program:
                if seg[0] == "loop" and seg[1] > 0:
                    for s in sorted(last_user):
                        release(*last_user[s])
                    place = places(seg[2])
                    loop_last.clear()
                    loop_dn.clear()
                    for r, m, step, dn in seg[2]:
                        if (r, m, step) in place:
                            loop_last[place[(r, m, step)]] = (r, m, step, dn)
                            loop_dn[(r, m, step)] = dn
                    for s in range(SLOTS):
                        last_user[s] = "last iteration"
                    walk(pe, [seg], handler)
                    for s in range(SLOTS):
                        r, m, step, dn = loop_last[s]
                        last_user[s] = (r, m, step, seg[1] - 1 + dn)
                else:
                    walk(pe, [seg], handler, pre)

    return nc


_OUTS = [((16, 256, 256), 'float32')]


def kernel(**inputs):
    import numpy as _np
    import concourse.bacc as _bacc
    from concourse import mybir as _mybir
    from concourse.bass_utils import run_bass_kernel_spmd as _run

    nc = _bacc.Bacc("TRN2", target_bir_lowering=False, num_devices=1)
    arrays, aps = {}, {}
    for name, value in inputs.items():
        a = _np.ascontiguousarray(value)
        arrays[f"in_{name}_dram"] = a
        aps[name] = nc.dram_tensor(f"in_{name}_dram", a.shape, _mybir.dt.from_np(a.dtype), kind="ExternalInput").ap()
    out = nc.dram_tensor("out_0_dram", _OUTS[0][0], _mybir.dt.from_np(_np.dtype(_OUTS[0][1])),
                         kind="ExternalOutput").ap()
    build_program(nc, aps, out)
    r = _run(nc, [arrays], core_ids=[0])
    return r.results[0]["out_0_dram"]
```

```python
from contextlib import ExitStack

import numpy as np

import concourse.bass as bass
from concourse import mybir

F32 = mybir.dt.float32
F32R = mybir.dt.float32r
ALU = mybir.AluOpType
ACT = mybir.ActivationFunctionType
AX = mybir.AxisListType

P = 128
D = 256
KC = D // P
H = 16
HD = D // H
NT = 256
TT = NT // P
S = 120
MLP = 4 * D
MC = MLP // P
QUAD = 4
SLOT = 1024
BANK = 512
SLOTS = 3
SCALE = HD ** -0.5
LO_ROW = 64
MAX_ROW = 96
STACK_ROWS = MAX_ROW + 2

FULL = (True, False, True, True)
EPS = (1e-6, 1e-5, 1e-6, 1e-6)
CTX_LN = (False, True, False, True)
LAYERS = 4


def head_of(j):
    return (j % 2) * (H // 2) + j // 2


OFF_PE = ("ld", "N", "NC", "ST")


def role_steps(layer, role):
    if not FULL[layer]:
        return [] if role == "E" else [w[2:] for who in "YX" for w in HALF if w[0] == who]
    words = [word.split(".") for word in BODY]
    return [step for who in (role + "+", role) for r, step in words if r == who and step not in OFF_PE]


COST = {"LN": 0.4, "QK": 3.5, "V": 1.8, "C": 0.2, "KV": 2.0, "Q": 1.8, "S": 0.45, "M": 0.1, "T": 0.45,
        "PV": 0.55, "O1": 0.9, "O2": 0.4, "PR": 1.8, "H": 3.5, "F20": 3.5, "F21": 3.5, "ld": 0.0, "ST": 0.0, "N": 0.0,
        "NC": 0.0}


def cost(step):
    return COST[step] if step in COST else COST[step.rstrip("01234567")]


def merge(a, b):
    total = [sum(cost(e[2]) for e in x) or 1 for x in (a, b)]
    at = [0.0, 0.0]
    out, i, j = [], 0, 0
    while i < len(a) or j < len(b):
        if j >= len(b) or (i < len(a) and at[0] / total[0] <= at[1] / total[1]):
            out.append(a[i])
            at[0] += cost(a[i][2])
            i += 1
        else:
            out.append(b[j])
            at[1] += cost(b[j][2])
            j += 1
    return out


BODY = """
G+.ld F.S0 G.T0 F.S1 G.T1 G.PV0 F.S2 G.T2 G.PV1 F.S3 G.T3 G.PV2 F.S4 G.PV3 F.M0 F.S5 F.S6 G.O1 F.T0 E.ld F.S7
G.O2 F.T1 F.PV0 F.T2 G.PR F.PV1 F.M1
E.N G+.N G+.NC F.T3 F.PV2 F.T4 F.PV3 G+.C F.T5 F.PV4 F+.ld F+.N G+.KV E.LN F.T6 F.PV5 G+.LN F.T7
F.PV6 G+.Q F.PV7 E.H0 F.O1 E.H1 F.O2 G+.S0 F.PR
F+.LN G+.S1 F+.QK E.F20 F+.V G+.S2 G+.S3 G+.M0 E.F21 E.ST G+.M1
""".split()
AHEAD = {"F+": 3, "F": 2, "G+": 1, "G": 0, "E": 0}

HALF = """
Y.C Y.LN X.M0 X.M1 Y.Q Y.KV X.T0 X.T1 X.PV0 X.T2 X.PV1 X.T3 X.PV2 X.PV3 Y.S0 X.O1 Y.S1 X.O2 Y.S2 X.PR Y.S3
""".split()
EARLY_AT = 9


def turn(layer, i, nb):
    out = []
    for word in BODY:
        role, step = word.split(".")
        if 0 <= i + AHEAD[role] < nb:
            out.append((role[0], layer, step, i + AHEAD[role]))
    return out


def entries(role, layer, steps, n):
    return [(role, layer, s, n) for s in steps]


def segments(nb):
    pairs = nb // 2
    out = []

    def run(steps):
        out.append(("run", steps))

    def loop(count, steps):
        if count > 0:
            out.append(("loop", count, steps))

    def full_turns(layer):
        run(turn(layer, 0, nb))
        loop(nb - 4, turn(layer, 1, nb))
        run(turn(layer, nb - 3, nb))

    def early(role, n):
        return entries(role, 1, ("ld", "N", "NC"), n)

    def half(x, xn, y, yn):
        steps = []
        for at, word in enumerate(HALF):
            if at == EARLY_AT and xn is not None and xn + 1 < pairs:
                steps += early(x, xn + 1)
            who, n = (x, xn) if word[0] == "X" else (y, yn)
            if n is not None and n < pairs:
                steps.append((who, 1, word[2:], n))
        return steps + ([(x, 1, "ST", xn)] if xn is not None else [])

    out += [("pre", 0), ("weights", 0), ("mlp", 0)]
    for i in (-3, -2, -1):
        run(turn(0, i, nb))
    full_turns(0)
    out.append(("pre", 1))
    run(merge(turn(0, nb - 2, nb), early("F", 0)))
    run(merge(turn(0, nb - 1, nb), half(None, None, "F", 0)) + early("G", 0))
    out.append(("weights", 2))
    out.append(("mlp", 2))
    run(half("F", 0, "G", 0) + half("G", 0, "F", 1))
    loop(pairs - 3, half("F", 1, "G", 1) + half("G", 1, "F", 2))
    if pairs > 2:
        run(half("F", pairs - 2, "G", pairs - 2) + half("G", pairs - 2, "F", pairs - 1))
    run(half("F", pairs - 1, "G", pairs - 1))
    out.append(("pre", 2))
    run(merge(half("G", pairs - 1, None, None), turn(2, -3, nb) + turn(2, -2, nb)))
    run(turn(2, -1, nb))
    full_turns(2)
    out.append(("pre", 3))
    run(merge(turn(2, nb - 2, nb), turn(3, -3, nb) + turn(3, -2, nb)))
    out.append(("weights", 3))
    old, new = turn(2, nb - 1, nb), turn(3, -1, nb)
    i = [e[2] for e in old].index("N") + 1
    j = [(e[0], e[2]) for e in new].index(("G", "N"))
    run(merge(old[:i], new[:j]) + merge(old[i:], new[j:]))
    out.append(("mlp", 3))
    full_turns(3)
    for i in (nb - 2, nb - 1):
        run(turn(3, i, nb))
    return out


class Signal:

    def __init__(self, sem, steps, batches, by=1):
        self.sem, self.by = sem, by
        self.steps = [list(steps(layer)) for layer in range(LAYERS)]
        self.base = [0]
        for layer in range(LAYERS):
            self.base.append(self.base[-1] + by * len(self.steps[layer]) * batches[layer])

    def after(self, layer, step, n, nth=-1):
        at = [i for i, s in enumerate(self.steps[layer]) if s == step][nth]
        return n * (self.by * len(self.steps[layer])) + (self.base[layer] + self.by * (at + 1))

    def before(self, layer, n):
        if not self.steps[layer]:
            return self.base[layer]
        return n * (self.by * len(self.steps[layer])) + self.base[layer]

    def wait_before(self, eng, layer, n):
        value = self.before(layer, n)
        if not isinstance(value, int) or value > 0:
            eng.wait_ge(self.sem, value)


def numbered(name, steps):
    return [s for s in steps if s.startswith(name) and s[len(name):].isdigit()]


def places(steps):
    users = [e[:3] for e in steps if e[2] not in OFF_PE and not e[2].startswith("PV")]
    return {e: i % SLOTS for i, e in enumerate(users)}


def walk(eng, program, handler, at_pre=None, at_weights=None, at_mlp=None):
    for seg in program:
        if seg[0] == "pre":
            if at_pre:
                at_pre(seg[1])
        elif seg[0] == "weights":
            if at_weights:
                at_weights(seg[1])
        elif seg[0] == "mlp":
            if at_mlp:
                at_mlp(seg[1])
        elif seg[0] == "run":
            place = places(seg[1])
            for role, layer, step, n in seg[1]:
                handler(role, layer, step, n, False, place.get((role, layer, step)))
        elif seg[1] > 0:
            place = places(seg[2])
            with eng.Fori(0, seg[1]) as it:
                for role, layer, step, dn in seg[2]:
                    handler(role, layer, step, it + dn, True, place.get((role, layer, step)))


def build_program(nc, a, out, nb=16):
    program = segments(nb)
    ctx = ExitStack()
    with ctx:
        def sb(name, shape, dt=F32):
            return ctx.enter_context(nc.sbuf_tensor(name, shape, dt))

        def scratch(name, shape):
            return nc.dram_tensor(name, shape, F32, kind="Internal").ap()

        x_in = [a["x"]] + [scratch(f"x_after_{m}", [nb, NT, D]) for m in range(LAYERS - 1)]
        x_out = x_in[1:] + [out]
        gate_rows = [scratch(f"gate_rows_{m}", [nb, 4, D]) if FULL[m] else None for m in range(LAYERS)]
        q_parts_dram = {r: scratch(f"q_parts_{r}", [P, 2, KC * NT]) for r in "FG"}
        k_parts_dram = {r: scratch(f"k_parts_{r}", [P, 2, KC * NT]) for r in "F"}
        kc_parts_dram = {r: scratch(f"kc_parts_{r}", [P, 2, KC * S]) for r in "FG"}

        ident = sb("ident", [P, P])
        w_qkv = sb("w_qkv", [P, KC, 3 * D])
        w_proj = [sb(f"w_proj{i}", [P, KC, D]) for i in range(2)]
        w_q2 = sb("w_q2", [P, KC, D])
        w_kv2 = sb("w_kv2", [P, KC, 2 * D])
        w_cp = sb("w_cp", [P, KC, D])
        w_fc1 = sb("w_fc1", [P, KC, MLP])
        w_fc2 = sb("w_fc2", [P, MC, D])
        w_ada = sb("w_ada", [P, KC, 6 * D])
        rows = sb("rows", [36, P])
        cols = [sb(f"cols{i}", [P, 36]) for i in range(2)]
        mods = [sb(f"mods{i}", [P, nb, 8]) for i in range(2)]
        v_bias = [sb(f"v_bias{i}", [P, D]) for i in range(2)]
        vc_bias = [sb(f"vc_bias{i}", [P, D]) for i in range(2)]
        cp_bias = [sb(f"cp_bias{i}", [P, D]) for i in range(2)]
        cond = sb("cond", [nb, D])
        cond_e = sb("cond_e", [nb, D])
        silu_t = sb("silu_t", [P, KC, nb])

        x = {r: sb(f"x_{r}", [P, TT, D]) for r in "FGE"}
        x_new = {r: sb(f"x_new_{r}", [P, TT, D]) for r in "FE"}
        x_new["G"] = x_new["E"]
        x_mid = x_new["F"]
        x_stage = {"F": sb("x_stage", [P, TT, D]), "G": x["E"]}
        x_hat = {r: sb(f"x_hat_{r}", [P, TT, D]) for r in "FGE"}
        x_t = {r: sb(f"x_t_{r}", [P, KC, NT]) for r in "FGE"}
        stats = {r: sb(f"stats_{r}", [P, TT, 6]) for r in "FGE"}
        mean_var = {r: sb(f"mean_var_{r}", [P, TT, 2]) for r in "FGE"}
        var_eps = {r: sb(f"var_eps_{r}", [P, TT]) for r in "FGE"}
        rstd = {r: sb(f"rstd_{r}", [P, TT]) for r in "FGE"}
        c_stats = {r: sb(f"c_stats_{r}", [P, 6]) for r in "FG"}
        c_mean_var = {r: sb(f"c_mean_var_{r}", [P, 2]) for r in "FG"}
        c_var_eps = {r: sb(f"c_var_eps_{r}", [P, 1]) for r in "FG"}
        c_rstd = {r: sb(f"c_rstd_{r}", [P, 1]) for r in "FG"}
        wait_mark = sb("wait_mark", [1, 1])
        minus_half = sb("minus_half", [P, TT])
        mod_now = {r: sb(f"mod_now_{r}", [P, 8]) for r in "FGE"}
        gate_now = {r: sb(f"gate_now_{r}", [P, 2, D]) for r in "FE"}
        gated = {r: sb(f"gated_{r}", [P, TT, D]) for r in "FE"}
        context = {r: sb(f"context_{r}", [P, D]) for r in "FG"}
        context_hat = {r: sb(f"context_hat_{r}", [P, D]) for r in "FG"}
        context_t = {r: sb(f"context_t_{r}", [P, KC, S]) for r in "FG"}
        q_parts = {r: sb(f"q_parts_sb_{r}", [P, 2, KC, NT]) for r in "FG"}
        k_parts = sb("k_parts_sb", [P, 2, KC, NT])
        kc_parts = {r: sb(f"kc_parts_sb_{r}", [P, 2, KC, S]) for r in "FG"}
        q_stack = {r: sb(f"q_stack_{r}", [P, H, NT]) for r in "FG"}
        k_stack = {"F": sb("k_stack_F", [P, H * NT]), "G": sb("k_stack_G", [P, H * S])}
        v_self = sb("v_self", [P, TT, H, 2 * HD])
        v_ctx = {r: sb(f"v_ctx_{r}", [P, H, 2 * HD]) for r in "FG"}
        row_max = {r: sb(f"row_max_{r}", [P, TT, H]) for r in "FG"}
        max_parts = {r: sb(f"max_parts_{r}", [P, TT, 2, 2, H // 2]) for r in "FG"}
        max_t = {r: [sb(f"max_t_{r}{h}", [H, NT]) for h in range(2)] for r in "FG"}
        probs = {r: [sb(f"probs_{r}{i}", [P, QUAD, NT]) for i in range(2)] for r in "FG"}
        o_raw = {r: q_parts[r][:, :, :, :].rearrange("p e m w -> p (e m) w") for r in "FG"}
        r_den = {r: sb(f"r_den_{r}", [P, TT, H]) for r in "FG"}
        o_norm = {"F": sb("o_norm_F", [P, TT, D]), "G": x_hat["G"]}
        o_t = x_t
        h_t = sb("h_t", [P, MC, NT])
        bias_rows = probs["F"][0]
        gate_sb = probs["F"][1]

        slot = [ctx.enter_context(nc.psum_tensor(f"slot{i}", [P, SLOT], F32)) for i in range(SLOTS)]
        o_acc = {r: ctx.enter_context(nc.psum_tensor(f"o_acc_{r}", [P, BANK], F32)) for r in "FG"}

        def batches(role):
            return [(nb if FULL[m] else nb // 2) for m in range(LAYERS)]

        def signal(name, steps, by=1):
            made = {}
            for r in "FGE":
                used = any(steps(m, r) for m in range(LAYERS))
                made[r] = Signal(ctx.enter_context(nc.semaphore(f"{name}_{r}")) if used else None,
                                 lambda m, r=r: steps(m, r), batches(r), by)
            return made

        def only(*names):
            return lambda m, r: [s for s in role_steps(m, r) if s in names]

        def norms(m, r):
            if not FULL[m]:
                return [] if r == "E" else ["N", "NC"]
            return ["N", "NC"] if r == "G" and CTX_LN[m] else ["N"]

        def loads_x(m, r):
            return r == "F" or (r == "G" and not FULL[m])

        def out_banks(m, r):
            if r == "E":
                return []
            return ["PV3", "PV7"] if FULL[m] and r == "F" else ["PV1", "PV3"]

        psum_ready = signal("psum_ready", lambda m, r: role_steps(m, r))
        x_t_ready = signal("x_t_ready", only("LN"))
        context_t_ready = signal("context_t_ready", only("C"))
        hi_ready = signal("hi_ready", only("QK", "Q", "KV"))
        max_t_ready = signal("max_t_ready", lambda m, r: numbered("M", role_steps(m, r)))
        probs_ready = signal("probs_ready", lambda m, r: numbered("T", role_steps(m, r)))
        o_raw_ready = signal("o_raw_ready", out_banks)
        o_t_ready = signal("o_t_ready", only("O2"))
        h_ready = signal("h_ready", only("H0", "H1"))
        mod_ready = signal("mod_ready", lambda m, r: [] if r == ("G" if FULL[m] else "E") else ["ld"])
        stats_ready = signal("stats_ready", norms)
        mean_ready = signal("mean_ready", norms)
        var_ready = signal("var_ready", norms)
        x_hat_ready = signal("x_hat_ready", norms)
        lo_ready = signal("lo_ready", only("QK", "Q", "KV"))
        v_ready = signal("v_ready", only("V", "KV"))
        row_max_ready = signal("row_max_ready", lambda m, r: numbered("S", role_steps(m, r)))
        max_hi_ready = signal("max_hi_ready", lambda m, r: numbered("M", role_steps(m, r)))
        max_parts_ready = signal("max_parts_ready", lambda m, r: numbered("M", role_steps(m, r)))
        r_den_ready = signal("r_den_ready", only("O1"))
        o_norm_ready = signal("o_norm_ready", only("O1"))
        gated_ready = signal("gated_ready", lambda m, r: {"F": ["PR"], "G": [], "E": ["F20", "F21"]}[r] if FULL[m] else [])
        x_cross_ready = signal("x_cross_ready", lambda m, r: ["PR"] if FULL[m] and r == "G" else [])
        rstd_ready = signal("rstd_ready", norms)
        x_biased = signal("x_biased", lambda m, r: [s for s in norms(m, r) if s == "N"])
        x_mid_ready = signal("x_mid_ready", lambda m, r: ["PR"] if FULL[m] and r == "F" else [])
        x_new_ready = signal("x_new_ready", lambda m, r: (["F21"] if r == "E" else []) if FULL[m] else
                             ([] if r == "E" else ["PR"]))
        x_loaded = signal("x_loaded", lambda m, r: ["ld"] if loads_x(m, r) else [], 16)
        gate_step = {"F": "LN", "E": "ld"}
        gate_loaded = signal("gate_loaded", lambda m, r: [gate_step[r]] if FULL[m] and r in gate_step else [], 16)
        context_loaded = signal("context_loaded", lambda m, r: ["ld"] if r == "G" or (r == "F" and not FULL[m]) else [], 16)
        q_stored = signal("q_stored", only("QK", "Q"), 16)
        k_stored = signal("k_stored", only("QK", "KV"), 16)
        q_stack_loaded = signal("q_stack_loaded", only("QK", "Q"), 48)
        k_stack_loaded = signal("k_stack_loaded", only("QK", "KV"), 48)
        max_row_loaded = [signal(f"max_row_loaded{h}", only(f"M{h}"), 16) for h in range(2)]
        x_stored = signal("x_stored", lambda m, r: ["ST"] if (r == "E") == FULL[m] else [], 16)

        cond_loaded = ctx.enter_context(nc.semaphore("cond_loaded"))
        silu_step = ctx.enter_context(nc.semaphore("silu_step"))
        silu_exp = ctx.enter_context(nc.semaphore("silu_exp"))
        silu_psum = ctx.enter_context(nc.semaphore("silu_psum"))
        const_ready = ctx.enter_context(nc.semaphore("const_ready"))
        ident_zero = ctx.enter_context(nc.semaphore("ident_zero"))
        ident_ready = ctx.enter_context(nc.semaphore("ident_ready"))
        rows_loaded = ctx.enter_context(nc.semaphore("rows_loaded"))
        ada_loaded = ctx.enter_context(nc.semaphore("ada_loaded"))
        bias_spread = ctx.enter_context(nc.semaphore("bias_spread"))
        gate_bias_loaded = ctx.enter_context(nc.semaphore("gate_bias_loaded"))
        wf_loaded = ctx.enter_context(nc.semaphore("wf_loaded"))
        wg_loaded = ctx.enter_context(nc.semaphore("wg_loaded"))
        we_loaded = ctx.enter_context(nc.semaphore("we_loaded"))
        pre_psum = ctx.enter_context(nc.semaphore("pre_psum"))
        cols_ready = ctx.enter_context(nc.semaphore("cols_ready"))
        mods_ready = ctx.enter_context(nc.semaphore("mods_ready"))
        gate_ready = ctx.enter_context(nc.semaphore("gate_ready"))
        gate_times_bias = ctx.enter_context(nc.semaphore("gate_times_bias"))
        gate_stored = ctx.enter_context(nc.semaphore("gate_stored"))

        CONSTS = 1 + 3 + 2 * 5

        def name(m, full_names, l1):
            return a[{0: f"L0_xcond_{full_names[0]}", 2: f"L2_xcond_{full_names[1]}",
                      3: f"L3_xcond_{full_names[2]}"}[m] if m != 1 else f"L1_xcond_{l1}"]

        def w(m, key):
            table = {
                "ada_w": ("adaln_w", "ada_w", "W_mod"), "ada_b": ("adaln_b", "ada_b", "b_mod"),
                "qkv_w": ("qkv_w", "qkv_w", "W_qkv"), "qkv_b": ("qkv_b", "qkv_b", "b_qkv"),
                "proj_w": ("sa_proj_w", "self_o_w", "W_proj"), "proj_b": ("sa_proj_b", "self_o_b", "b_proj"),
                "q_w": ("q_w", "q_w", "W_qc"), "q_b": ("q_b", "q_b", "b_qc"),
                "kv_w": ("kv_w", "kv_w", "W_kvc"), "kv_b": ("kv_b", "kv_b", "b_kvc"),
                "cp_w": ("ca_proj_w", "cross_o_w", "W_cproj"), "cp_b": ("ca_proj_b", "cross_o_b", "b_cproj"),
                "fc1_w": ("fc1_w", "mlp_w1", "W_mlp1"), "fc1_b": ("fc1_b", "mlp_b1", "b_mlp1"),
                "fc2_w": ("fc2_w", "mlp_w2", "W_mlp2"), "fc2_b": ("fc2_b", "mlp_b2", "b_mlp2"),
            }
            return name(m, table[key], None)

        l1 = {k: a[f"L1_xcond_{k}"] for k in ("Wq", "bq", "Wkv", "bkv", "Wp", "bp", "Wss_q", "bss_q", "Wss_kv",
                                              "bss_kv")}
        COL = {"ada": 0, "qkv": 12, "q": 18, "kv": 20, "fc1": 24, "gamma": 32, "beta": 34} 
        COL1 = {"ada": 0, "q": 8, "kv": 10}

        def row_vectors(m):
            if not FULL[m]:
                return [(0, l1["bss_q"]), (4, l1["bss_kv"]), (COL1["q"], l1["bq"]), (COL1["kv"], l1["bkv"])]
            v = [(COL["ada"], w(m, "ada_b")), (COL["qkv"], w(m, "qkv_b")), (COL["q"], w(m, "q_b")),
                 (COL["kv"], w(m, "kv_b")), (COL["fc1"], w(m, "fc1_b"))]
            if m == 2:
                v += [(COL["gamma"], a["L2_xcond_norm2_g"]), (COL["beta"], a["L2_xcond_norm2_b"])]
            return v

        def n_rows(m):
            return max(at + v.shape[0] // P for at, v in row_vectors(m))

        def col(m, key, i):
            at = (COL if FULL[m] else COL1)[key] + i
            return cols[m % 2][:, at:at + 1]

        def mod_sources(m):
            starts = (256, 0, 1024, 768) if FULL[m] else (0, 256, 512, 768)
            return [s + P * c for s in starts for c in range(KC)]

        def rows_done(m):
            return 16 * sum(len(row_vectors(i)) for i in range(m + 1))

        ADA_DMAS = [1, 2, 1, 1]

        def ada_done(m):
            return 16 * sum(ADA_DMAS[:m + 1])

        SPREAD = [3, 2, 3, 3]

        def spread_done(m):
            return 16 * sum(SPREAD[:m + 1])

        WF_DMAS = [2, 3, 2, 2]

        def wf_done(m):
            return 16 * sum(WF_DMAS[:m + 1])

        PRE_PSUM = [3, 2, 3, 3]

        def pre_done(m, k):
            return sum(PRE_PSUM[:m]) + k

        FULL_BEFORE = [sum(FULL[:m]) for m in range(LAYERS + 1)]

        def stack_source(dram, part, width):
            return dram.rearrange("(h d) e w -> e d h w", d=HD)[part]

        def hat_of(r, m):
            return x_hat["E" if r == "G" and not FULL[m] else r]

        def is_self(m, r):
            return FULL[m] and r == "F"

        def parts_of(r, m, step, here):
            for c in range(KC):
                if step == "QK":
                    yield slot[here][:, c * NT:(c + 1) * NT], col(m, "qkv", c), q_parts[r], c
                    yield slot[here][:, BANK + c * NT:BANK + (c + 1) * NT], col(m, "qkv", KC + c), k_parts, c
                elif step == "Q":
                    yield slot[here][:, c * NT:(c + 1) * NT], col(m, "q", c), q_parts[r], c
                else:
                    yield slot[here][:, c * S:(c + 1) * S], col(m, "kv", c), kc_parts[r], c

        block = ctx.enter_context(nc.Block())

        @block.sync
        def _(sp):
            def weight(dst, src, sem, chunks=KC):
                sp.dma_start(dst, src.rearrange("(k p) n -> p k n", k=chunks)).then_inc(sem, 16)

            def load_ada(m):
                if FULL[m]:
                    weight(w_ada[:, :, :], w(m, "ada_w"), ada_loaded)
                else:
                    weight(w_ada[:, :, 0:2 * D], l1["Wss_q"], ada_loaded)
                    weight(w_ada[:, :, 2 * D:4 * D], l1["Wss_kv"], ada_loaded)

            def pre(m):
                if m == 0:
                    sp.dma_start(cond[:, :], a["cond_1024"][0:nb, :]).then_inc(cond_loaded, 16)
                    load_ada(0)
                else:
                    sp.wait_ge(pre_psum, pre_done(m - 1, 1))
                for at, v in row_vectors(m):
                    sp.dma_start(rows[at:at + v.shape[0] // P, :], v.rearrange("(n p) -> n p", p=P))\
                        .then_inc(rows_loaded, 16)
                if FULL[m]:
                    if m > 0:
                        prev = "PV3" if not FULL[m - 1] else "PV7"
                        last = nb - 1 if FULL[m - 1] else nb // 2 - 1
                        sp.wait_ge(psum_ready["F"].sem, psum_ready["F"].after(m - 1, prev, last))
                    ab = w(m, "ada_b").rearrange("(g d) -> g d", d=D)
                    for i, v in enumerate((ab[2], w(m, "proj_b"), ab[5], w(m, "fc2_b"))):
                        sp.dma_start(bias_rows[0:nb, i, :], v.unsqueeze(0).to_broadcast([nb, D]))\
                            .then_inc(gate_bias_loaded, 16)
                if m > 0:
                    if FULL[m - 1]:
                        sp.wait_ge(psum_ready["F"].sem, psum_ready["F"].after(m - 1, "V", nb - 1))
                    else:
                        for r in "FG":
                            sp.wait_ge(psum_ready[r].sem, psum_ready[r].after(m - 1, "Q", nb // 2 - 1))
                if FULL[m]:
                    weight(w_qkv[:, :, :], w(m, "qkv_w"), wf_loaded)
                    weight(w_proj[m % 2][:, :, :], w(m, "proj_w"), wf_loaded)
                    spread = ((v_bias, w(m, "qkv_b")[2 * D:3 * D]), (vc_bias, w(m, "kv_b")[D:2 * D]),
                              (cp_bias, w(m, "cp_b")))
                else:
                    weight(w_qkv[:, :, 0:D], l1["Wq"], wf_loaded)
                    weight(w_qkv[:, :, D:3 * D], l1["Wkv"], wf_loaded)
                    weight(w_proj[m % 2][:, :, :], l1["Wp"], wf_loaded)
                    spread = ((vc_bias, l1["bkv"][D:2 * D]), (cp_bias, l1["bp"]))
                for tile, v in spread:
                    sp.dma_start(tile[m % 2][:, :], v.unsqueeze(0).to_broadcast([P, D])).then_inc(bias_spread, 16)
                if FULL[m]:
                    sp.wait_ge(gate_times_bias, FULL_BEFORE[m] + 1)
                    sp.dma_start(gate_rows[m], gate_sb[0:nb, :, :]).then_inc(gate_stored, 16)
                if m + 1 < LAYERS:
                    sp.wait_ge(pre_psum, pre_done(m, PRE_PSUM[m]))
                    load_ada(m + 1)

            def weights_g(m):
                if m > 0:
                    prev = 0 if m == 2 else m - 1
                    sp.wait_ge(psum_ready["G"].sem, psum_ready["G"].after(prev, "Q", nb - 1))
                weight(w_kv2[:, :, :], w(m, "kv_w"), wg_loaded)
                weight(w_q2[:, :, :], w(m, "q_w"), wg_loaded)

            def weights_e(m):
                if m > 0:
                    prev = 0 if m == 2 else m - 1
                    sp.wait_ge(psum_ready["G"].sem, psum_ready["G"].after(prev, "PR", nb - 1))
                    sp.wait_ge(psum_ready["E"].sem, psum_ready["E"].after(prev, "F21", nb - 1))
                weight(w_cp[:, :, :], w(m, "cp_w"), we_loaded)
                weight(w_fc1[:, :, :], w(m, "fc1_w"), we_loaded)
                weight(w_fc2[:, :, :], w(m, "fc2_w"), we_loaded, MC)

            def batch(r, m, n):
                return n if FULL[m] else 2 * n + (r == "G")

            def handler(r, m, step, n, looping, here):
                b = batch(r, m, n)
                if FULL[m] and step == gate_step.get(r):
                    g = 0 if r == "F" else 2
                    gate_src = gate_rows[m][bass.ds(b, 1), g:g + 2, :].to_broadcast([P, 2, D])
                    (x_mid_ready if r == "F" else x_new_ready)[r].wait_before(sp, m, n)
                    sp.wait_ge(gate_stored, 16 * (FULL_BEFORE[m] + 1))
                    sp.dma_start(gate_now[r][:, :, :], gate_src).then_inc(gate_loaded[r].sem, 16)
                if step == "ld":
                    if loads_x(m, r):
                        x_src = x_in[m][bass.ds(b, 1)].rearrange("o (t p) d -> p (o t) d", p=P)
                        x_biased[r].wait_before(sp, m, n)
                        if r == "G":
                            x_new_ready["E"].wait_before(sp, m, 0)
                        if m > 0:
                            if looping:
                                for q in "FGE":
                                    x_stored[q].wait_before(sp, m, 0)
                            else:
                                q = "E" if FULL[m - 1] else "FG"[b % 2]
                                sp.wait_ge(x_stored[q].sem,
                                           x_stored[q].after(m - 1, "ST", b if FULL[m - 1] else b // 2))
                        sp.dma_start(x_stage[r][:, :, :], x_src).then_inc(x_loaded[r].sem, 16)
                    if r == "G" or (r == "F" and not FULL[m]):
                        context_src = a["ctx_1024"][bass.ds(b, 1)].rearrange("o s d -> (o s) d")
                        (x_hat_ready if CTX_LN[m] else context_t_ready)[r].wait_before(sp, m, n)
                        sp.dma_start(context[r][0:S, :], context_src).then_inc(context_loaded[r].sem, 16)
                elif step in ("QK", "Q", "KV"):
                    sp.wait_ge(lo_ready[r].sem, lo_ready[r].after(m, step, n))
                    if step in ("QK", "Q"):
                        sp.dma_start(q_parts_dram[r].rearrange("p e w -> p (e w)"),
                                     q_parts[r][:, :, :, :].rearrange("p e m w -> p (e m w)"))\
                            .then_inc(q_stored[r].sem, 16)
                    if step == "QK":
                        sp.dma_start(k_parts_dram["F"].rearrange("p e w -> p (e w)"),
                                     k_parts[:, :, :, :].rearrange("p e m w -> p (e m w)"))\
                            .then_inc(k_stored[r].sem, 16)
                    if step == "KV":
                        sp.dma_start(kc_parts_dram[r].rearrange("p e w -> p (e w)"),
                                     kc_parts[r][:, :, :, :].rearrange("p e m w -> p (e m w)"))\
                            .then_inc(k_stored[r].sem, 16)
                    if step in ("QK", "Q"):
                        sp.wait_ge(q_stored[r].sem, q_stored[r].after(m, step, n))
                        if not looping:
                            sp.wait_ge(const_ready, CONSTS)
                        for row, part in ((0, 0), (HD, 0), (LO_ROW, 1)):
                            sp.dma_start(q_stack[r][row:row + HD, :, :].rearrange("p (h m) w -> p h (m w)", m=KC),
                                         stack_source(q_parts_dram[r], part, NT)).then_inc(q_stack_loaded[r].sem, 16)
                    if step in ("QK", "KV"):
                        sp.wait_ge(k_stored[r].sem, k_stored[r].after(m, step, n))
                        if not looping:
                            sp.wait_ge(const_ready, CONSTS)
                        width, dram = (NT, k_parts_dram["F"]) if step == "QK" else (S, kc_parts_dram[r])
                        for row, part in ((0, 0), (HD, 1), (LO_ROW, 0)):
                            sp.dma_start(k_stack[r][row:row + HD, 0:H * width].rearrange("p (h w) -> p h w", h=H // 2),
                                         stack_source(dram, part, width)).then_inc(k_stack_loaded[r].sem, 16)
                elif step in ("M0", "M1"):
                    h = int(step[1])
                    sp.wait_ge(max_t_ready[r].sem, max_t_ready[r].after(m, step, n))
                    sp.dma_start(q_stack[r][MAX_ROW:MAX_ROW + 2, h * 8:h * 8 + 8, :], max_t[r][h][:, :])\
                        .then_inc(max_row_loaded[h][r].sem, 16)
                elif step == "ST":
                    b = batch(r, m, n)
                    after = "F21" if FULL[m] else "PR"
                    dst = x_out[m][bass.ds(b, 1)].rearrange("o (t p) d -> p (o t) d", p=P)
                    sp.wait_ge(x_new_ready[r].sem, x_new_ready[r].after(m, after, n))
                    sp.dma_start(dst, x_new[r][:, :, :]).then_inc(x_stored[r].sem, 16)

            walk(sp, program, handler, pre, weights_g, weights_e)
            for r in "FGE":
                sp.wait_ge(x_stored[r].sem, x_stored[r].base[LAYERS])

        @block.gpsimd
        def _(pool):
            nc.gpsimd.memset(ident[:, :], 0.0).then_inc(ident_zero, 1)
            pool.wait_ge(ident_zero, 1)
            nc.gpsimd.affine_select(out=ident[:, :], in_=ident[:, :], compare_op=ALU.not_equal, fill=1.0, base=0,
                                    pattern=[[-1, P]], channel_multiplier=1).then_inc(ident_ready, 1)
            nc.gpsimd.memset(minus_half[:, :], -0.5).then_inc(const_ready, 1)
            for t in (v_self, v_ctx["F"], v_ctx["G"]):
                flat = t[:, :, :, :].rearrange("p c h k -> p (c h) k") if len(t.shape) == 4 else t[:, :, :]
                nc.gpsimd.memset(flat[:, :, HD:2 * HD], 1.0).then_inc(const_ready, 1)
            done = 4
            for r in "FG":
                for t, lo, hi, value in ((q_stack[r][:, :, :], 32, 64, 0.0), (q_stack[r][:, :, :], 64, 96, 0.0),
                                         (k_stack[r][:, :], 32, 64, 0.0), (k_stack[r][:, :], 64, 96, 0.0),
                                         (k_stack[r][:, :], MAX_ROW, MAX_ROW + 2, 1.0)):
                    pool.wait_ge(const_ready, done)
                    nc.gpsimd.memset(t[lo:hi], value).then_inc(const_ready, 1)
                    done += 1
            pool.wait_ge(const_ready, done)

            def rstd_of(r, m, step, n):
                pool.wait_ge(var_ready[r].sem, var_ready[r].after(m, step, n))
                if step == "NC":
                    nc.gpsimd.tensor_tensor(c_rstd[r][0:S, :], c_var_eps[r][0:S, :], minus_half[0:S, 0:1], ALU.pow)\
                        .then_inc(rstd_ready[r].sem, 1)
                else:
                    nc.gpsimd.tensor_tensor(rstd[r][:, :], var_eps[r][:, :], minus_half[:, :], ALU.pow)\
                        .then_inc(rstd_ready[r].sem, 1)

            def pre_add(r, m, n):
                pool.wait_ge(x_hat_ready[r].sem, x_hat_ready[r].after(m, "N", n))
                x_mid_ready[r].wait_before(pool, m, n)
                x_new_ready[r].wait_before(pool, m, n)
                if r == "G":
                    x_hat_ready["E"].wait_before(pool, m, n if FULL[m] else 0)
                    x_biased["E"].wait_before(pool, m, n if FULL[m] else 0)
                if r == "E":
                    src = x["G"]
                else:
                    src = x_stage[r] if loads_x(m, r) else x_mid
                if FULL[m] and r != "G":
                    pool.wait_ge(gate_loaded[r].sem, gate_loaded[r].after(m, gate_step[r], n))
                    bias = gate_now[r][:, 1:2, :].to_broadcast([P, TT, D])
                else:
                    pool.wait_ge(bias_spread, spread_done(m))
                    bias = cp_bias[m % 2][:, :].unsqueeze(1).to_broadcast([P, TT, D])
                nc.gpsimd.tensor_tensor(x[r][:, :, :], src[:, :, :], bias, ALU.add).then_inc(x_biased[r].sem, 1)

            def handler(r, m, step, n, looping, here):
                if step == "N" or (step == "NC" and CTX_LN[m]):
                    rstd_of(r, m, step, n)
                if step == ("LN" if loads_x(m, r) else "N"):
                    pre_add(r, m, n)
                if step == "PR" and FULL[m] and r == "F":
                    pool.wait_ge(gated_ready[r].sem, gated_ready[r].after(m, "PR", n))
                    pool.wait_ge(x_biased[r].sem, x_biased[r].after(m, "N", n))
                    x_biased["G"].wait_before(pool, m, n)
                    if not looping:
                        x_stored["F"].wait_before(pool, m, 0)
                    nc.gpsimd.tensor_tensor(x_mid[:, :, :], x["F"][:, :, :], gated["F"][:, :, :], ALU.add)\
                        .then_inc(x_mid_ready[r].sem, 1)
                elif step == "F21":
                    pool.wait_ge(gated_ready[r].sem, gated_ready[r].after(m, "F21", n))
                    pool.wait_ge(x_biased[r].sem, x_biased[r].after(m, "N", n))
                    x_stored[r].wait_before(pool, m, n)
                    if not looping:
                        x_stored["G"].wait_before(pool, m, 0)
                    nc.gpsimd.tensor_tensor(x_new["E"][:, :, :], x["E"][:, :, :], gated["E"][:, :, :], ALU.add)\
                        .then_inc(x_new_ready[r].sem, 1)

            walk(pool, program, handler)

        @block.vector
        def _(dve):
            def pre(m):
                if m == 0:
                    dve.wait_ge(silu_exp, 1)
                    nc.vector.tensor_scalar(cond_e[:, :], cond_e[:, :], 1.0, None, ALU.add).then_inc(silu_step, 1)
                    dve.wait_ge(silu_step, 1)
                    nc.vector.reciprocal(cond_e[:, :], cond_e[:, :]).then_inc(silu_step, 1)
                    dve.wait_ge(silu_step, 2)
                    nc.vector.tensor_tensor(cond[:, :], cond[:, :], cond_e[:, :], ALU.mult).then_inc(silu_step, 1)
                    dve.wait_ge(silu_psum, 1)
                    nc.vector.tensor_copy(silu_t[:, :, :].rearrange("p k b -> p (k b)"), o_acc["F"][:, 0:KC * nb])\
                        .then_inc(silu_step, 1)
                dve.wait_ge(pre_psum, pre_done(m, 1))
                nc.vector.tensor_copy(cols[m % 2][:, 0:n_rows(m)], o_acc["F"][:, 0:n_rows(m)])\
                    .then_inc(cols_ready, 1)
                dve.wait_ge(pre_psum, pre_done(m, 2))
                dve.wait_ge(cols_ready, m + 1)
                for j, src in enumerate(mod_sources(m)):
                    one = 1.0 if j % 4 < KC else 0.0
                    last = nc.vector.tensor_scalar(mods[m % 2][:, :, j], o_acc["F"][:, 64 + nb * j:64 + nb * (j + 1)],
                                                   col(m, "ada", src // P), one, ALU.add, ALU.add)
                last.then_inc(mods_ready, 1)
                if FULL[m]:
                    dve.wait_ge(pre_psum, pre_done(m, 3))
                    dve.wait_ge(gate_bias_loaded, 64 * (FULL_BEFORE[m] + 1))
                    for g in range(2):
                        last = nc.vector.tensor_tensor(gate_sb[0:nb, 2 * g, :], o_acc["F"][0:nb, g * D:(g + 1) * D],
                                                       bias_rows[0:nb, 2 * g, :], ALU.add)
                    last.then_inc(gate_ready, 1)
                    dve.wait_ge(gate_ready, FULL_BEFORE[m] + 1)
                    for g in range(2):
                        last = nc.vector.tensor_tensor(gate_sb[0:nb, 2 * g + 1, :], gate_sb[0:nb, 2 * g, :],
                                                       bias_rows[0:nb, 2 * g + 1, :], ALU.mult)
                    last.then_inc(gate_times_bias, 1)

            def norm(r, m, step, n):
                if step == "NC":
                    dve.wait_ge(context_loaded[r].sem, context_loaded[r].after(m, "ld", n))
                    tiles = [(context[r][0:S, :], context_hat[r][0:S, :])]
                    st, mv, ve, rs = (c_stats[r][0:S, :].unsqueeze(1), c_mean_var[r][0:S, :].unsqueeze(1),
                                      c_var_eps[r][0:S, :], c_rstd[r][0:S, :])
                else:
                    x_src = x["G"] if r == "E" else x_stage[r] if loads_x(m, r) else x_mid
                    tiles = [(x_src[:, t, :], hat_of(r, m)[:, t, :]) for t in range(TT)]
                    st, mv, ve, rs = stats[r][:, :, :], mean_var[r][:, :, :], var_eps[r][:, :], rstd[r][:, :]
                    if r == "E":
                        dve.wait_ge(x_cross_ready["G"].sem, x_cross_ready["G"].after(m, "PR", n))
                    elif FULL[m] and r == "G":
                        dve.wait_ge(x_mid_ready["F"].sem, x_mid_ready["F"].after(m, "PR", n))
                    else:
                        dve.wait_ge(x_loaded[r].sem, x_loaded[r].after(m, "ld", n))
                for t, (src, _) in enumerate(tiles):
                    last = nc.vector.bn_stats(st[:, t, :], src)
                last.then_inc(stats_ready[r].sem, 1)
                dve.wait_ge(stats_ready[r].sem, stats_ready[r].after(m, step, n))
                nc.vector.memset(wait_mark[:, :], 0.0)
                for t in range(len(tiles)):
                    last = nc.vector.bn_aggr(mv[:, t, :], st[:, t, :])
                last.then_inc(mean_ready[r].sem, 1)
                dve.wait_ge(mean_ready[r].sem, mean_ready[r].after(m, step, n))
                nc.vector.tensor_scalar(ve, mv[:, :, 1], EPS[m], None, ALU.add).then_inc(var_ready[r].sem, 1)
                dve.wait_ge(rstd_ready[r].sem, rstd_ready[r].after(m, step, n))
                for t, (src, dst) in enumerate(tiles):
                    last = nc.vector.tensor_scalar(dst, src, mv[:, t, 0:1], rs[:, t:t + 1], ALU.subtract, ALU.mult)
                last.then_inc(x_hat_ready[r].sem, 1)

            def low_parts(r, m, step, n, here):
                dve.wait_ge(hi_ready[r].sem, hi_ready[r].after(m, step, n))
                for src, bias, tile, c in parts_of(r, m, step, here):
                    last = nc.vector.scalar_tensor_tensor(out=tile[:, 1, c, :].bitcast(F32R), in0=src, scalar=bias,
                                                          in1=tile[:, 0, c, :], op0=ALU.add, op1=ALU.subtract)
                last.then_inc(lo_ready[r].sem, 1)

            def handler(r, m, step, n, looping, here):
                if step == "ld":
                    if not looping:
                        dve.wait_ge(mods_ready, m + 1)
                    x_t_ready[r].wait_before(dve, m, n)
                    context_t_ready[r].wait_before(dve, m, n)
                    if FULL[m] and r == "G":
                        return
                    b = n if FULL[m] else 2 * n + (r == "G")
                    nc.vector.tensor_copy(mod_now[r][:, :], mods[m % 2][:, bass.ds(b, 1), :].rearrange("p o c -> p (o c)"))\
                        .then_inc(mod_ready[r].sem, 1)
                elif step == "N" or (step == "NC" and CTX_LN[m]):
                    norm(r, m, step, n)
                elif step in ("QK", "Q"):
                    low_parts(r, m, step, n, here)
                elif step == "KV":
                    low_parts(r, m, step, n, here)
                    if not looping:
                        dve.wait_ge(bias_spread, spread_done(m))
                    nc.vector.tensor_tensor(v_ctx[r][0:S, :, 0:HD],
                                            slot[here][0:S, BANK:BANK + D].rearrange("p (h d) -> p h d", d=HD),
                                            vc_bias[m % 2][0:S, :].rearrange("p (h d) -> p h d", d=HD), ALU.add)\
                        .then_inc(v_ready[r].sem, 1)
                elif step == "V":
                    dve.wait_ge(psum_ready[r].sem, psum_ready[r].after(m, step, n))
                    if not looping:
                        dve.wait_ge(bias_spread, spread_done(m))
                    for t in range(TT):
                        last = nc.vector.tensor_tensor(v_self[:, t, :, 0:HD],
                                                       slot[here][:, t * D:(t + 1) * D].rearrange("p (h d) -> p h d", d=HD),
                                                       v_bias[m % 2][:, :].rearrange("p (h d) -> p h d", d=HD), ALU.add)
                    last.then_inc(v_ready[r].sem, 1)
                elif step[0] == "S" and step[1:].isdigit():
                    u = int(step[1])
                    dve.wait_ge(psum_ready[r].sem, psum_ready[r].after(m, step, n))
                    if is_self(m, r):
                        heads, t = QUAD * (u // 2), u % 2
                        src = slot[here][:, :].rearrange("p (h k) -> p h k", h=QUAD)
                        dst = row_max[r][:, t, heads:heads + QUAD]
                    else:
                        heads, t = 2 * QUAD * (u // 2), u % 2
                        src = slot[here][:, :].rearrange("p (b w) -> p b w", b=2)[:, :, 0:QUAD * S]\
                            .rearrange("p b (h k) -> p b h k", h=QUAD)
                        dst = row_max[r][:, t, heads:heads + 2 * QUAD].rearrange("p (b h) -> p b h", b=2)
                    nc.vector.tensor_reduce(dst, src, AX.X, ALU.max).then_inc(row_max_ready[r].sem, 1)
                elif step in ("M0", "M1"):
                    h = int(step[1])
                    need = {True: ("S3", "S7"), False: ("S1", "S3")}[is_self(m, r)][h]
                    src = row_max[r][:, :, 8 * h:8 * h + 8]
                    hi, lo = max_parts[r][:, :, h, 0, :], max_parts[r][:, :, h, 1, :]
                    dve.wait_ge(row_max_ready[r].sem, row_max_ready[r].after(m, need, n))
                    nc.vector.tensor_scalar(hi.bitcast(F32R), src, -1.0, None, ALU.mult)\
                        .then_inc(max_hi_ready[r].sem, 1)
                    dve.wait_ge(max_hi_ready[r].sem, max_hi_ready[r].after(m, step, n))
                    nc.vector.scalar_tensor_tensor(out=lo.bitcast(F32R), in0=src, scalar=-1.0, in1=hi,
                                                   op0=ALU.mult, op1=ALU.subtract).then_inc(max_parts_ready[r].sem, 1)
                elif step == "O1":
                    dve.wait_ge(psum_ready[r].sem, psum_ready[r].after(m, step, n))
                    o = slot[here][:, :].rearrange("p (t j k) -> p t j k", t=TT, j=H)
                    nc.vector.reciprocal(r_den[r][:, :, :], o[:, :, :, HD]).then_inc(r_den_ready[r].sem, 1)
                    dve.wait_ge(r_den_ready[r].sem, r_den_ready[r].after(m, step, n))
                    for t in range(TT):
                        last = nc.vector.tensor_tensor(
                            o_norm[r][:, t, :].rearrange("p (e i d) -> p i e d", e=2, i=H // 2),
                            o[:, t, :, 0:HD].rearrange("p (i e) d -> p i e d", e=2),
                            r_den[r][:, t, :].rearrange("p (i e) -> p i e", e=2).unsqueeze(3)
                            .to_broadcast([P, H // 2, 2, HD]), ALU.mult)
                    last.then_inc(o_norm_ready[r].sem, 1)
                elif step == "PR":
                    dve.wait_ge(psum_ready[r].sem, psum_ready[r].after(m, step, n))
                    src = slot[here][:, 0:TT * D].rearrange("p (t d) -> p t d", t=TT)
                    if FULL[m] and r == "F":
                        dve.wait_ge(gate_loaded[r].sem, gate_loaded[r].after(m, gate_step[r], n))
                        nc.vector.tensor_tensor(gated[r][:, :, :], src, gate_now[r][:, 0:1, :].to_broadcast([P, TT, D]),
                                                ALU.mult).then_inc(gated_ready[r].sem, 1)
                    else:
                        dve.wait_ge(x_biased[r].sem, x_biased[r].after(m, "N", n))
                        if FULL[m]:
                            nc.vector.tensor_tensor(x[r][:, :, :], src, x[r][:, :, :], ALU.add)\
                                .then_inc(x_cross_ready[r].sem, 1)
                        else:
                            x_stored[r].wait_before(dve, m, n)
                            x_biased["G"].wait_before(dve, m, 0)
                            x_stored["E"].wait_before(dve, m, 0)
                            nc.vector.tensor_tensor(x_new[r][:, :, :], src, x[r][:, :, :], ALU.add)\
                                .then_inc(x_new_ready[r].sem, 1)
                elif step in ("F20", "F21"):
                    t = int(step[2])
                    dve.wait_ge(psum_ready[r].sem, psum_ready[r].after(m, step, n))
                    if t == 0:
                        dve.wait_ge(gate_loaded[r].sem, gate_loaded[r].after(m, gate_step[r], n))
                        x_new_ready[r].wait_before(dve, m, n)
                    nc.vector.tensor_tensor(gated[r][:, t, :], slot[here][:, 0:D], gate_now[r][:, 0, :], ALU.mult)\
                        .then_inc(gated_ready[r].sem, 1)

            walk(dve, program, handler, pre)

        @block.scalar
        def _(act):
            def pre(m):
                if m == 0:
                    act.wait_ge(cond_loaded, 16)
                    nc.scalar.activation(cond_e[:, :], cond[:, :], ACT.Exp, scale=-1.0).then_inc(silu_exp, 1)

            def handler(r, m, step, n, looping, here):
                if here is not None:
                    ps = slot[here]
                if step == "LN":
                    act.wait_ge(psum_ready[r].sem, psum_ready[r].after(m, step, n))
                    plain = FULL[m] and r == "G"
                    if not plain:
                        act.wait_ge(mod_ready[r].sem, mod_ready[r].after(m, "ld", n))
                    elif m == 2 and not looping:
                        act.wait_ge(cols_ready, m + 1)
                    at = 4 if r == "E" else 0
                    for c in range(KC):
                        if not plain:
                            bias, scale = mod_now[r][:, at + 2 + c:at + 3 + c], mod_now[r][:, at + c:at + c + 1]
                        elif m == 2:
                            bias, scale = col(m, "beta", c), col(m, "gamma", c)
                        else:
                            bias, scale = 0.0, 1.0
                        last = nc.scalar.activation(x_t[r][:, c, :], ps[:, c * NT:(c + 1) * NT], ACT.Identity,
                                                    bias=bias, scale=scale)
                    last.then_inc(x_t_ready[r].sem, 1)
                elif step == "C":
                    act.wait_ge(psum_ready[r].sem, psum_ready[r].after(m, step, n))
                    if FULL[m]:
                        nc.scalar.activation(context_t[r][:, :, :],
                                             ps[:, 0:KC * S].rearrange("p (c s) -> p c s", c=KC), ACT.Identity)\
                            .then_inc(context_t_ready[r].sem, 1)
                    else:
                        act.wait_ge(mod_ready[r].sem, mod_ready[r].after(m, "ld", n))
                        for c in range(KC):
                            last = nc.scalar.activation(context_t[r][:, c, :], ps[:, c * S:(c + 1) * S],
                                                        ACT.Identity, bias=mod_now[r][:, 6 + c:7 + c],
                                                        scale=mod_now[r][:, 4 + c:5 + c])
                        last.then_inc(context_t_ready[r].sem, 1)
                elif step in ("QK", "Q", "KV"):
                    act.wait_ge(psum_ready[r].sem, psum_ready[r].after(m, step, n))
                    if not looping:
                        act.wait_ge(cols_ready, m + 1)
                    if step in ("QK", "Q"):
                        q_stored[r].wait_before(act, m, n)
                    if step in ("QK", "KV"):
                        k_stored[r].wait_before(act, m, n)
                    for src, bias, tile, c in parts_of(r, m, step, here):
                        last = nc.scalar.activation(tile[:, 0, c, :].bitcast(F32R), src, ACT.Identity, bias=bias)
                    last.then_inc(hi_ready[r].sem, 1)
                elif step in ("M0", "M1"):
                    act.wait_ge(psum_ready[r].sem, psum_ready[r].after(m, step, n))
                    nc.scalar.activation(max_t[r][int(step[1])][:, :], ps[0:H, 0:NT], ACT.Identity)\
                        .then_inc(max_t_ready[r].sem, 1)
                elif step[0] == "T":
                    v = int(step[1:])
                    keys = P if is_self(m, r) else S
                    act.wait_ge(psum_ready[r].sem, psum_ready[r].after(m, step, n))
                    if not looping and is_self(m, r):
                        act.wait_ge(gate_stored, 16 * (FULL_BEFORE[m] + 1))
                    nc.scalar.activation(probs[r][v % 2][0:keys, :, :],
                                         ps[0:keys, :].rearrange("p (g q) -> p g q", g=QUAD), ACT.Exp, scale=SCALE)\
                        .then_inc(probs_ready[r].sem, 1)
                elif step in out_banks(m, r):
                    act.wait_ge(psum_ready[r].sem, psum_ready[r].after(m, step, n))
                    i = out_banks(m, r).index(step)
                    nc.scalar.activation(o_raw[r][:, 2 * i:2 * i + 2, :],
                                         o_acc[r][:, :].rearrange("p (i q) -> p i q", i=2), ACT.Identity)\
                        .then_inc(o_raw_ready[r].sem, 1)
                elif step == "O2":
                    act.wait_ge(psum_ready[r].sem, psum_ready[r].after(m, step, n))
                    nc.scalar.activation(o_t[r][:, :, :], ps[:, 0:KC * NT].rearrange("p (k q) -> p k q", k=KC),
                                         ACT.Identity).then_inc(o_t_ready[r].sem, 1)
                elif step in ("H0", "H1"):
                    act.wait_ge(psum_ready[r].sem, psum_ready[r].after(m, step, n))
                    for i in range(4):
                        c = 4 * int(step[1]) + i
                        last = nc.scalar.activation(h_t[:, c, :], ps[:, i * NT:(i + 1) * NT], ACT.Gelu_apprx_tanh,
                                                    bias=col(m, "fc1", c))
                    last.then_inc(h_ready[r].sem, 1)

            walk(act, program, handler, pre)

        @block.tensor
        def _(pe):
            mm = nc.tensor.matmul

            def transpose(dst, src, rows_in):
                return nc.tensor.transpose(dst, src, ident[0:rows_in, 0:rows_in])

            def release(r, m, step, n=None, before=False):
                if step == "LN":
                    s = x_t_ready
                elif step == "C":
                    s = context_t_ready
                elif step in ("QK", "Q"):
                    s = lo_ready
                elif step in ("V", "KV"):
                    s = v_ready
                elif step[0] == "S":
                    s = row_max_ready
                elif step[0] == "M":
                    s = max_t_ready
                elif step[0] == "T":
                    s = probs_ready
                elif step == "O1":
                    s = o_norm_ready
                elif step == "O2":
                    s = o_t_ready
                elif step[0] == "H":
                    s = h_ready
                elif step[:2] == "F2" or (step == "PR" and is_self(m, r)):
                    s = gated_ready
                else:
                    s = x_cross_ready if FULL[m] else x_new_ready
                if before:
                    s[r].wait_before(pe, m, n)
                else:
                    pe.wait_ge(s[r].sem, s[r].after(m, step, n))

            last_user = {}

            def pre(m):
                pre_bank = o_acc["F"]
                if m == 0:
                    pe.wait_ge(ident_ready, 1)
                    pe.wait_ge(silu_step, 3)
                    for k in range(KC):
                        last = transpose(pre_bank[:, k * nb:(k + 1) * nb], cond[0:nb, k * P:(k + 1) * P], nb)
                    last.then_inc(silu_psum, 1)
                    pe.wait_ge(silu_step, 4)
                else:
                    end = out_banks(m - 1, "F")[-1]
                    pe.wait_ge(o_raw_ready["F"].sem,
                               o_raw_ready["F"].after(m - 1, end, (nb if FULL[m - 1] else nb // 2) - 1))
                pe.wait_ge(rows_loaded, rows_done(m))
                transpose(pre_bank[:, 0:n_rows(m)], rows[0:n_rows(m), :], n_rows(m)).then_inc(pre_psum, 1)
                pe.wait_ge(ada_loaded, ada_done(m))
                pe.wait_ge(cols_ready, m + 1)
                for j, src in enumerate(mod_sources(m)):
                    for k in range(KC):
                        last = mm(pre_bank[:, 64 + nb * j:64 + nb * (j + 1)], w_ada[:, k, src:src + P],
                                  silu_t[:, k, :], start=k == 0, stop=k == KC - 1)
                last.then_inc(pre_psum, 1)
                if FULL[m]:
                    pe.wait_ge(mods_ready, m + 1)
                    for g, at in enumerate((2 * D, 5 * D)):
                        for k in range(KC):
                            last = mm(pre_bank[0:nb, g * D:(g + 1) * D], silu_t[:, k, :],
                                      w_ada[:, k, at:at + D], start=k == 0, stop=k == KC - 1)
                    last.then_inc(pre_psum, 1)

            def weights_wait(r, m, step, looping):
                if looping:
                    return
                if r == "F" or not FULL[m]:
                    pe.wait_ge(wf_loaded, wf_done(m))
                else:
                    sem, dmas = (we_loaded, 3) if r == "E" or step == "PR" else (wg_loaded, 2)
                    pe.wait_ge(sem, 16 * dmas * (FULL_BEFORE[m] + 1))

            def handler(r, m, step, n, looping, here):
                if step in OFF_PE:
                    return
                if here is not None:
                    user = last_user.get(here)
                    if user == "last iteration":
                        ur, um, ustep, udn = loop_last[here]
                        release(ur, um, ustep, n - loop_dn[(r, m, step)] + udn, before=True)
                    elif user:
                        release(*user)
                    last_user[here] = (r, m, step, n)
                    ps = slot[here]
                if step == "LN":
                    pe.wait_ge(x_hat_ready[r].sem, x_hat_ready[r].after(m, "N", n))
                    for k in range(KC):
                        for t in range(TT):
                            last = transpose(ps[:, k * NT + t * P:k * NT + (t + 1) * P],
                                             hat_of(r, m)[:, t, k * P:(k + 1) * P], P)
                elif step == "C":
                    if CTX_LN[m]:
                        pe.wait_ge(x_hat_ready[r].sem, x_hat_ready[r].after(m, "NC", n))
                    else:
                        pe.wait_ge(context_loaded[r].sem, context_loaded[r].after(m, "ld", n))
                    src = (context_hat if CTX_LN[m] else context)[r]
                    for k in range(KC):
                        last = transpose(ps[:, k * S:(k + 1) * S], src[0:S, k * P:(k + 1) * P], S)
                elif step in ("QK", "Q"):
                    weights_wait(r, m, step, looping)
                    pe.wait_ge(x_t_ready[r].sem, x_t_ready[r].after(m, "LN", n))
                    weight = w_q2 if FULL[m] and r == "G" else w_qkv
                    for c in range(4 if step == "QK" else 2):
                        for k in range(KC):
                            last = mm(ps[:, c * NT:(c + 1) * NT], weight[:, k, c * P:(c + 1) * P], x_t[r][:, k, :],
                                      start=k == 0, stop=k == KC - 1)
                elif step == "V":
                    for t in range(TT):
                        for k in range(KC):
                            last = mm(ps[:, t * D:(t + 1) * D], x_t[r][:, k, t * P:(t + 1) * P],
                                      w_qkv[:, k, 2 * D:3 * D], start=k == 0, stop=k == KC - 1)
                elif step == "KV":
                    weights_wait(r, m, step, looping)
                    pe.wait_ge(context_t_ready[r].sem, context_t_ready[r].after(m, "C", n))
                    weight, at = (w_kv2, 0) if FULL[m] else (w_qkv, D)
                    for c in range(KC):
                        for k in range(KC):
                            mm(ps[:, c * S:(c + 1) * S], weight[:, k, at + c * P:at + (c + 1) * P],
                               context_t[r][:, k, :], start=k == 0, stop=k == KC - 1)
                    for k in range(KC):
                        last = mm(ps[0:S, BANK:BANK + D], context_t[r][:, k, :], weight[:, k, at + D:at + 2 * D],
                                  start=k == 0, stop=k == KC - 1)
                elif step[0] == "S":
                    u = int(step[1:])
                    t = u % 2
                    if step == "S0":
                        qk = ("QK", "QK") if is_self(m, r) else ("Q", "KV")
                        pe.wait_ge(q_stack_loaded[r].sem, q_stack_loaded[r].after(m, qk[0], n))
                        pe.wait_ge(k_stack_loaded[r].sem, k_stack_loaded[r].after(m, qk[1], n))
                        if not looping:
                            pe.wait_ge(const_ready, CONSTS)
                    heads, width = (QUAD, NT) if is_self(m, r) else (2 * QUAD, S)
                    for i in range(heads):
                        j = heads * (u // 2) + i
                        at = i * width if is_self(m, r) else i // QUAD * BANK + i % QUAD * S
                        last = mm(ps[:, at:at + width], q_stack[r][0:MAX_ROW, j, t * P:(t + 1) * P].bitcast(F32R),
                                  k_stack[r][0:MAX_ROW, j * width:(j + 1) * width].bitcast(F32R),
                                  start=True, stop=True)
                elif step[0] == "M":
                    h = int(step[1:])
                    pe.wait_ge(max_parts_ready[r].sem, max_parts_ready[r].after(m, step, n))
                    for t in range(TT):
                        last = transpose(ps[0:H, t * P:(t + 1) * P],
                                         max_parts[r][:, t, h, :, :].rearrange("p e h -> p (e h)"), P)
                elif step[0] == "T":
                    v = int(step[1:])
                    quad, c, keys, width = (v // 2, v % 2, P, NT) if is_self(m, r) else (v, 0, S, S)
                    half = quad // 2
                    if quad % 2 == 0 and c == 0:
                        sem = max_row_loaded[half][r]
                        pe.wait_ge(sem.sem, sem.after(m, f"M{half}", n))
                    for g in range(QUAD):
                        j = QUAD * quad + g
                        last = mm(ps[0:keys, g * NT:(g + 1) * NT],
                                  k_stack[r][0:STACK_ROWS, j * width + c * P:j * width + c * P + keys].bitcast(F32R),
                                  q_stack[r][0:STACK_ROWS, j, :].bitcast(F32R), start=True, stop=True)
                elif step[:2] == "PV":
                    v = int(step[2:])
                    quad, c, keys = (v // 2, v % 2, P) if is_self(m, r) else (v, 0, S)
                    ends = out_banks(m, r)
                    if v == 0:
                        o_raw_ready[r].wait_before(pe, m, n)
                        kv = "V" if is_self(m, r) else "KV"
                        pe.wait_ge(v_ready[r].sem, v_ready[r].after(m, kv, n))
                    elif quad == 2 and c == 0:
                        pe.wait_ge(o_raw_ready[r].sem, o_raw_ready[r].after(m, ends[0], n))
                    pe.wait_ge(probs_ready[r].sem, probs_ready[r].after(m, f"T{v}", n))
                    for g in range(QUAD):
                        head = head_of(QUAD * quad + g)
                        v_head = v_self[:, c, head, :] if is_self(m, r) else v_ctx[r][0:S, head, :]
                        at = quad % 2 * NT
                        last = mm(o_acc[r][g * 2 * HD:(g + 1) * 2 * HD, at:at + NT], v_head,
                                  probs[r][v % 2][0:keys, g, :], start=c == 0, stop=c == 1 or not is_self(m, r))
                elif step == "O1":
                    pe.wait_ge(o_raw_ready[r].sem, o_raw_ready[r].after(m, out_banks(m, r)[1], n))
                    for t in range(TT):
                        for quad in range(H // QUAD):
                            last = transpose(ps[:, t * BANK + quad * P:t * BANK + (quad + 1) * P],
                                             o_raw[r][:, quad, t * P:(t + 1) * P], P)
                elif step == "O2":
                    pe.wait_ge(o_norm_ready[r].sem, o_norm_ready[r].after(m, "O1", n))
                    for k in range(KC):
                        for t in range(TT):
                            last = transpose(ps[:, k * NT + t * P:k * NT + (t + 1) * P],
                                             o_norm[r][:, t, k * P:(k + 1) * P], P)
                elif step == "PR":
                    pe.wait_ge(o_t_ready[r].sem, o_t_ready[r].after(m, "O2", n))
                    weights_wait(r, m, step, looping)
                    weight = w_cp if FULL[m] and r == "G" else w_proj[m % 2]
                    for t in range(TT):
                        for k in range(KC):
                            last = mm(ps[:, t * D:(t + 1) * D], o_t[r][:, k, t * P:(t + 1) * P], weight[:, k, :],
                                      start=k == 0, stop=k == KC - 1)
                elif step[0] == "H":
                    pe.wait_ge(x_t_ready[r].sem, x_t_ready[r].after(m, "LN", n))
                    weights_wait(r, m, step, looping)
                    for i in range(4):
                        c = 4 * int(step[1:]) + i
                        for k in range(KC):
                            last = mm(ps[:, i * NT:(i + 1) * NT], w_fc1[:, k, c * P:(c + 1) * P], x_t[r][:, k, :],
                                      start=k == 0, stop=k == KC - 1)
                elif step in ("F20", "F21"):
                    t = int(step[2])
                    pe.wait_ge(h_ready[r].sem, h_ready[r].after(m, "H1", n))
                    for k in range(MC):
                        last = mm(ps[:, 0:D], h_t[:, k, t * P:(t + 1) * P], w_fc2[:, k, :],
                                  start=k == 0, stop=k == MC - 1)
                last.then_inc(psum_ready[r].sem, 1)

            loop_last, loop_dn = {}, {}
            for seg in program:
                if seg[0] == "loop" and seg[1] > 0:
                    for s in sorted(last_user):
                        release(*last_user[s])
                    place = places(seg[2])
                    loop_last.clear()
                    loop_dn.clear()
                    for r, m, step, dn in seg[2]:
                        if (r, m, step) in place:
                            loop_last[place[(r, m, step)]] = (r, m, step, dn)
                            loop_dn[(r, m, step)] = dn
                    for s in range(SLOTS):
                        last_user[s] = "last iteration"
                    walk(pe, [seg], handler)
                    for s in range(SLOTS):
                        r, m, step, dn = loop_last[s]
                        last_user[s] = (r, m, step, seg[1] - 1 + dn)
                else:
                    walk(pe, [seg], handler, pre)

    return nc


_OUTS = [((16, 256, 256), 'float32')]


def kernel(**inputs):
    import numpy as _np
    import concourse.bacc as _bacc
    from concourse import mybir as _mybir
    from concourse.bass_utils import run_bass_kernel_spmd as _run

    nc = _bacc.Bacc("TRN2", target_bir_lowering=False, num_devices=1)
    arrays, aps = {}, {}
    for name, value in inputs.items():
        a = _np.ascontiguousarray(value)
        arrays[f"in_{name}_dram"] = a
        aps[name] = nc.dram_tensor(f"in_{name}_dram", a.shape, _mybir.dt.from_np(a.dtype), kind="ExternalInput").ap()
    out = nc.dram_tensor("out_0_dram", _OUTS[0][0], _mybir.dt.from_np(_np.dtype(_OUTS[0][1])),
                         kind="ExternalOutput").ap()
    build_program(nc, aps, out)
    r = _run(nc, [arrays], core_ids=[0])
    return r.results[0]["out_0_dram"]
```

```python
from contextlib import ExitStack

import numpy as np

import concourse.bass as bass
from concourse import mybir

F32 = mybir.dt.float32
F32R = mybir.dt.float32r
ALU = mybir.AluOpType
ACT = mybir.ActivationFunctionType
AX = mybir.AxisListType

P = 128
D = 256
KC = D // P
H = 16
HD = D // H
NT = 256
TT = NT // P
S = 120
MLP = 4 * D
MC = MLP // P
QUAD = 4
SLOT = 1024
BANK = 512
SLOTS = 3
SCALE = HD ** -0.5
LO_ROW = 64
MAX_ROW = 96
STACK_ROWS = MAX_ROW + 2

FULL = (True, False, True, True)
EPS = (1e-6, 1e-5, 1e-6, 1e-6)
CTX_LN = (False, True, False, True)
LAYERS = 4


def head_of(j):
    return (j % 2) * (H // 2) + j // 2


OFF_PE = ("ld", "N", "NC", "A", "AC", "X0", "X1", "ST")


def role_steps(layer, role):
    if not FULL[layer]:
        return [] if role == "E" else [w[2:] for who in "YX" for w in HALF if w[0] == who and w[2:] not in OFF_PE]
    words = [word.split(".") for word in BODY]
    return [step for who in (role + "+", role) for r, step in words if r == who and step not in OFF_PE]


COST = {"LN": 0.4, "QK": 3.5, "V": 1.8, "C": 0.2, "KV": 2.0, "Q": 1.8, "S": 0.45, "M": 0.1, "T": 0.45,
        "PV": 0.55, "O1": 0.9, "O2": 0.4, "PR": 1.8, "H": 3.5, "F20": 3.5, "F21": 3.5, "ld": 0.0, "ST": 0.0, "N": 0.0,
        "NC": 0.0, "X0": 0.0, "X1": 0.0, "A": 0.0, "AC": 0.0}


def cost(step):
    return COST[step] if step in COST else COST[step.rstrip("01234567")]


def merge(a, b):
    total = [sum(cost(e[2]) for e in x) or 1 for x in (a, b)]
    at = [0.0, 0.0]
    out, i, j = [], 0, 0
    while i < len(a) or j < len(b):
        if j >= len(b) or (i < len(a) and at[0] / total[0] <= at[1] / total[1]):
            out.append(a[i])
            at[0] += cost(a[i][2])
            i += 1
        else:
            out.append(b[j])
            at[1] += cost(b[j][2])
            j += 1
    return out


BODY = """
F.S0 G.T0 G+.ld F.S1 G.T1 G.PV0 F.S2 G.T2 G.PV1 F.S3 F.X0 G.T3 F.S5 G.PV2 G.PV3 F.M0 F.S4 F.S6 G.O1 F.T0
E.ld F.S7 F.X1 G.O2 F.T1 F.PV0 G.PR F.M1 G+.N E.N F.T2 G+.NC F.PV1 E.A F+.ld G+.A G+.AC F.T3 F.PV2 F.T4
F.PV3 F.T5 F+.N F.PV4 G+.C G+.LN F.T6 F+.A F.PV5 F.T7 E.LN G+.Q G+.KV F.PV6 F.PV7 E.H0 F.O1 E.H1 F.O2 G+.S0
F.PR F+.LN G+.S1 G+.X0 F+.QK F+.V E.F20 G+.M0 G+.S2 G+.S3 G+.X1 E.F21 G+.M1 E.ST
""".split()
AHEAD = {"F+": 3, "F": 2, "G+": 1, "G": 0, "E": 0}

HALF = """
X.M1 X.M0 Y.C Y.LN Y.KV X.T0 Y.Q X.T1 X.PV0 X.T2 X.PV1 X.T3 X.PV2 X.PV3 X.O1 X.O2 X.PR Y.S0 Y.S2 Y.S3 Y.X1
Y.S1 Y.X0
""".split()
EARLY_AT = 15


def turn(layer, i, nb):
    out = []
    for word in BODY:
        role, step = word.split(".")
        n = i + AHEAD[role]
        if 0 <= n < nb:
            out.append((role[0], layer, step, n))
        elif n >= nb and layer == 2:
            out.append((role[0], 3, step, n - nb))
    return out


def entries(role, layer, steps, n):
    return [(role, layer, s, n) for s in steps]


def segments(nb):
    pairs = nb // 2
    out = []

    def run(steps):
        out.append(("run", steps))

    def loop(count, steps):
        if count > 0:
            out.append(("loop", count, steps))

    def full_turns(layer):
        run(turn(layer, 0, nb))
        loop(nb - 4, turn(layer, 1, nb))
        if layer + 1 < LAYERS:
            out.append(("weights_f", layer + 1))
        run(turn(layer, nb - 3, nb) + (early("F", 0) + apply("F", 0) if layer == 0 else []))

    def early(role, n):
        return entries(role, 1, ("ld", "N", "NC"), n)

    def apply(role, n):
        return entries(role, 1, ("A", "AC"), n)

    def half(x, xn, y, yn):
        steps = []
        for at, word in enumerate(HALF):
            if xn is not None and xn + 1 < pairs:
                if at == EARLY_AT:
                    steps += early(x, xn + 1)
                elif at == EARLY_AT + 2:
                    steps += apply(x, xn + 1)
            who, n = (x, xn) if word[0] == "X" else (y, yn)
            if n is not None and n < pairs:
                steps.append((who, 1, word[2:], n))
        return steps + ([(x, 1, "ST", xn)] if xn is not None else [])

    out += [("rows", 0), ("pre", 0), ("weights_f", 0)]
    run(turn(0, -3, nb)[:3])
    out += [("gates", 0), ("rows", 1)]
    run(turn(0, -3, nb)[3:])
    out += [("weights_g", 0), ("pre", 1), ("gates", 1), ("rows", 2), ("weights_e", 0)]
    run(turn(0, -2, nb))
    out += [("pre", 2), ("gates", 2), ("rows", 3)]
    run(turn(0, -1, nb))
    out += [("pre", 3), ("gates", 3)]
    full_turns(0)
    run(turn(0, nb - 2, nb))
    run(merge(turn(0, nb - 1, nb), half(None, None, "F", 0)) + early("G", 0) + apply("G", 0))
    out.append(("weights_g", 2))
    out.append(("weights_e", 2))
    run(half("F", 0, "G", 0) + half("G", 0, "F", 1))
    loop(pairs - 3, half("F", 1, "G", 1) + half("G", 1, "F", 2))
    if pairs > 2:
        run(half("F", pairs - 2, "G", pairs - 2) + half("G", pairs - 2, "F", pairs - 1))
    run(half("F", pairs - 1, "G", pairs - 1) + turn(2, -3, nb)[:3])
    out.append(("weights_f", 2))
    run(merge(half("G", pairs - 1, None, None), turn(2, -3, nb)[3:] + turn(2, -2, nb)))
    run(turn(2, -1, nb))
    full_turns(2)
    run(turn(2, nb - 2, nb))
    out.append(("weights_g", 3))
    run(turn(2, nb - 1, nb))
    out.append(("weights_e", 3))
    full_turns(3)
    for i in (nb - 2, nb - 1):
        run(turn(3, i, nb))
    return out


class Signal:

    def __init__(self, sem, steps, batches, by=1):
        self.sem, self.by = sem, by
        self.steps = [list(steps(layer)) for layer in range(LAYERS)]
        self.base = [0]
        for layer in range(LAYERS):
            self.base.append(self.base[-1] + by * len(self.steps[layer]) * batches[layer])

    def after(self, layer, step, n, nth=-1):
        at = [i for i, s in enumerate(self.steps[layer]) if s == step][nth]
        return n * (self.by * len(self.steps[layer])) + (self.base[layer] + self.by * (at + 1))

    def before(self, layer, n):
        if not self.steps[layer]:
            return self.base[layer]
        return n * (self.by * len(self.steps[layer])) + self.base[layer]

    def wait_before(self, eng, layer, n):
        value = self.before(layer, n)
        if not isinstance(value, int) or value > 0:
            eng.wait_ge(self.sem, value)


def numbered(name, steps):
    return [s for s in steps if s.startswith(name) and s[len(name):].isdigit()]


def places(steps):
    users = [e[:3] for e in steps if e[2] not in OFF_PE and not e[2].startswith("PV")]
    return {e: i % SLOTS for i, e in enumerate(users)}


def walk(eng, program, handler, at=None):
    for seg in program:
        if seg[0] not in ("run", "loop"):
            if at and seg[0] in at:
                at[seg[0]](seg[1])
        elif seg[0] == "run":
            place = places(seg[1])
            for role, layer, step, n in seg[1]:
                handler(role, layer, step, n, False, place.get((role, layer, step)))
        elif seg[1] > 0:
            place = places(seg[2])
            with eng.Fori(0, seg[1]) as it:
                for role, layer, step, dn in seg[2]:
                    handler(role, layer, step, it + dn, True, place.get((role, layer, step)))


def build_program(nc, a, out, nb=16):
    program = segments(nb)
    ctx = ExitStack()
    with ctx:
        def sb(name, shape, dt=F32):
            return ctx.enter_context(nc.sbuf_tensor(name, shape, dt))

        def scratch(name, shape):
            return nc.dram_tensor(name, shape, F32, kind="Internal").ap()

        x_in = [a["x"]] + [scratch(f"x_after_{m}", [nb, NT, D]) for m in range(LAYERS - 1)]
        x_out = x_in[1:] + [out]
        gate_rows = [scratch(f"gate_rows_{m}", [nb, 4, D]) if FULL[m] else None for m in range(LAYERS)]
        q_parts_dram = {r: scratch(f"q_parts_{r}", [P, 2, KC * NT]) for r in "FG"}
        k_parts_dram = {r: scratch(f"k_parts_{r}", [P, 2, KC * NT]) for r in "F"}
        kc_parts_dram = {r: scratch(f"kc_parts_{r}", [P, 2, KC * S]) for r in "FG"}

        ident = sb("ident", [P, P])
        w_qkv = sb("w_qkv", [P, KC, 3 * D])
        w_proj = [sb(f"w_proj{i}", [P, KC, D]) for i in range(2)]
        w_q2 = sb("w_q2", [P, KC, D])
        w_kv2 = sb("w_kv2", [P, KC, 2 * D])
        w_cp = sb("w_cp", [P, KC, D])
        w_fc1 = sb("w_fc1", [P, KC, MLP])
        w_fc2 = sb("w_fc2", [P, MC, D])
        w_ada = sb("w_ada", [P, KC, 6 * D])
        rows = sb("rows", [36, P])
        cols = [sb(f"cols{i}", [P, 36]) for i in range(LAYERS)]
        mods = [sb(f"mods{i}", [P, nb, 8]) for i in range(LAYERS)]
        v_bias = [sb(f"v_bias{i}", [P, D]) for i in range(2)]
        vc_bias = [sb(f"vc_bias{i}", [P, D]) for i in range(2)]
        cp_bias = [sb(f"cp_bias{i}", [P, D]) for i in range(2)]
        cond = sb("cond", [nb, D])
        cond_e = sb("cond_e", [nb, D])
        silu_t = sb("silu_t", [P, KC, nb])

        x = {r: sb(f"x_{r}", [P, TT, D]) for r in "FGE"}
        x_new = {r: sb(f"x_new_{r}", [P, TT, D]) for r in "FE"}
        x_new["G"] = x_new["E"]
        x_mid = x_new["F"]
        x_stage = {"F": sb("x_stage", [P, TT, D]), "G": x["E"]}
        x_hat = {r: sb(f"x_hat_{r}", [P, TT, D]) for r in "FGE"}
        x_t = {r: sb(f"x_t_{r}", [P, KC, NT]) for r in "FGE"}
        stats = {r: sb(f"stats_{r}", [P, TT, 6]) for r in "FGE"}
        mean_var = {r: sb(f"mean_var_{r}", [P, TT, 2]) for r in "FGE"}
        var_eps = {r: sb(f"var_eps_{r}", [P, TT]) for r in "FGE"}
        rstd = {r: sb(f"rstd_{r}", [P, TT]) for r in "FGE"}
        c_stats = {r: sb(f"c_stats_{r}", [P, 6]) for r in "FG"}
        c_mean_var = {r: sb(f"c_mean_var_{r}", [P, 2]) for r in "FG"}
        c_var_eps = {r: sb(f"c_var_eps_{r}", [P, 1]) for r in "FG"}
        c_rstd = {r: sb(f"c_rstd_{r}", [P, 1]) for r in "FG"}
        wait_mark = sb("wait_mark", [1, 1])
        minus_half = sb("minus_half", [P, TT])
        mod_now = {r: sb(f"mod_now_{r}", [P, 8]) for r in "FGE"}
        gate_now = {r: sb(f"gate_now_{r}", [P, 2, D]) for r in "FE"}
        gated = {r: sb(f"gated_{r}", [P, TT, D]) for r in "FE"}
        context = {r: sb(f"context_{r}", [P, D]) for r in "FG"}
        context_hat = {r: sb(f"context_hat_{r}", [P, D]) for r in "FG"}
        context_t = {r: sb(f"context_t_{r}", [P, KC, S]) for r in "FG"}
        q_parts = {r: sb(f"q_parts_sb_{r}", [P, 2, KC, NT]) for r in "FG"}
        k_parts = sb("k_parts_sb", [P, 2, KC, NT])
        kc_parts = {r: sb(f"kc_parts_sb_{r}", [P, 2, KC, S]) for r in "FG"}
        q_stack = {r: sb(f"q_stack_{r}", [P, H, NT]) for r in "FG"}
        k_stack = {"F": sb("k_stack_F", [P, H * NT]), "G": sb("k_stack_G", [P, H * S])}
        v_self = sb("v_self", [P, TT, H, 2 * HD])
        v_ctx = {r: sb(f"v_ctx_{r}", [P, H, 2 * HD]) for r in "FG"}
        row_max = {r: sb(f"row_max_{r}", [P, TT, H]) for r in "FG"}
        max_parts = {r: sb(f"max_parts_{r}", [P, TT, 2, 2, H // 2]) for r in "FG"}
        max_t = {r: [sb(f"max_t_{r}{h}", [H, NT]) for h in range(2)] for r in "FG"}
        probs = {r: [sb(f"probs_{r}{i}", [P, QUAD, NT]) for i in range(2)] for r in "FG"}
        o_raw = {r: q_parts[r][:, :, :, :].rearrange("p e m w -> p (e m) w") for r in "FG"}
        r_den = {r: sb(f"r_den_{r}", [P, TT, H]) for r in "FG"}
        o_norm = {"F": sb("o_norm_F", [P, TT, D]), "G": x_hat["G"]}
        o_t = x_t
        h_t = sb("h_t", [P, MC, NT])
        bias_rows = probs["G"][0]
        gate_sb = probs["G"][1]

        slot = [ctx.enter_context(nc.psum_tensor(f"slot{i}", [P, SLOT], F32)) for i in range(SLOTS)]
        o_acc = {r: ctx.enter_context(nc.psum_tensor(f"o_acc_{r}", [P, BANK], F32)) for r in "FG"}

        pre_bank = o_acc["G"]

        def batches(role):
            return [(nb if FULL[m] else nb // 2) for m in range(LAYERS)]

        def signal(name, steps, by=1):
            made = {}
            for r in "FGE":
                used = any(steps(m, r) for m in range(LAYERS))
                made[r] = Signal(ctx.enter_context(nc.semaphore(f"{name}_{r}")) if used else None,
                                 lambda m, r=r: steps(m, r), batches(r), by)
            return made

        def only(*names):
            return lambda m, r: [s for s in role_steps(m, r) if s in names]

        def norms(m, r):
            if not FULL[m]:
                return [] if r == "E" else ["N", "NC"]
            return ["N", "NC"] if r == "G" and CTX_LN[m] else ["N"]

        def loads_x(m, r):
            return r == "F" or (r == "G" and not FULL[m])

        def out_banks(m, r):
            if r == "E":
                return []
            return ["PV3", "PV7"] if FULL[m] and r == "F" else ["PV1", "PV3"]

        psum_ready = signal("psum_ready", lambda m, r: role_steps(m, r))
        x_t_ready = signal("x_t_ready", only("LN"))
        context_t_ready = signal("context_t_ready", only("C"))
        hi_ready = signal("hi_ready", only("QK", "Q", "KV"))
        max_t_ready = signal("max_t_ready", lambda m, r: numbered("M", role_steps(m, r)))
        probs_ready = signal("probs_ready", lambda m, r: numbered("T", role_steps(m, r)))
        o_raw_ready = signal("o_raw_ready", out_banks)
        o_t_ready = signal("o_t_ready", only("O2"))
        h_ready = signal("h_ready", only("H0", "H1"))
        mod_ready = signal("mod_ready", lambda m, r: [] if r == ("G" if FULL[m] else "E") else ["ld"])
        stats_ready = signal("stats_ready", norms)
        mean_ready = signal("mean_ready", norms)
        var_ready = signal("var_ready", norms)
        x_hat_ready = signal("x_hat_ready", norms)
        lo_ready = signal("lo_ready", only("QK", "Q", "KV"))
        v_ready = signal("v_ready", only("V", "KV"))
        row_max_ready = signal("row_max_ready", lambda m, r: numbered("S", role_steps(m, r)))
        max_hi_ready = signal("max_hi_ready", lambda m, r: numbered("M", role_steps(m, r)))
        max_parts_ready = signal("max_parts_ready", lambda m, r: numbered("M", role_steps(m, r)))
        r_den_ready = signal("r_den_ready", only("O1"))
        o_norm_ready = signal("o_norm_ready", only("O1"))
        gated_ready = signal("gated_ready", lambda m, r: {"F": ["PR"], "G": [], "E": ["F20", "F21"]}[r] if FULL[m] else [])
        x_cross_ready = signal("x_cross_ready", lambda m, r: ["PR"] if FULL[m] and r == "G" else [])
        rstd_ready = signal("rstd_ready", norms)
        x_biased = signal("x_biased", lambda m, r: [s for s in norms(m, r) if s == "N"])
        x_mid_ready = signal("x_mid_ready", lambda m, r: ["PR"] if FULL[m] and r == "F" else [])
        x_new_ready = signal("x_new_ready", lambda m, r: (["F21"] if r == "E" else []) if FULL[m] else
                             ([] if r == "E" else ["PR"]))
        x_loaded = signal("x_loaded", lambda m, r: ["ld"] if loads_x(m, r) else [], 16)
        gate_step = {"F": "LN", "E": "ld"}
        gate_loaded = signal("gate_loaded", lambda m, r: [gate_step[r]] if FULL[m] and r in gate_step else [], 16)
        context_loaded = signal("context_loaded", lambda m, r: ["ld"] if r == "G" or (r == "F" and not FULL[m]) else [], 16)
        q_stored = [signal(f"q_{part}_stored", only("QK", "Q"), 16) for part in ("high", "low")]
        k_stored = [signal(f"k_{part}_stored", only("QK", "KV"), 16) for part in ("high", "low")]
        q_stack_loaded = signal("q_stack_loaded", only("QK", "Q"), 48)
        k_stack_loaded = signal("k_stack_loaded", only("QK", "KV"), 48)
        max_row_loaded = [signal(f"max_row_loaded{h}", only(f"M{h}"), 16) for h in range(2)]
        x_stored = signal("x_stored", lambda m, r: ["ST"] if (r == "E") == FULL[m] else [], 16)

        cond_loaded = ctx.enter_context(nc.semaphore("cond_loaded"))
        silu_step = ctx.enter_context(nc.semaphore("silu_step"))
        silu_exp = ctx.enter_context(nc.semaphore("silu_exp"))
        silu_psum = ctx.enter_context(nc.semaphore("silu_psum"))
        const_ready = ctx.enter_context(nc.semaphore("const_ready"))
        ident_zero = ctx.enter_context(nc.semaphore("ident_zero"))
        ident_ready = ctx.enter_context(nc.semaphore("ident_ready"))
        rows_loaded = ctx.enter_context(nc.semaphore("rows_loaded"))
        ada_loaded = ctx.enter_context(nc.semaphore("ada_loaded"))
        bias_spread = ctx.enter_context(nc.semaphore("bias_spread"))
        gate_bias_loaded = ctx.enter_context(nc.semaphore("gate_bias_loaded"))
        wf_loaded = ctx.enter_context(nc.semaphore("wf_loaded"))
        wg_loaded = ctx.enter_context(nc.semaphore("wg_loaded"))
        we_loaded = ctx.enter_context(nc.semaphore("we_loaded"))
        pre_psum = ctx.enter_context(nc.semaphore("pre_psum"))
        cols_ready = ctx.enter_context(nc.semaphore("cols_ready"))
        mods_ready = ctx.enter_context(nc.semaphore("mods_ready"))
        gate_ready = ctx.enter_context(nc.semaphore("gate_ready"))
        gate_times_bias = ctx.enter_context(nc.semaphore("gate_times_bias"))
        gate_stored = ctx.enter_context(nc.semaphore("gate_stored"))

        CONSTS = {"F": 1 + 3 + 5, "G": 1 + 3 + 2 * 5}

        def name(m, full_names, l1):
            return a[{0: f"L0_xcond_{full_names[0]}", 2: f"L2_xcond_{full_names[1]}",
                      3: f"L3_xcond_{full_names[2]}"}[m] if m != 1 else f"L1_xcond_{l1}"]

        def w(m, key):
            table = {
                "ada_w": ("adaln_w", "ada_w", "W_mod"), "ada_b": ("adaln_b", "ada_b", "b_mod"),
                "qkv_w": ("qkv_w", "qkv_w", "W_qkv"), "qkv_b": ("qkv_b", "qkv_b", "b_qkv"),
                "proj_w": ("sa_proj_w", "self_o_w", "W_proj"), "proj_b": ("sa_proj_b", "self_o_b", "b_proj"),
                "q_w": ("q_w", "q_w", "W_qc"), "q_b": ("q_b", "q_b", "b_qc"),
                "kv_w": ("kv_w", "kv_w", "W_kvc"), "kv_b": ("kv_b", "kv_b", "b_kvc"),
                "cp_w": ("ca_proj_w", "cross_o_w", "W_cproj"), "cp_b": ("ca_proj_b", "cross_o_b", "b_cproj"),
                "fc1_w": ("fc1_w", "mlp_w1", "W_mlp1"), "fc1_b": ("fc1_b", "mlp_b1", "b_mlp1"),
                "fc2_w": ("fc2_w", "mlp_w2", "W_mlp2"), "fc2_b": ("fc2_b", "mlp_b2", "b_mlp2"),
            }
            return name(m, table[key], None)

        l1 = {k: a[f"L1_xcond_{k}"] for k in ("Wq", "bq", "Wkv", "bkv", "Wp", "bp", "Wss_q", "bss_q", "Wss_kv",
                                              "bss_kv")}
        COL = {"ada": 0, "qkv": 12, "q": 18, "kv": 20, "fc1": 24, "gamma": 32, "beta": 34} 
        COL1 = {"ada": 0, "q": 8, "kv": 10}

        def row_vectors(m):
            if not FULL[m]:
                return [(0, l1["bss_q"]), (4, l1["bss_kv"]), (COL1["q"], l1["bq"]), (COL1["kv"], l1["bkv"])]
            v = [(COL["ada"], w(m, "ada_b")), (COL["qkv"], w(m, "qkv_b")), (COL["q"], w(m, "q_b")),
                 (COL["kv"], w(m, "kv_b")), (COL["fc1"], w(m, "fc1_b"))]
            if m == 2:
                v += [(COL["gamma"], a["L2_xcond_norm2_g"]), (COL["beta"], a["L2_xcond_norm2_b"])]
            return v

        def n_rows(m):
            return max(at + v.shape[0] // P for at, v in row_vectors(m))

        def col(m, key, i):
            at = (COL if FULL[m] else COL1)[key] + i
            return cols[m][:, at:at + 1]

        def mod_sources(m):
            starts = (256, 0, 1024, 768) if FULL[m] else (0, 256, 512, 768)
            return [s + P * c for s in starts for c in range(KC)]

        def rows_done(m):
            return 16 * sum(len(row_vectors(i)) for i in range(m + 1))

        ADA_DMAS = [1, 2, 1, 1]

        def ada_done(m):
            return 16 * sum(ADA_DMAS[:m + 1])

        SPREAD = [3, 2, 3, 3]

        def spread_done(m):
            return 16 * sum(SPREAD[:m + 1])

        WF_DMAS = [2, 3, 2, 2]

        def wf_done(m):
            return 16 * sum(WF_DMAS[:m + 1])

        PRE_PSUM = [3, 2, 3, 3]

        def pre_done(m, k):
            return sum(PRE_PSUM[:m]) + k

        FULL_BEFORE = [sum(FULL[:m]) for m in range(LAYERS + 1)]

        def stack_source(dram, part, width):
            return dram.rearrange("(h d) e w -> e d h w", d=HD)[part]

        def hat_of(r, m):
            return x_hat["E" if r == "G" and not FULL[m] else r]

        def is_self(m, r):
            return FULL[m] and r == "F"

        def parts_of(r, m, step, here):
            for c in range(KC):
                if step == "QK":
                    yield slot[here][:, c * NT:(c + 1) * NT], col(m, "qkv", c), q_parts[r], c
                    yield slot[here][:, BANK + c * NT:BANK + (c + 1) * NT], col(m, "qkv", KC + c), k_parts, c
                elif step == "Q":
                    yield slot[here][:, c * NT:(c + 1) * NT], col(m, "q", c), q_parts[r], c
                else:
                    yield slot[here][:, c * S:(c + 1) * S], col(m, "kv", c), kc_parts[r], c

        block = ctx.enter_context(nc.Block())

        @block.sync
        def _(sp):
            def weight(dst, src, sem, chunks=KC):
                sp.dma_start(dst, src.rearrange("(k p) n -> p k n", k=chunks)).then_inc(sem, 16)

            def load_ada(m):
                if FULL[m]:
                    weight(w_ada[:, :, :], w(m, "ada_w"), ada_loaded)
                else:
                    weight(w_ada[:, :, 0:2 * D], l1["Wss_q"], ada_loaded)
                    weight(w_ada[:, :, 2 * D:4 * D], l1["Wss_kv"], ada_loaded)

            def load_rows(m):
                if m == 0:
                    sp.dma_start(cond[:, :], a["cond_1024"][0:nb, :]).then_inc(cond_loaded, 16)
                else:
                    sp.wait_ge(pre_psum, pre_done(m - 1, 1))
                for at, v in row_vectors(m):
                    sp.dma_start(rows[at:at + v.shape[0] // P, :], v.rearrange("(n p) -> n p", p=P))\
                        .then_inc(rows_loaded, 16)
                if m == 0:
                    load_ada(0)
                if FULL[m]:
                    if FULL_BEFORE[m] > 0:
                        sp.wait_ge(gate_times_bias, FULL_BEFORE[m])
                    ab = w(m, "ada_b").rearrange("(g d) -> g d", d=D)
                    for i, v in enumerate((ab[2], w(m, "proj_b"), ab[5], w(m, "fc2_b"))):
                        sp.dma_start(bias_rows[0:nb, i, :], v.unsqueeze(0).to_broadcast([nb, D]))\
                            .then_inc(gate_bias_loaded, 16)

            def gates(m):
                if FULL[m]:
                    sp.wait_ge(gate_times_bias, FULL_BEFORE[m] + 1)
                    sp.dma_start(gate_rows[m], gate_sb[0:nb, :, :]).then_inc(gate_stored, 16)
                if m + 1 < LAYERS:
                    sp.wait_ge(pre_psum, pre_done(m, PRE_PSUM[m]))
                    load_ada(m + 1)

            def weights_f(m):
                if m > 0:
                    if FULL[m - 1]:
                        sp.wait_ge(psum_ready["F"].sem, psum_ready["F"].after(m - 1, "V", nb - 1))
                    else:
                        for r in "FG":
                            last = max(("Q", "KV"), key=role_steps(m - 1, r).index)
                            sp.wait_ge(psum_ready[r].sem, psum_ready[r].after(m - 1, last, nb // 2 - 1))
                if FULL[m]:
                    weight(w_qkv[:, :, :], w(m, "qkv_w"), wf_loaded)
                    weight(w_proj[m % 2][:, :, :], w(m, "proj_w"), wf_loaded)
                    spread = ((v_bias, w(m, "qkv_b")[2 * D:3 * D]), (vc_bias, w(m, "kv_b")[D:2 * D]),
                              (cp_bias, w(m, "cp_b")))
                else:
                    weight(w_qkv[:, :, 0:D], l1["Wq"], wf_loaded)
                    weight(w_qkv[:, :, D:3 * D], l1["Wkv"], wf_loaded)
                    weight(w_proj[m % 2][:, :, :], l1["Wp"], wf_loaded)
                    spread = ((vc_bias, l1["bkv"][D:2 * D]), (cp_bias, l1["bp"]))
                for tile, v in spread:
                    sp.dma_start(tile[m % 2][:, :], v.unsqueeze(0).to_broadcast([P, D])).then_inc(bias_spread, 16)

            def weights_g(m):
                if m > 0:
                    prev = 0 if m == 2 else m - 1
                    last = max(("Q", "KV"), key=role_steps(prev, "G").index)
                    sp.wait_ge(psum_ready["G"].sem, psum_ready["G"].after(prev, last, nb - 1))
                weight(w_kv2[:, :, :], w(m, "kv_w"), wg_loaded)
                weight(w_q2[:, :, :], w(m, "q_w"), wg_loaded)

            def weights_e(m):
                if m > 0:
                    prev = 0 if m == 2 else m - 1
                    sp.wait_ge(psum_ready["G"].sem, psum_ready["G"].after(prev, "PR", nb - 1))
                    sp.wait_ge(psum_ready["E"].sem, psum_ready["E"].after(prev, "F21", nb - 1))
                weight(w_cp[:, :, :], w(m, "cp_w"), we_loaded)
                weight(w_fc1[:, :, :], w(m, "fc1_w"), we_loaded)
                weight(w_fc2[:, :, :], w(m, "fc2_w"), we_loaded, MC)

            def batch(r, m, n):
                return n if FULL[m] else 2 * n + (r == "G")

            def handler(r, m, step, n, looping, here):
                b = batch(r, m, n)
                if FULL[m] and step == gate_step.get(r):
                    g = 0 if r == "F" else 2
                    gate_src = gate_rows[m][bass.ds(b, 1), g:g + 2, :].to_broadcast([P, 2, D])
                    (x_mid_ready if r == "F" else x_new_ready)[r].wait_before(sp, m, n)
                    sp.wait_ge(gate_stored, 16 * (FULL_BEFORE[m] + 1))
                    sp.dma_start(gate_now[r][:, :, :], gate_src).then_inc(gate_loaded[r].sem, 16)
                if step == "ld":
                    if loads_x(m, r):
                        x_src = x_in[m][bass.ds(b, 1)].rearrange("o (t p) d -> p (o t) d", p=P)
                        x_biased[r].wait_before(sp, m, n)
                        if r == "G":
                            x_new_ready["E"].wait_before(sp, m, 0)
                        if m > 0:
                            if looping:
                                for q in "FGE":
                                    x_stored[q].wait_before(sp, m, 0)
                            else:
                                q = "E" if FULL[m - 1] else "FG"[b % 2]
                                sp.wait_ge(x_stored[q].sem,
                                           x_stored[q].after(m - 1, "ST", b if FULL[m - 1] else b // 2))
                        sp.dma_start(x_stage[r][:, :, :], x_src).then_inc(x_loaded[r].sem, 16)
                    if r == "G" or (r == "F" and not FULL[m]):
                        context_src = a["ctx_1024"][bass.ds(b, 1)].rearrange("o s d -> (o s) d")
                        (x_hat_ready if CTX_LN[m] else context_t_ready)[r].wait_before(sp, m, n)
                        sp.dma_start(context[r][0:S, :], context_src).then_inc(context_loaded[r].sem, 16)
                if step in ("QK", "Q", "KV"):
                    for part, ready in enumerate((hi_ready, lo_ready)):
                        sp.wait_ge(ready[r].sem, ready[r].after(m, step, n))
                        if step in ("QK", "Q"):
                            sp.dma_start(q_parts_dram[r][:, part], q_parts[r][:, part, :, :].rearrange("p m w -> p (m w)"))\
                                .then_inc(q_stored[part][r].sem, 16)
                        if step == "QK":
                            sp.dma_start(k_parts_dram["F"][:, part], k_parts[:, part, :, :].rearrange("p m w -> p (m w)"))\
                                .then_inc(k_stored[part][r].sem, 16)
                        if step == "KV":
                            sp.dma_start(kc_parts_dram[r][:, part],
                                         kc_parts[r][:, part, :, :].rearrange("p m w -> p (m w)"))\
                                .then_inc(k_stored[part][r].sem, 16)
                    if step != "QK" and step != max(("Q", "KV"), key=role_steps(m, r).index):
                        return
                    if not looping:
                        sp.wait_ge(const_ready, CONSTS[r])

                    q_step, k_step = ("QK", "QK") if step == "QK" else ("Q", "KV")
                    width, k_dram = (NT, k_parts_dram["F"]) if step == "QK" else (S, kc_parts_dram[r])
                    for part, q_rows, k_rows in ((0, (0, HD), (0, LO_ROW)), (1, (LO_ROW,), (HD,))):
                        sp.wait_ge(q_stored[part][r].sem, q_stored[part][r].after(m, q_step, n))
                        for row in q_rows:
                            sp.dma_start(q_stack[r][row:row + HD, :, :].rearrange("p (h m) w -> p h (m w)", m=KC),
                                         stack_source(q_parts_dram[r], part, NT)).then_inc(q_stack_loaded[r].sem, 16)
                        sp.wait_ge(k_stored[part][r].sem, k_stored[part][r].after(m, k_step, n))
                        for row in k_rows:
                            sp.dma_start(k_stack[r][row:row + HD, 0:H * width].rearrange("p (h w) -> p h w", h=H // 2),
                                         stack_source(k_dram, part, width)).then_inc(k_stack_loaded[r].sem, 16)
                elif step in ("M0", "M1"):
                    h = int(step[1])
                    sp.wait_ge(max_t_ready[r].sem, max_t_ready[r].after(m, step, n))
                    sp.dma_start(q_stack[r][MAX_ROW:MAX_ROW + 2, h * 8:h * 8 + 8, :], max_t[r][h][:, :])\
                        .then_inc(max_row_loaded[h][r].sem, 16)
                elif step == "ST":
                    b = batch(r, m, n)
                    after = "F21" if FULL[m] else "PR"
                    dst = x_out[m][bass.ds(b, 1)].rearrange("o (t p) d -> p (o t) d", p=P)
                    sp.wait_ge(x_new_ready[r].sem, x_new_ready[r].after(m, after, n))
                    sp.dma_start(dst, x_new[r][:, :, :]).then_inc(x_stored[r].sem, 16)

            walk(sp, program, handler, {"rows": load_rows, "gates": gates, "weights_f": weights_f, "weights_g": weights_g,
                                        "weights_e": weights_e})
            for r in "FGE":
                sp.wait_ge(x_stored[r].sem, x_stored[r].base[LAYERS])

        @block.gpsimd
        def _(pool):
            nc.gpsimd.memset(ident[:, :], 0.0).then_inc(ident_zero, 1)
            pool.wait_ge(ident_zero, 1)
            nc.gpsimd.affine_select(out=ident[:, :], in_=ident[:, :], compare_op=ALU.not_equal, fill=1.0, base=0,
                                    pattern=[[-1, P]], channel_multiplier=1).then_inc(ident_ready, 1)
            nc.gpsimd.memset(minus_half[:, :], -0.5).then_inc(const_ready, 1)
            for t in (v_self, v_ctx["F"], v_ctx["G"]):
                flat = t[:, :, :, :].rearrange("p c h k -> p (c h) k") if len(t.shape) == 4 else t[:, :, :]
                nc.gpsimd.memset(flat[:, :, HD:2 * HD], 1.0).then_inc(const_ready, 1)

            def fill_stacks(r):
                done = CONSTS[r] - 5
                for t, lo, hi, value in ((q_stack[r][:, :, :], 32, 64, 0.0), (q_stack[r][:, :, :], 64, 96, 0.0),
                                         (k_stack[r][:, :], 32, 64, 0.0), (k_stack[r][:, :], 64, 96, 0.0),
                                         (k_stack[r][:, :], MAX_ROW, MAX_ROW + 2, 1.0)):
                    pool.wait_ge(const_ready, done)
                    nc.gpsimd.memset(t[lo:hi], value).then_inc(const_ready, 1)
                    done += 1
                pool.wait_ge(const_ready, done)

            fill_stacks("F")

            def pre(m):
                if m == 1:
                    pool.wait_ge(x_biased["F"].sem, x_biased["F"].after(0, "N", 0))
                    fill_stacks("G")

            def rstd_of(r, m, step, n):
                pool.wait_ge(var_ready[r].sem, var_ready[r].after(m, step, n))
                if step == "NC":
                    nc.gpsimd.tensor_tensor(c_rstd[r][0:S, :], c_var_eps[r][0:S, :], minus_half[0:S, 0:1], ALU.pow)\
                        .then_inc(rstd_ready[r].sem, 1)
                else:
                    nc.gpsimd.tensor_tensor(rstd[r][:, :], var_eps[r][:, :], minus_half[:, :], ALU.pow)\
                        .then_inc(rstd_ready[r].sem, 1)

            def pre_add(r, m, n):
                pool.wait_ge(x_hat_ready[r].sem, x_hat_ready[r].after(m, "N", n))
                x_mid_ready[r].wait_before(pool, m, n)
                x_new_ready[r].wait_before(pool, m, n)
                if r == "G":
                    x_hat_ready["E"].wait_before(pool, m, n if FULL[m] else 0)
                    x_biased["E"].wait_before(pool, m, n if FULL[m] else 0)
                if r == "E":
                    src = x["G"]
                else:
                    src = x_stage[r] if loads_x(m, r) else x_mid
                if FULL[m] and r != "G":
                    pool.wait_ge(gate_loaded[r].sem, gate_loaded[r].after(m, gate_step[r], n))
                    bias = gate_now[r][:, 1:2, :].to_broadcast([P, TT, D])
                else:
                    pool.wait_ge(bias_spread, spread_done(m))
                    bias = cp_bias[m % 2][:, :].unsqueeze(1).to_broadcast([P, TT, D])
                nc.gpsimd.tensor_tensor(x[r][:, :, :], src[:, :, :], bias, ALU.add).then_inc(x_biased[r].sem, 1)

            def handler(r, m, step, n, looping, here):
                if step == "N" or (step == "NC" and CTX_LN[m]):
                    rstd_of(r, m, step, n)
                if step == ("LN" if loads_x(m, r) else "A"):
                    pre_add(r, m, n)
                if step == "PR" and FULL[m] and r == "F":
                    pool.wait_ge(gated_ready[r].sem, gated_ready[r].after(m, "PR", n))
                    pool.wait_ge(x_biased[r].sem, x_biased[r].after(m, "N", n))
                    x_biased["G"].wait_before(pool, m, n)
                    if not looping:
                        x_stored["F"].wait_before(pool, m, 0)
                    nc.gpsimd.tensor_tensor(x_mid[:, :, :], x["F"][:, :, :], gated["F"][:, :, :], ALU.add)\
                        .then_inc(x_mid_ready[r].sem, 1)
                elif step == "F21":
                    pool.wait_ge(gated_ready[r].sem, gated_ready[r].after(m, "F21", n))
                    pool.wait_ge(x_biased[r].sem, x_biased[r].after(m, "N", n))
                    x_stored[r].wait_before(pool, m, n)
                    if not looping:
                        x_stored["G"].wait_before(pool, m, 0)
                    nc.gpsimd.tensor_tensor(x_new["E"][:, :, :], x["E"][:, :, :], gated["E"][:, :, :], ALU.add)\
                        .then_inc(x_new_ready[r].sem, 1)

            walk(pool, program, handler, {"pre": pre})

        @block.vector
        def _(dve):
            def pre(m):
                if m == 0:
                    dve.wait_ge(silu_exp, 1)
                    nc.vector.tensor_scalar(cond_e[:, :], cond_e[:, :], 1.0, None, ALU.add).then_inc(silu_step, 1)
                    dve.wait_ge(silu_step, 1)
                    nc.vector.reciprocal(cond_e[:, :], cond_e[:, :]).then_inc(silu_step, 1)
                    dve.wait_ge(silu_step, 2)
                    nc.vector.tensor_tensor(cond[:, :], cond[:, :], cond_e[:, :], ALU.mult).then_inc(silu_step, 1)
                    dve.wait_ge(silu_psum, 1)
                    nc.vector.tensor_copy(silu_t[:, :, :].rearrange("p k b -> p (k b)"), pre_bank[:, 0:KC * nb])\
                        .then_inc(silu_step, 1)
                dve.wait_ge(pre_psum, pre_done(m, 1))
                nc.vector.tensor_copy(cols[m][:, 0:n_rows(m)], pre_bank[:, 0:n_rows(m)])\
                    .then_inc(cols_ready, 1)
                dve.wait_ge(pre_psum, pre_done(m, 2))
                dve.wait_ge(cols_ready, m + 1)
                for j, src in enumerate(mod_sources(m)):
                    one = 1.0 if j % 4 < KC else 0.0
                    last = nc.vector.tensor_scalar(mods[m][:, :, j], pre_bank[:, 64 + nb * j:64 + nb * (j + 1)],
                                                   col(m, "ada", src // P), one, ALU.add, ALU.add)
                last.then_inc(mods_ready, 1)
                if FULL[m]:
                    dve.wait_ge(pre_psum, pre_done(m, 3))
                    dve.wait_ge(gate_bias_loaded, 64 * (FULL_BEFORE[m] + 1))
                    if FULL_BEFORE[m] > 0:
                        dve.wait_ge(gate_stored, 16 * FULL_BEFORE[m])
                    for g in range(2):
                        last = nc.vector.tensor_tensor(gate_sb[0:nb, 2 * g, :], pre_bank[0:nb, g * D:(g + 1) * D],
                                                       bias_rows[0:nb, 2 * g, :], ALU.add)
                    last.then_inc(gate_ready, 1)
                    dve.wait_ge(gate_ready, FULL_BEFORE[m] + 1)
                    for g in range(2):
                        last = nc.vector.tensor_tensor(gate_sb[0:nb, 2 * g + 1, :], gate_sb[0:nb, 2 * g, :],
                                                       bias_rows[0:nb, 2 * g + 1, :], ALU.mult)
                    last.then_inc(gate_times_bias, 1)

            def norm_tiles(r, m, step):
                if step == "NC":
                    return ([(context[r][0:S, :], context_hat[r][0:S, :])], c_stats[r][0:S, :].unsqueeze(1),
                            c_mean_var[r][0:S, :].unsqueeze(1), c_var_eps[r][0:S, :], c_rstd[r][0:S, :])
                x_src = x["G"] if r == "E" else x_stage[r] if loads_x(m, r) else x_mid
                return ([(x_src[:, t, :], hat_of(r, m)[:, t, :]) for t in range(TT)], stats[r][:, :, :],
                        mean_var[r][:, :, :], var_eps[r][:, :], rstd[r][:, :])

            def norm_statistics(r, m, step, n):
                tiles, st, mv, ve, _ = norm_tiles(r, m, step)
                if step == "NC":
                    dve.wait_ge(context_loaded[r].sem, context_loaded[r].after(m, "ld", n))
                elif r == "E":
                    dve.wait_ge(x_cross_ready["G"].sem, x_cross_ready["G"].after(m, "PR", n))
                elif FULL[m] and r == "G":
                    dve.wait_ge(x_mid_ready["F"].sem, x_mid_ready["F"].after(m, "PR", n))
                else:
                    dve.wait_ge(x_loaded[r].sem, x_loaded[r].after(m, "ld", n))
                for t, (src, _) in enumerate(tiles):
                    last = nc.vector.bn_stats(st[:, t, :], src)
                last.then_inc(stats_ready[r].sem, 1)
                dve.wait_ge(stats_ready[r].sem, stats_ready[r].after(m, step, n))
                nc.vector.memset(wait_mark[:, :], 0.0)
                for t in range(len(tiles)):
                    last = nc.vector.bn_aggr(mv[:, t, :], st[:, t, :])
                last.then_inc(mean_ready[r].sem, 1)
                dve.wait_ge(mean_ready[r].sem, mean_ready[r].after(m, step, n))
                nc.vector.tensor_scalar(ve, mv[:, :, 1], EPS[m], None, ALU.add).then_inc(var_ready[r].sem, 1)

            def norm_apply(r, m, step, n):
                tiles, _, mv, _, rs = norm_tiles(r, m, step)
                dve.wait_ge(rstd_ready[r].sem, rstd_ready[r].after(m, step, n))
                for t, (src, dst) in enumerate(tiles):
                    last = nc.vector.tensor_scalar(dst, src, mv[:, t, 0:1], rs[:, t:t + 1], ALU.subtract, ALU.mult)
                last.then_inc(x_hat_ready[r].sem, 1)

            def last_score_step(r, m, h):
                count = 4 if is_self(m, r) else 2
                return max((f"S{i}" for i in range(count * h, count * h + count)), key=role_steps(m, r).index)

            def low_parts(r, m, step, n, here):
                dve.wait_ge(hi_ready[r].sem, hi_ready[r].after(m, step, n))
                if step in ("QK", "Q"):
                    q_stored[1][r].wait_before(dve, m, n)
                if step in ("QK", "KV"):
                    k_stored[1][r].wait_before(dve, m, n)
                for src, bias, tile, c in parts_of(r, m, step, here):
                    last = nc.vector.scalar_tensor_tensor(out=tile[:, 1, c, :].bitcast(F32R), in0=src, scalar=bias,
                                                          in1=tile[:, 0, c, :], op0=ALU.add, op1=ALU.subtract)
                last.then_inc(lo_ready[r].sem, 1)

            def handler(r, m, step, n, looping, here):
                if step == "ld":
                    if not looping:
                        dve.wait_ge(mods_ready, m + 1)
                    x_t_ready[r].wait_before(dve, m, n)
                    context_t_ready[r].wait_before(dve, m, n)
                    if FULL[m] and r == "G":
                        return
                    b = n if FULL[m] else 2 * n + (r == "G")
                    nc.vector.tensor_copy(mod_now[r][:, :], mods[m][:, bass.ds(b, 1), :].rearrange("p o c -> p (o c)"))\
                        .then_inc(mod_ready[r].sem, 1)
                elif step == "N" or (step == "NC" and CTX_LN[m]):
                    norm_statistics(r, m, step, n)
                elif step == "A" or (step == "AC" and CTX_LN[m]):
                    norm_apply(r, m, {"A": "N", "AC": "NC"}[step], n)
                elif step in ("QK", "Q"):
                    low_parts(r, m, step, n, here)
                elif step == "KV":
                    low_parts(r, m, step, n, here)
                    if not looping:
                        dve.wait_ge(bias_spread, spread_done(m))
                    nc.vector.tensor_tensor(v_ctx[r][0:S, :, 0:HD],
                                            slot[here][0:S, BANK:BANK + D].rearrange("p (h d) -> p h d", d=HD),
                                            vc_bias[m % 2][0:S, :].rearrange("p (h d) -> p h d", d=HD), ALU.add)\
                        .then_inc(v_ready[r].sem, 1)
                elif step == "V":
                    dve.wait_ge(psum_ready[r].sem, psum_ready[r].after(m, step, n))
                    if not looping:
                        dve.wait_ge(bias_spread, spread_done(m))
                    for t in range(TT):
                        last = nc.vector.tensor_tensor(v_self[:, t, :, 0:HD],
                                                       slot[here][:, t * D:(t + 1) * D].rearrange("p (h d) -> p h d", d=HD),
                                                       v_bias[m % 2][:, :].rearrange("p (h d) -> p h d", d=HD), ALU.add)
                    last.then_inc(v_ready[r].sem, 1)
                elif step[0] == "S" and step[1:].isdigit():
                    u = int(step[1])
                    dve.wait_ge(psum_ready[r].sem, psum_ready[r].after(m, step, n))
                    if is_self(m, r):
                        heads, t = QUAD * (u // 2), u % 2
                        src = slot[here][:, :].rearrange("p (h k) -> p h k", h=QUAD)
                        dst = row_max[r][:, t, heads:heads + QUAD]
                    else:
                        heads, t = 2 * QUAD * (u // 2), u % 2
                        src = slot[here][:, :].rearrange("p (b w) -> p b w", b=2)[:, :, 0:QUAD * S]\
                            .rearrange("p b (h k) -> p b h k", h=QUAD)
                        dst = row_max[r][:, t, heads:heads + 2 * QUAD].rearrange("p (b h) -> p b h", b=2)
                    nc.vector.tensor_reduce(dst, src, AX.X, ALU.max).then_inc(row_max_ready[r].sem, 1)
                elif step in ("X0", "X1"):
                    h = int(step[1])
                    need = last_score_step(r, m, h)
                    src = row_max[r][:, :, 8 * h:8 * h + 8]
                    hi, lo = max_parts[r][:, :, h, 0, :], max_parts[r][:, :, h, 1, :]
                    dve.wait_ge(row_max_ready[r].sem, row_max_ready[r].after(m, need, n))
                    nc.vector.tensor_scalar(hi.bitcast(F32R), src, -1.0, None, ALU.mult)\
                        .then_inc(max_hi_ready[r].sem, 1)
                    dve.wait_ge(max_hi_ready[r].sem, max_hi_ready[r].after(m, f"M{h}", n))
                    nc.vector.scalar_tensor_tensor(out=lo.bitcast(F32R), in0=src, scalar=-1.0, in1=hi,
                                                   op0=ALU.mult, op1=ALU.subtract).then_inc(max_parts_ready[r].sem, 1)
                elif step == "O1":
                    dve.wait_ge(psum_ready[r].sem, psum_ready[r].after(m, step, n))
                    o = slot[here][:, :].rearrange("p (t j k) -> p t j k", t=TT, j=H)
                    nc.vector.reciprocal(r_den[r][:, :, :], o[:, :, :, HD]).then_inc(r_den_ready[r].sem, 1)
                    dve.wait_ge(r_den_ready[r].sem, r_den_ready[r].after(m, step, n))
                    for t in range(TT):
                        last = nc.vector.tensor_tensor(
                            o_norm[r][:, t, :].rearrange("p (e i d) -> p i e d", e=2, i=H // 2),
                            o[:, t, :, 0:HD].rearrange("p (i e) d -> p i e d", e=2),
                            r_den[r][:, t, :].rearrange("p (i e) -> p i e", e=2).unsqueeze(3)
                            .to_broadcast([P, H // 2, 2, HD]), ALU.mult)
                    last.then_inc(o_norm_ready[r].sem, 1)
                elif step == "PR":
                    dve.wait_ge(psum_ready[r].sem, psum_ready[r].after(m, step, n))
                    src = slot[here][:, 0:TT * D].rearrange("p (t d) -> p t d", t=TT)
                    if FULL[m] and r == "F":
                        dve.wait_ge(gate_loaded[r].sem, gate_loaded[r].after(m, gate_step[r], n))
                        nc.vector.tensor_tensor(gated[r][:, :, :], src, gate_now[r][:, 0:1, :].to_broadcast([P, TT, D]),
                                                ALU.mult).then_inc(gated_ready[r].sem, 1)
                    else:
                        dve.wait_ge(x_biased[r].sem, x_biased[r].after(m, "N", n))
                        if FULL[m]:
                            nc.vector.tensor_tensor(x[r][:, :, :], src, x[r][:, :, :], ALU.add)\
                                .then_inc(x_cross_ready[r].sem, 1)
                        else:
                            x_stored[r].wait_before(dve, m, n)
                            x_biased["G"].wait_before(dve, m, 0)
                            x_stored["E"].wait_before(dve, m, 0)
                            nc.vector.tensor_tensor(x_new[r][:, :, :], src, x[r][:, :, :], ALU.add)\
                                .then_inc(x_new_ready[r].sem, 1)
                elif step in ("F20", "F21"):
                    t = int(step[2])
                    dve.wait_ge(psum_ready[r].sem, psum_ready[r].after(m, step, n))
                    if t == 0:
                        dve.wait_ge(gate_loaded[r].sem, gate_loaded[r].after(m, gate_step[r], n))
                        x_new_ready[r].wait_before(dve, m, n)
                    nc.vector.tensor_tensor(gated[r][:, t, :], slot[here][:, 0:D], gate_now[r][:, 0, :], ALU.mult)\
                        .then_inc(gated_ready[r].sem, 1)

            walk(dve, program, handler, {"pre": pre})

        @block.scalar
        def _(act):
            def pre(m):
                if m == 0:
                    act.wait_ge(cond_loaded, 16)
                    nc.scalar.activation(cond_e[:, :], cond[:, :], ACT.Exp, scale=-1.0).then_inc(silu_exp, 1)

            def handler(r, m, step, n, looping, here):
                if here is not None:
                    ps = slot[here]
                if step == "LN":
                    act.wait_ge(psum_ready[r].sem, psum_ready[r].after(m, step, n))
                    plain = FULL[m] and r == "G"
                    if not plain:
                        act.wait_ge(mod_ready[r].sem, mod_ready[r].after(m, "ld", n))
                    elif m == 2 and not looping:
                        act.wait_ge(cols_ready, m + 1)
                    at = 4 if r == "E" else 0
                    for c in range(KC):
                        if not plain:
                            bias, scale = mod_now[r][:, at + 2 + c:at + 3 + c], mod_now[r][:, at + c:at + c + 1]
                        elif m == 2:
                            bias, scale = col(m, "beta", c), col(m, "gamma", c)
                        else:
                            bias, scale = 0.0, 1.0
                        last = nc.scalar.activation(x_t[r][:, c, :], ps[:, c * NT:(c + 1) * NT], ACT.Identity,
                                                    bias=bias, scale=scale)
                    last.then_inc(x_t_ready[r].sem, 1)
                elif step == "C":
                    act.wait_ge(psum_ready[r].sem, psum_ready[r].after(m, step, n))
                    if FULL[m]:
                        nc.scalar.activation(context_t[r][:, :, :],
                                             ps[:, 0:KC * S].rearrange("p (c s) -> p c s", c=KC), ACT.Identity)\
                            .then_inc(context_t_ready[r].sem, 1)
                    else:
                        act.wait_ge(mod_ready[r].sem, mod_ready[r].after(m, "ld", n))
                        for c in range(KC):
                            last = nc.scalar.activation(context_t[r][:, c, :], ps[:, c * S:(c + 1) * S],
                                                        ACT.Identity, bias=mod_now[r][:, 6 + c:7 + c],
                                                        scale=mod_now[r][:, 4 + c:5 + c])
                        last.then_inc(context_t_ready[r].sem, 1)
                elif step in ("QK", "Q", "KV"):
                    act.wait_ge(psum_ready[r].sem, psum_ready[r].after(m, step, n))
                    if not looping:
                        act.wait_ge(cols_ready, m + 1)
                    if step in ("QK", "Q"):
                        q_stored[0][r].wait_before(act, m, n)
                    if step in ("QK", "KV"):
                        k_stored[0][r].wait_before(act, m, n)
                    for src, bias, tile, c in parts_of(r, m, step, here):
                        last = nc.scalar.activation(tile[:, 0, c, :].bitcast(F32R), src, ACT.Identity, bias=bias)
                    last.then_inc(hi_ready[r].sem, 1)
                elif step in ("M0", "M1"):
                    act.wait_ge(psum_ready[r].sem, psum_ready[r].after(m, step, n))
                    nc.scalar.activation(max_t[r][int(step[1])][:, :], ps[0:H, 0:NT], ACT.Identity)\
                        .then_inc(max_t_ready[r].sem, 1)
                elif step[0] == "T":
                    v = int(step[1:])
                    keys = P if is_self(m, r) else S
                    act.wait_ge(psum_ready[r].sem, psum_ready[r].after(m, step, n))
                    if r == "G" and m == 0 and not looping:
                        act.wait_ge(gate_stored, 16 * sum(FULL))
                    nc.scalar.activation(probs[r][v % 2][0:keys, :, :],
                                         ps[0:keys, :].rearrange("p (g q) -> p g q", g=QUAD), ACT.Exp, scale=SCALE)\
                        .then_inc(probs_ready[r].sem, 1)
                elif step in out_banks(m, r):
                    act.wait_ge(psum_ready[r].sem, psum_ready[r].after(m, step, n))
                    i = out_banks(m, r).index(step)
                    nc.scalar.activation(o_raw[r][:, 2 * i:2 * i + 2, :],
                                         o_acc[r][:, :].rearrange("p (i q) -> p i q", i=2), ACT.Identity)\
                        .then_inc(o_raw_ready[r].sem, 1)
                elif step == "O2":
                    act.wait_ge(psum_ready[r].sem, psum_ready[r].after(m, step, n))
                    nc.scalar.activation(o_t[r][:, :, :], ps[:, 0:KC * NT].rearrange("p (k q) -> p k q", k=KC),
                                         ACT.Identity).then_inc(o_t_ready[r].sem, 1)
                elif step in ("H0", "H1"):
                    act.wait_ge(psum_ready[r].sem, psum_ready[r].after(m, step, n))
                    for i in range(4):
                        c = 4 * int(step[1]) + i
                        last = nc.scalar.activation(h_t[:, c, :], ps[:, i * NT:(i + 1) * NT], ACT.Gelu_apprx_tanh,
                                                    bias=col(m, "fc1", c))
                    last.then_inc(h_ready[r].sem, 1)

            walk(act, program, handler, {"pre": pre})

        @block.tensor
        def _(pe):
            mm = nc.tensor.matmul

            def transpose(dst, src, rows_in):
                return nc.tensor.transpose(dst, src, ident[0:rows_in, 0:rows_in])

            def release(r, m, step, n=None, before=False):
                if step == "LN":
                    s = x_t_ready
                elif step == "C":
                    s = context_t_ready
                elif step in ("QK", "Q"):
                    s = lo_ready
                elif step in ("V", "KV"):
                    s = v_ready
                elif step[0] == "S":
                    s = row_max_ready
                elif step[0] == "M":
                    s = max_t_ready
                elif step[0] == "T":
                    s = probs_ready
                elif step == "O1":
                    s = o_norm_ready
                elif step == "O2":
                    s = o_t_ready
                elif step[0] == "H":
                    s = h_ready
                elif step[:2] == "F2" or (step == "PR" and is_self(m, r)):
                    s = gated_ready
                else:
                    s = x_cross_ready if FULL[m] else x_new_ready
                if before:
                    s[r].wait_before(pe, m, n)
                else:
                    pe.wait_ge(s[r].sem, s[r].after(m, step, n))

            last_user = {}

            def pre(m):
                if m == 0:
                    pe.wait_ge(ident_ready, 1)
                    pe.wait_ge(silu_step, 3)
                    for k in range(KC):
                        last = transpose(pre_bank[:, k * nb:(k + 1) * nb], cond[0:nb, k * P:(k + 1) * P], nb)
                    last.then_inc(silu_psum, 1)
                    pe.wait_ge(silu_step, 4)
                elif FULL[m - 1]:
                    pe.wait_ge(gate_ready, FULL_BEFORE[m])
                else:
                    pe.wait_ge(mods_ready, m)
                pe.wait_ge(rows_loaded, rows_done(m))
                transpose(pre_bank[:, 0:n_rows(m)], rows[0:n_rows(m), :], n_rows(m)).then_inc(pre_psum, 1)
                pe.wait_ge(ada_loaded, ada_done(m))
                pe.wait_ge(cols_ready, m + 1)
                for j, src in enumerate(mod_sources(m)):
                    for k in range(KC):
                        last = mm(pre_bank[:, 64 + nb * j:64 + nb * (j + 1)], w_ada[:, k, src:src + P],
                                  silu_t[:, k, :], start=k == 0, stop=k == KC - 1)
                last.then_inc(pre_psum, 1)
                if FULL[m]:
                    pe.wait_ge(mods_ready, m + 1)
                    for g, at in enumerate((2 * D, 5 * D)):
                        for k in range(KC):
                            last = mm(pre_bank[0:nb, g * D:(g + 1) * D], silu_t[:, k, :],
                                      w_ada[:, k, at:at + D], start=k == 0, stop=k == KC - 1)
                    last.then_inc(pre_psum, 1)

            def weights_wait(r, m, step, looping):
                if looping:
                    return
                if r == "F" or not FULL[m]:
                    pe.wait_ge(wf_loaded, wf_done(m))
                else:
                    sem, dmas = (we_loaded, 3) if r == "E" or step == "PR" else (wg_loaded, 2)
                    pe.wait_ge(sem, 16 * dmas * (FULL_BEFORE[m] + 1))

            def handler(r, m, step, n, looping, here):
                if step in OFF_PE:
                    return
                if here is not None:
                    user = last_user.get(here)
                    if user == "last iteration":
                        ur, um, ustep, udn = loop_last[here]
                        release(ur, um, ustep, n - loop_dn[(r, m, step)] + udn, before=True)
                    elif user:
                        release(*user)
                    last_user[here] = (r, m, step, n)
                    ps = slot[here]
                if step == "LN":
                    pe.wait_ge(x_hat_ready[r].sem, x_hat_ready[r].after(m, "N", n))
                    for k in range(KC):
                        for t in range(TT):
                            last = transpose(ps[:, k * NT + t * P:k * NT + (t + 1) * P],
                                             hat_of(r, m)[:, t, k * P:(k + 1) * P], P)
                elif step == "C":
                    if CTX_LN[m]:
                        pe.wait_ge(x_hat_ready[r].sem, x_hat_ready[r].after(m, "NC", n))
                    else:
                        pe.wait_ge(context_loaded[r].sem, context_loaded[r].after(m, "ld", n))
                    src = (context_hat if CTX_LN[m] else context)[r]
                    for k in range(KC):
                        last = transpose(ps[:, k * S:(k + 1) * S], src[0:S, k * P:(k + 1) * P], S)
                elif step in ("QK", "Q"):
                    weights_wait(r, m, step, looping)
                    pe.wait_ge(x_t_ready[r].sem, x_t_ready[r].after(m, "LN", n))
                    weight = w_q2 if FULL[m] and r == "G" else w_qkv
                    for c in range(4 if step == "QK" else 2):
                        for k in range(KC):
                            last = mm(ps[:, c * NT:(c + 1) * NT], weight[:, k, c * P:(c + 1) * P], x_t[r][:, k, :],
                                      start=k == 0, stop=k == KC - 1)
                elif step == "V":
                    for t in range(TT):
                        for k in range(KC):
                            last = mm(ps[:, t * D:(t + 1) * D], x_t[r][:, k, t * P:(t + 1) * P],
                                      w_qkv[:, k, 2 * D:3 * D], start=k == 0, stop=k == KC - 1)
                elif step == "KV":
                    weights_wait(r, m, step, looping)
                    pe.wait_ge(context_t_ready[r].sem, context_t_ready[r].after(m, "C", n))
                    weight, at = (w_kv2, 0) if FULL[m] else (w_qkv, D)
                    for c in range(KC):
                        for k in range(KC):
                            mm(ps[:, c * S:(c + 1) * S], weight[:, k, at + c * P:at + (c + 1) * P],
                               context_t[r][:, k, :], start=k == 0, stop=k == KC - 1)
                    for k in range(KC):
                        last = mm(ps[0:S, BANK:BANK + D], context_t[r][:, k, :], weight[:, k, at + D:at + 2 * D],
                                  start=k == 0, stop=k == KC - 1)
                elif step[0] == "S":
                    u = int(step[1:])
                    t = u % 2
                    if step == "S0":
                        qk = ("QK", "QK") if is_self(m, r) else ("Q", "KV")
                        pe.wait_ge(q_stack_loaded[r].sem, q_stack_loaded[r].after(m, qk[0], n))
                        pe.wait_ge(k_stack_loaded[r].sem, k_stack_loaded[r].after(m, qk[1], n))
                        if not looping:
                            pe.wait_ge(const_ready, CONSTS[r])
                    heads, width = (QUAD, NT) if is_self(m, r) else (2 * QUAD, S)
                    for i in range(heads):
                        j = heads * (u // 2) + i
                        at = i * width if is_self(m, r) else i // QUAD * BANK + i % QUAD * S
                        last = mm(ps[:, at:at + width], q_stack[r][0:MAX_ROW, j, t * P:(t + 1) * P].bitcast(F32R),
                                  k_stack[r][0:MAX_ROW, j * width:(j + 1) * width].bitcast(F32R),
                                  start=True, stop=True)
                elif step[0] == "M":
                    h = int(step[1:])
                    pe.wait_ge(max_parts_ready[r].sem, max_parts_ready[r].after(m, step, n))
                    for t in range(TT):
                        last = transpose(ps[0:H, t * P:(t + 1) * P],
                                         max_parts[r][:, t, h, :, :].rearrange("p e h -> p (e h)"), P)
                elif step[0] == "T":
                    v = int(step[1:])
                    quad, c, keys, width = (v // 2, v % 2, P, NT) if is_self(m, r) else (v, 0, S, S)
                    half = quad // 2
                    if quad % 2 == 0 and c == 0:
                        sem = max_row_loaded[half][r]
                        pe.wait_ge(sem.sem, sem.after(m, f"M{half}", n))
                    for g in range(QUAD):
                        j = QUAD * quad + g
                        last = mm(ps[0:keys, g * NT:(g + 1) * NT],
                                  k_stack[r][0:STACK_ROWS, j * width + c * P:j * width + c * P + keys].bitcast(F32R),
                                  q_stack[r][0:STACK_ROWS, j, :].bitcast(F32R), start=True, stop=True)
                elif step[:2] == "PV":
                    v = int(step[2:])
                    quad, c, keys = (v // 2, v % 2, P) if is_self(m, r) else (v, 0, S)
                    ends = out_banks(m, r)
                    if v == 0:
                        o_raw_ready[r].wait_before(pe, m, n)
                        if r == "G" and m == 0 and not looping:
                            pe.wait_ge(gate_ready, sum(FULL))
                        kv = "V" if is_self(m, r) else "KV"
                        pe.wait_ge(v_ready[r].sem, v_ready[r].after(m, kv, n))
                    elif quad == 2 and c == 0:
                        pe.wait_ge(o_raw_ready[r].sem, o_raw_ready[r].after(m, ends[0], n))
                    pe.wait_ge(probs_ready[r].sem, probs_ready[r].after(m, f"T{v}", n))
                    for g in range(QUAD):
                        head = head_of(QUAD * quad + g)
                        v_head = v_self[:, c, head, :] if is_self(m, r) else v_ctx[r][0:S, head, :]
                        at = quad % 2 * NT
                        last = mm(o_acc[r][g * 2 * HD:(g + 1) * 2 * HD, at:at + NT], v_head,
                                  probs[r][v % 2][0:keys, g, :], start=c == 0, stop=c == 1 or not is_self(m, r))
                elif step == "O1":
                    pe.wait_ge(o_raw_ready[r].sem, o_raw_ready[r].after(m, out_banks(m, r)[1], n))
                    for t in range(TT):
                        for quad in range(H // QUAD):
                            last = transpose(ps[:, t * BANK + quad * P:t * BANK + (quad + 1) * P],
                                             o_raw[r][:, quad, t * P:(t + 1) * P], P)
                elif step == "O2":
                    pe.wait_ge(o_norm_ready[r].sem, o_norm_ready[r].after(m, "O1", n))
                    for k in range(KC):
                        for t in range(TT):
                            last = transpose(ps[:, k * NT + t * P:k * NT + (t + 1) * P],
                                             o_norm[r][:, t, k * P:(k + 1) * P], P)
                elif step == "PR":
                    pe.wait_ge(o_t_ready[r].sem, o_t_ready[r].after(m, "O2", n))
                    weights_wait(r, m, step, looping)
                    weight = w_cp if FULL[m] and r == "G" else w_proj[m % 2]
                    for t in range(TT):
                        for k in range(KC):
                            last = mm(ps[:, t * D:(t + 1) * D], o_t[r][:, k, t * P:(t + 1) * P], weight[:, k, :],
                                      start=k == 0, stop=k == KC - 1)
                elif step[0] == "H":
                    pe.wait_ge(x_t_ready[r].sem, x_t_ready[r].after(m, "LN", n))
                    weights_wait(r, m, step, looping)
                    for i in range(4):
                        c = 4 * int(step[1:]) + i
                        for k in range(KC):
                            last = mm(ps[:, i * NT:(i + 1) * NT], w_fc1[:, k, c * P:(c + 1) * P], x_t[r][:, k, :],
                                      start=k == 0, stop=k == KC - 1)
                elif step in ("F20", "F21"):
                    t = int(step[2])
                    pe.wait_ge(h_ready[r].sem, h_ready[r].after(m, "H1", n))
                    for k in range(MC):
                        last = mm(ps[:, 0:D], h_t[:, k, t * P:(t + 1) * P], w_fc2[:, k, :],
                                  start=k == 0, stop=k == MC - 1)
                last.then_inc(psum_ready[r].sem, 1)

            loop_last, loop_dn = {}, {}
            for seg in program:
                if seg[0] == "loop" and seg[1] > 0:
                    for s in sorted(last_user):
                        release(*last_user[s])
                    place = places(seg[2])
                    loop_last.clear()
                    loop_dn.clear()
                    for r, m, step, dn in seg[2]:
                        if (r, m, step) in place:
                            loop_last[place[(r, m, step)]] = (r, m, step, dn)
                            loop_dn[(r, m, step)] = dn
                    for s in range(SLOTS):
                        last_user[s] = "last iteration"
                    walk(pe, [seg], handler)
                    for s in range(SLOTS):
                        r, m, step, dn = loop_last[s]
                        last_user[s] = (r, m, step, seg[1] - 1 + dn)
                else:
                    walk(pe, [seg], handler, {"pre": pre})

    return nc


_OUTS = [((16, 256, 256), 'float32')]


def kernel(**inputs):
    import numpy as _np
    import concourse.bacc as _bacc
    from concourse import mybir as _mybir
    from concourse.bass_utils import run_bass_kernel_spmd as _run

    nc = _bacc.Bacc("TRN2", target_bir_lowering=False, num_devices=1)
    arrays, aps = {}, {}
    for name, value in inputs.items():
        a = _np.ascontiguousarray(value)
        arrays[f"in_{name}_dram"] = a
        aps[name] = nc.dram_tensor(f"in_{name}_dram", a.shape, _mybir.dt.from_np(a.dtype), kind="ExternalInput").ap()
    out = nc.dram_tensor("out_0_dram", _OUTS[0][0], _mybir.dt.from_np(_np.dtype(_OUTS[0][1])),
                         kind="ExternalOutput").ap()
    build_program(nc, aps, out)
    r = _run(nc, [arrays], core_ids=[0])
    return r.results[0]["out_0_dram"]
```
